# Optimizing a Trainium2 kernel written in Bass

```python
import numpy as np
import jax
import jax.numpy as jnp

def _softmax(x, axis=-1):
    return jax.nn.softmax(x, axis=axis)

def _gelu(x):
    return jax.nn.gelu(x, approximate=True)

def _silu(x):
    return jax.nn.silu(x)

def _sigmoid(x):
    return jax.nn.sigmoid(x)

def _layernorm(x, axis=-1, eps=1e-05):
    m = jnp.mean(x, axis=axis, keepdims=True)
    v = jnp.var(x, axis=axis, keepdims=True)
    return (x - m) / jnp.sqrt(v + eps)

def _scatter_add(tgt, idx, src, axis=0):
    return tgt.at[idx].add(src)

def _segment_sum(src, seg, n):
    return jax.ops.segment_sum(src, seg, n)
kernel_name = 'mk_adj_ffn_d2_adj_r2_478934'

def setup_inputs(seed: int=0):
    np.random.seed(seed)
    _w = jnp.asarray

    def _rec_inputs():
        import jax
        import jax.numpy as jnp
        _gk = jax.random.key(seed)
        x = -0.0002928 + 1 * jax.random.normal(jax.random.fold_in(_gk, 1), (8, 1024, 128), jnp.float32)
        _a = jax.random.bernoulli(jax.random.fold_in(_gk, 2), 0.0078125, (8, 1024, 1024))
        _a = jnp.logical_or(_a, jnp.swapaxes(_a, -1, -2))
        _a = jnp.logical_or(_a, jnp.eye(1024, dtype=bool))
        adj = _a.astype(jnp.int32)
        return (x, adj)
    x, adj = _rec_inputs()

    def _L0_gnn_setup():
        import jax, jax.numpy as jnp
        import numpy as np
        ALPHA = 0.2
        NEG_BIG = -9000000000000000.0
        key = jax.random.key(seed)
        k1, k2, k3, k4 = jax.random.split(key, 4)
        bs, N, Fin, Fout = (4, 2048, 128, 128)
        inp = jax.random.normal(k1, (bs, N, Fin), dtype=jnp.float32)
        adj = jax.random.randint(k2, (bs, N, N), 0, 2, dtype=jnp.int32)
        W = jax.random.normal(k3, (Fin, Fout), dtype=jnp.float32) * (1.414 / np.sqrt(Fin))
        a = jax.random.normal(k4, (2 * Fout, 1), dtype=jnp.float32) * 0.1
        return {'input': inp, 'adj': adj, 'W': W, 'a': a}
    _L0_gnn_all = _L0_gnn_setup()
    _L0_gnn_in = {k: v for k, v in _L0_gnn_all.items() if k in ('W', 'a')}
    del _L0_gnn_all

    def _L0_ffn_setup():
        import jax, jax.numpy as jnp
        import numpy as np
        E = 8
        K = 2
        D = 128
        H = 256
        DOUT = 128
        EPS = 1e-05
        key = jax.random.key(seed)
        ks = jax.random.split(key, 9)
        s = 0.02
        return {'x': jax.random.normal(ks[0], (4, 4096, D), jnp.float32), 'gamma': 1.0 + 0.05 * jax.random.normal(ks[1], (D,), jnp.float32), 'beta': 0.05 * jax.random.normal(ks[2], (D,), jnp.float32), 'Wr': 0.01 * jax.random.normal(ks[3], (D, E), jnp.float32), 'br': jnp.zeros((E,), jnp.float32), 'W1': s * jax.random.normal(ks[4], (E, D, H), jnp.float32), 'b1': s * jax.random.normal(ks[5], (E, H), jnp.float32), 'W2': s * jax.random.normal(ks[6], (E, H, DOUT), jnp.float32), 'b2': s * jax.random.normal(ks[7], (E, DOUT), jnp.float32)}
    _L0_ffn_all = _L0_ffn_setup()
    _L0_ffn_in = {k: v for k, v in _L0_ffn_all.items() if k in ('gamma', 'beta', 'Wr', 'br', 'W1', 'b1', 'W2', 'b2')}
    del _L0_ffn_all

    def _L1_gnn_setup():
        import jax, jax.numpy as jnp
        import numpy as np
        NEG_INF = -9000000000000000.0
        LEAKY_SLOPE = 0.2
        key = jax.random.key(seed)
        k1, k2, k3, k4, k5, k6 = jax.random.split(key, 6)
        B, N, D = (256, 200, 128)
        hidden = jax.random.normal(k1, (B, N, D), dtype=jnp.float32)
        adj = jax.random.randint(k2, (B, N, N), 0, 5, dtype=jnp.int32)
        a0 = jax.random.normal(k3, (D,), dtype=jnp.float32)
        a1 = jax.random.normal(k4, (D,), dtype=jnp.float32)
        a2 = jax.random.normal(k5, (D,), dtype=jnp.float32)
        a3 = jax.random.normal(k6, (D,), dtype=jnp.float32)
        return {'hidden': hidden, 'adj': adj, 'a0': a0, 'a1': a1, 'a2': a2, 'a3': a3}
    _L1_gnn_all = _L1_gnn_setup()
    _L1_gnn_in = {k: v for k, v in _L1_gnn_all.items() if k in ('a0', 'a1', 'a2', 'a3')}
    del _L1_gnn_all

    def _L1_ffn_setup():
        import jax, jax.numpy as jnp
        import numpy as np
        BN_EPS = 0.001

        def _bn(h, g, b, m, v):
            return g * (h - m) * jax.lax.rsqrt(v + BN_EPS) + b
        key = jax.random.key(seed)
        ks = jax.random.split(key, 8)
        B, F, Df = (128, 64, 128)
        E, H, D = (8, 128, 128)
        s1 = 1.0 / np.sqrt(Df)
        s2 = 1.0 / np.sqrt(H)
        return {'x': jax.random.normal(ks[0], (B, F, Df), jnp.float32), 'Wr': jax.random.normal(ks[1], (Df, E), jnp.float32) * s1, 'br': jnp.zeros((E,), jnp.float32), 'W1': jax.random.normal(ks[2], (E, Df, H), jnp.float32) * s1, 'b1': jnp.zeros((E, H), jnp.float32), 'g1': jnp.ones((E, H), jnp.float32), 'be1': jnp.zeros((E, H), jnp.float32), 'm1': jnp.zeros((E, H), jnp.float32), 'v1': jnp.ones((E, H), jnp.float32), 'W2': jax.random.normal(ks[3], (E, H, H), jnp.float32) * s2, 'b2': jnp.zeros((E, H), jnp.float32), 'g2': jnp.ones((E, H), jnp.float32), 'be2': jnp.zeros((E, H), jnp.float32), 'm2': jnp.zeros((E, H), jnp.float32), 'v2': jnp.ones((E, H), jnp.float32), 'Wo': jax.random.normal(ks[4], (E, H, D), jnp.float32) * s2, 'bo': jnp.zeros((E, D), jnp.float32)}
    _L1_ffn_all = _L1_ffn_setup()
    _L1_ffn_in = {k: v for k, v in _L1_ffn_all.items() if k in ('Wr', 'br', 'W1', 'b1', 'g1', 'be1', 'm1', 'v1', 'W2', 'b2', 'g2', 'be2', 'm2', 'v2', 'Wo', 'bo')}
    del _L1_ffn_all
    return {'x': x, 'adj': adj, 'L0_gnn_W': _L0_gnn_in['W'], 'L0_gnn_a': _L0_gnn_in['a'], 'L0_ffn_gamma': _L0_ffn_in['gamma'], 'L0_ffn_beta': _L0_ffn_in['beta'], 'L0_ffn_Wr': _L0_ffn_in['Wr'], 'L0_ffn_br': _L0_ffn_in['br'], 'L0_ffn_W1': _L0_ffn_in['W1'], 'L0_ffn_b1': _L0_ffn_in['b1'], 'L0_ffn_W2': _L0_ffn_in['W2'], 'L0_ffn_b2': _L0_ffn_in['b2'], 'L1_gnn_a0': _L1_gnn_in['a0'], 'L1_gnn_a1': _L1_gnn_in['a1'], 'L1_gnn_a2': _L1_gnn_in['a2'], 'L1_gnn_a3': _L1_gnn_in['a3'], 'L1_ffn_Wr': _L1_ffn_in['Wr'], 'L1_ffn_br': _L1_ffn_in['br'], 'L1_ffn_W1': _L1_ffn_in['W1'], 'L1_ffn_b1': _L1_ffn_in['b1'], 'L1_ffn_g1': _L1_ffn_in['g1'], 'L1_ffn_be1': _L1_ffn_in['be1'], 'L1_ffn_m1': _L1_ffn_in['m1'], 'L1_ffn_v1': _L1_ffn_in['v1'], 'L1_ffn_W2': _L1_ffn_in['W2'], 'L1_ffn_b2': _L1_ffn_in['b2'], 'L1_ffn_g2': _L1_ffn_in['g2'], 'L1_ffn_be2': _L1_ffn_in['be2'], 'L1_ffn_m2': _L1_ffn_in['m2'], 'L1_ffn_v2': _L1_ffn_in['v2'], 'L1_ffn_Wo': _L1_ffn_in['Wo'], 'L1_ffn_bo': _L1_ffn_in['bo']}

def reference(x, adj, L0_gnn_W, L0_gnn_a, L0_ffn_gamma, L0_ffn_beta, L0_ffn_Wr, L0_ffn_br, L0_ffn_W1, L0_ffn_b1, L0_ffn_W2, L0_ffn_b2, L1_gnn_a0, L1_gnn_a1, L1_gnn_a2, L1_gnn_a3, L1_ffn_Wr, L1_ffn_br, L1_ffn_W1, L1_ffn_b1, L1_ffn_g1, L1_ffn_be1, L1_ffn_m1, L1_ffn_v1, L1_ffn_W2, L1_ffn_b2, L1_ffn_g2, L1_ffn_be2, L1_ffn_m2, L1_ffn_v2, L1_ffn_Wo, L1_ffn_bo):
    import jax
    import jax.numpy as jnp

    def _L0_gnn_ref(input, adj, W, a):
        import jax, jax.numpy as jnp
        import numpy as np
        ALPHA = 0.2
        NEG_BIG = -9000000000000000.0
        h = jnp.matmul(input, W)
        Fout = W.shape[1]
        a1 = a[:Fout, 0]
        a2 = a[Fout:, 0]
        f1 = jnp.einsum('bnf,f->bn', h, a1)
        f2 = jnp.einsum('bnf,f->bn', h, a2)
        e = jax.nn.leaky_relu(f1[:, :, None] + f2[:, None, :], negative_slope=ALPHA)
        logits = jnp.where(adj > 0, e, NEG_BIG)
        attention = jax.nn.softmax(logits, axis=1)
        h_prime = jnp.matmul(attention, h)
        return jax.nn.elu(h_prime)

    def _L0_ffn_ref(x, gamma, beta, Wr, br, W1, b1, W2, b2):
        import jax, jax.numpy as jnp
        import numpy as np
        E = 8
        K = 2
        D = 128
        H = 256
        DOUT = 128
        EPS = 1e-05
        mu = jnp.mean(x, axis=-1, keepdims=True)
        var = jnp.mean(jnp.square(x - mu), axis=-1, keepdims=True)
        xn = (x - mu) * jax.lax.rsqrt(var + EPS) * gamma + beta
        logits = jnp.einsum('bsd,de->bse', xn, Wr) + br
        top_vals, top_idx = jax.lax.top_k(logits, K)
        w = jax.nn.softmax(top_vals, axis=-1)
        w_full = jnp.einsum('bsk,bske->bse', w, jax.nn.one_hot(top_idx, E, dtype=w.dtype))
        y = jnp.zeros(x.shape[:-1] + (DOUT,), x.dtype)
        for e in range(E):
            h = jax.nn.gelu(jnp.einsum('bsd,dh->bsh', xn, W1[e]) + b1[e], approximate=False)
            y_e = jnp.einsum('bsh,hd->bsd', h, W2[e]) + b2[e]
            y = y + y_e * w_full[..., e, None]
        return y

    def _L1_gnn_ref(hidden, adj, a0, a1, a2, a3):
        import jax, jax.numpy as jnp
        import numpy as np
        NEG_INF = -9000000000000000.0
        LEAKY_SLOPE = 0.2

        def edge_score(a):
            s = jnp.einsum('bid,bjd->bij', hidden * a, hidden)
            return jax.nn.leaky_relu(s, LEAKY_SLOPE)
        e0, e1, e2, e3 = (edge_score(a0), edge_score(a1), edge_score(a2), edge_score(a3))
        alpha = jnp.where(adj == 1, e0, NEG_INF)
        alpha = jnp.where(adj == 2, e1, alpha)
        alpha = jnp.where(adj == 3, e2, alpha)
        alpha = jnp.where(adj == 4, e3, alpha)
        alpha = jax.nn.softmax(alpha, axis=-1)
        return jnp.matmul(alpha, hidden)

    def _L1_ffn_ref(x, Wr, br, W1, b1, g1, be1, m1, v1, W2, b2, g2, be2, m2, v2, Wo, bo):
        import jax, jax.numpy as jnp
        import numpy as np
        BN_EPS = 0.001

        def _bn(h, g, b, m, v):
            return g * (h - m) * jax.lax.rsqrt(v + BN_EPS) + b
        feat = jnp.mean(x, axis=0)
        w = jax.nn.softmax(feat @ Wr + br, axis=-1)
        h = jnp.einsum('bfd,edh->bfeh', x, W1) + b1
        h = jax.nn.relu(_bn(h, g1, be1, m1, v1))
        h = jnp.einsum('bfeh,ehk->bfek', h, W2) + b2
        h = jax.nn.relu(_bn(h, g2, be2, m2, v2))
        y = jnp.einsum('bfeh,ehd->bfed', h, Wo) + bo
        return jnp.einsum('bfed,fe->bfd', y, w)
    x = x + _L0_gnn_ref(_layernorm(x, axis=-1), adj, L0_gnn_W, L0_gnn_a)
    x = x + _L0_ffn_ref(_layernorm(x, axis=-1), L0_ffn_gamma, L0_ffn_beta, L0_ffn_Wr, L0_ffn_br, L0_ffn_W1, L0_ffn_b1, L0_ffn_W2, L0_ffn_b2)
    x = x + _L1_gnn_ref(_layernorm(x, axis=-1), adj, L1_gnn_a0, L1_gnn_a1, L1_gnn_a2, L1_gnn_a3)
    x = x + _L1_ffn_ref(_layernorm(x, axis=-1), L1_ffn_Wr, L1_ffn_br, L1_ffn_W1, L1_ffn_b1, L1_ffn_g1, L1_ffn_be1, L1_ffn_m1, L1_ffn_v1, L1_ffn_W2, L1_ffn_b2, L1_ffn_g2, L1_ffn_be2, L1_ffn_m2, L1_ffn_v2, L1_ffn_Wo, L1_ffn_bo)
    return x

_drawn_inputs = setup_inputs


def setup_inputs(seed=0):
    import zlib

    import numpy as np

    out = dict(_drawn_inputs(seed))
    spreads = {'L0_ffn_br': (0.0, 0.1),
     'L1_ffn_br': (0.0, 0.8),
     'L1_ffn_b1': (0.0, 0.675),
     'L1_ffn_g1': (1.0, 0.6),
     'L1_ffn_be1': (0.0, 0.731),
     'L1_ffn_m1': (0.0, 0.676),
     'L1_ffn_v1': (1.0, 0.6),
     'L1_ffn_b2': (0.0, 0.484),
     'L1_ffn_g2': (1.0, 0.6),
     'L1_ffn_be2': (0.0, 0.528),
     'L1_ffn_m2': (0.0, 0.503),
     'L1_ffn_v2': (1.0, 0.6),
     'L1_ffn_bo': (0.0, 0.356)}
    factors = {'L0_ffn_gamma': 6.413, 'L0_ffn_beta': 6.795, 'L0_ffn_b1': 8.0}
    for name, (base, spread) in spreads.items():
        noise = np.random.default_rng([zlib.crc32(name.encode()), seed]).standard_normal(out[name].shape)
        drawn = base * np.exp(spread * noise) if base else spread * noise
        out[name] = jnp.asarray(drawn.astype(out[name].dtype))
    for name, factor in factors.items():
        out[name] = (out[name] * factor).astype(out[name].dtype)
    return out
```

```python
from contextlib import ExitStack

import concourse.bass as bass
from concourse import mybir

F32 = mybir.dt.float32
BF16 = mybir.dt.bfloat16
I32 = mybir.dt.int32
ALU = mybir.AluOpType
ACT = mybir.ActivationFunctionType
AX_X = mybir.AxisListType.X

P = 128
HALF = 512
SLOPE = 0.2
BLOCKED = -float(2 ** 55)
EPS = 1e-5
BN_EPS = 1e-3


class Count:

    def __init__(self):
        self.base, self.n = 0, 0

    def next(self):
        self.n += 1
        return self.base + self.n

    def now(self):
        return self.base + self.n

    def loop(self, turn, per):
        self.start, self.per = self.base + self.n, per
        self.base, self.n = self.start + turn * per, 0

    def end(self, turns):
        assert self.n == self.per, (self.n, self.per)
        self.base, self.n = self.start + turns * self.per, 0


def wait(eng, sem, value):
    if not isinstance(value, int) or value > 0:
        eng.wait_ge(sem, value)


def program(nc, x, adj, p, out):
    B, N, D = x.shape
    NT = N // P
    E = p["L0_ffn_W1"].shape[0]
    HID = p["L0_ffn_W1"].shape[2]
    HC = HID // P
    assert D == P and N == 2 * HALF

    with ExitStack() as whole:
        sems = []

        def sem(name):
            sems.append(name)
            return whole.enter_context(nc.semaphore(name))

        def sb(name, shape, dt=F32, ctx=whole):
            return ctx.enter_context(nc.sbuf_tensor(name, shape, dt))

        X = sb("X", [P, B * N])
        ident = sb("ident", [P, P])
        identb = sb("identb", [P, P], BF16)
        blockI = sb("blockI", [P, P], BF16)
        ones3 = sb("ones3", [3, P], BF16)
        pick = sb("pick", [3 * E, E * P], BF16)
        half8 = sb("half8", [P, NT])
        eps8 = sb("eps8", [P, NT])
        order = sb("order", [P, E])
        Wg = sb("Wg", [P, P])
        WgT = sb("WgT", [P, 2])
        W1 = sb("W1", [P, E * HID])
        W2 = sb("W2", [P, E * HC * P])
        Wr0 = sb("Wr0", [P, E])
        br0 = sb("br0", [P, E])
        b20 = sb("b20", [E, P])
        V1 = sb("V1", [P, E * P])
        V2 = sb("V2", [P, E * P])
        Vo = sb("Vo", [P, E * P])
        Wr1 = sb("Wr1", [P, E])
        br1 = sb("br1", [P, E])
        bo1 = sb("bo1", [E, P])
        names = ([("L0_ffn_b1", E * HC), ("L0_ffn_gamma", 1), ("L0_ffn_beta", 1)]
                 + [(f"L1_gnn_a{k}", 1) for k in range(4)]
                 + [(f"L1_ffn_{n}", E) for n in ("b1", "g1", "be1", "m1", "v1", "b2", "g2", "be2", "m2", "v2")])
        at, R = {}, 0
        for n, rows in names:
            at[n] = R
            R += rows
        prow = sb("prow", [R, P])
        pcol = sb("pcol", [P, R])
        bn = sb("bn", [P, 4 * E])

        flag = sb("flag", [1, 1], I32)
        ones_or_more = sb("ones_or_more", [P, N])
        excess = sb("excess", [P, B * NT // 2])
        minus1 = sb("minus1", [P, 1])
        held = sem("held")
        x_first, x_second, x_rest, par_loaded = sem("x_first"), sem("x_second"), sem("x_rest"), sem("par_loaded")
        adj_loaded = [sem(f"adj_loaded{i}") for i in range(4)]

        loads = [(W1[:, :].rearrange("d (e h) -> d e h", e=E), p["L0_ffn_W1"].rearrange("e d h -> d e h")),
                 (W2[:, :].rearrange("h (e c d) -> h e c d", e=E, c=HC),
                  p["L0_ffn_W2"].rearrange("e (c h) d -> h e c d", c=HC)),
                 (Wr0[:, :], p["L0_ffn_Wr"]),
                 (br0[:, :], p["L0_ffn_br"].rearrange("(o e) -> o e", o=1).to_broadcast([P, E])),
                 (b20[:, :], p["L0_ffn_b2"]),
                 (V1[:, :].rearrange("d (e h) -> d e h", e=E), p["L1_ffn_W1"].rearrange("e d h -> d e h")),
                 (V2[:, :].rearrange("d (e h) -> d e h", e=E), p["L1_ffn_W2"].rearrange("e d h -> d e h")),
                 (Vo[:, :].rearrange("d (e h) -> d e h", e=E), p["L1_ffn_Wo"].rearrange("e d h -> d e h")),
                 (Wr1[:, :], p["L1_ffn_Wr"]),
                 (br1[:, :], p["L1_ffn_br"].rearrange("(o e) -> o e", o=1).to_broadcast([P, E])),
                 (bo1[:, :], p["L1_ffn_bo"])]
        for n, k in names:
            src = p[n]
            if n == "L0_ffn_b1":
                src = src.rearrange("e (c h) -> (e c) h", h=P)
            elif k == 1:
                src = src.rearrange("(o h) -> o h", o=1)
            loads.append((prow[at[n]:at[n] + k, :], src))

        with ExitStack() as ctx:
            A12 = sb("A12", [P, 2 * P], ctx=ctx)
            junk = sb("junk", [P, P], ctx=ctx)
            gat_loaded, cstep = sem("gat_loaded"), sem("const_step")
            block = ctx.enter_context(nc.Block())

            @block.sync
            def _(sp):
                sp.dma_start(X[:, 0:N].rearrange("p (t d) -> p t d", t=NT),
                             x[0].rearrange("(t p) d -> p t d", p=P)).then_inc(x_first, 16)
                sp.dma_start(Wg[:, :], p["L0_gnn_W"]).then_inc(gat_loaded, 16)
                sp.dma_start(A12[:, :], p["L0_gnn_a"].rearrange("k o -> o k").to_broadcast([P, 2 * P])
                             ).then_inc(gat_loaded, 16)

            @block.gpsimd
            def _(pool):
                c = Count()
                for tile, value in ((ident, 0.0), (identb, 0.0), (blockI, 0.0), (pick, 0.0), (ones3, 1.0), (half8, -0.5), (eps8, EPS), (minus1, -1.0), (ones_or_more, 0.0),
                                    *((order[:, e:e + 1], float(E - e)) for e in range(E))):
                    nc.gpsimd.memset(tile[:, :], value).then_inc(cstep, 1)
                    c.next()
                pool.wait_ge(cstep, c.now())
                for tile, fill in ((ident, 1.0), (identb, 1.0), (blockI, BLOCKED)):
                    nc.gpsimd.affine_select(out=tile[:, :], in_=tile[:, :], compare_op=ALU.not_equal, fill=fill,
                                            base=0, pattern=[[-1, P]], channel_multiplier=1).then_inc(cstep, 1)
                    c.next()
                v = pick[:, :].rearrange("r (e m) -> r e m", e=E)
                for k in range(3):
                    nc.gpsimd.affine_select(out=v, in_=v, compare_op=ALU.not_equal, fill=1.0, base=-k * E,
                                            pattern=[[-1, E], [0, P]], channel_multiplier=1).then_inc(cstep, 1)
                    pool.wait_ge(cstep, c.next())

            @block.vector
            def _(dve):
                dve.wait_ge(gat_loaded, 32)
                for k in range(2):
                    nc.vector.tensor_tensor_reduce(junk[:, :], Wg[:, :], A12[:, k * P:(k + 1) * P], 1.0, 0.0, ALU.mult,
                                                   ALU.add, WgT[:, k:k + 1]).then_inc(gat_loaded, 1)
                    dve.wait_ge(gat_loaded, 33 + k)

        def hold(eng, s, value):
            eng.wait_ge(s, value)
            eng.sem_inc(held, 1)

        def ln_stats(dve, b, ST, MV, stepsem, step, mv_ready):
            for t in range(NT):
                i = nc.vector.bn_stats(ST[:, t, :], X[:, bass.ds(b * N + t * P, P)])
            i.then_inc(stepsem, 1)
            hold(dve, stepsem, step.next())
            for t in range(NT):
                i = nc.vector.bn_aggr(MV[:, t, :], ST[:, t, :])
            i.then_inc(mv_ready, 1)

        def ln_root(pool, b, MV, RS, stepsem, step, mv_ready, rs_ready, twice):
            pool.wait_ge(mv_ready, b + 1)
            var = MV[:, :, 1]

            def op(*a):
                nc.gpsimd.tensor_tensor(*a).then_inc(stepsem, 1)
                pool.wait_ge(stepsem, step.next())
            op(RS[:, 0, :], var, eps8[:, :], ALU.add)
            if not twice:
                nc.gpsimd.tensor_tensor(RS[:, 1, :], RS[:, 0, :], half8[:, :], ALU.pow).then_inc(rs_ready, 1)
                return
            op(RS[:, 1, :], RS[:, 0, :], half8[:, :], ALU.pow)
            op(RS[:, 2, :], RS[:, 1, :], RS[:, 1, :], ALU.mult)
            op(RS[:, 3, :], RS[:, 2, :], var, ALU.mult)
            op(RS[:, 4, :], RS[:, 3, :], eps8[:, :], ALU.add)
            op(RS[:, 5, :], RS[:, 4, :], half8[:, :], ALU.pow)
            nc.gpsimd.tensor_tensor(RS[:, 6, :], RS[:, 5, :], RS[:, 1, :], ALU.mult).then_inc(rs_ready, 1)

        def ln_apply(dve, b, MV, rs, XN, xn_at, rs_ready, xn_ready):
            dve.wait_ge(rs_ready, b + 1)
            for t in range(NT):
                i = nc.vector.tensor_scalar(XN[:, bass.ds(xn_at + t * P, P)], X[:, bass.ds(b * N + t * P, P)],
                                            MV[:, t, 0:1], rs[:, t:t + 1], ALU.subtract, ALU.mult)
            i.then_inc(xn_ready, 1)

        with ExitStack() as ctx:
            def tile(name, shape, dt=F32):
                return sb(name, shape, dt, ctx)

            ADJ = tile("ADJ", [P, 4, N], I32)
            NM = tile("NM", [P, 2 * NT * N], BF16)
            ST, MV, RS = tile("ST", [P, NT, 6]), tile("MV", [P, NT, 2]), tile("RS", [P, 7, NT])
            XN, XNT = tile("XN", [P, N]), tile("XNT", [P, N])
            H = tile("H", [P, 2 * N])
            F2 = tile("F2", [P, 2 * NT])
            F3 = tile("F3", [P, NT, 3], BF16)
            FR = tile("FR", [P, NT])
            F1R = tile("F1R", [3, 2 * N], BF16)
            R4, Y, PR = tile("R4", [P, 2, N]), tile("Y", [P, 2, N]), tile("PR", [P, 2, N])
            MX, NMX, Z, RZ = tile("MX", [P, NT]), tile("NMX", [P, NT]), tile("Z", [P, NT]), tile("RZ", [P, NT])
            HS = tile("HS", [P, 2, P])
            RO, EX, EL = tile("RO", [P, N]), tile("EX", [P, N]), tile("EL", [P, N])
            T = [ctx.enter_context(nc.psum_tensor(f"T{i}", [P, N], F32)) for i in range(2)]
            O = ctx.enter_context(nc.psum_tensor("O", [P, N], F32))
            M = [ctx.enter_context(nc.psum_tensor(f"M{i}", [P, HALF], F32)) for i in range(2)]
            F1T = M[1][:, :].bitcast(BF16)

            mv_ready, rs_ready, xn_ready, dstep, pstep = (sem("a_" + n) for n in (
                "mv_ready", "rs_ready", "xn_ready", "dve_step", "pool_step"))
            xnt_ps, xnt_ready, h_ps, h_ready, elt_ps, x_added = ([sem(f"a_{n}{h}") for h in range(2)] for n in (
                "xnt_ps", "xnt_ready", "h_ps", "h_ready", "elt_ps", "x_added"))
            f12_ps, f2_ready, f1t_ps, f1r_ready, nm_ready, t_ready, r4_ready, y_ready, shift_ready, pr_ready = (
                sem("a_" + n) for n in ("f12_ps", "f2_ready", "f1t_ps", "f1r_ready", "nm_ready", "t_ready", "r4_ready",
                                        "y_ready", "shift_ready", "pr_ready"))
            CL = tile("CL", [P, 2, N])
            seen = tile("seen", [P, N], BF16)
            pool_looked, act_looked, added = sem("a_pool_looked"), sem("a_act_looked"), sem("a_added")
            hs_ready, pv_done, ro_ready, ex_ready, el_ready = (sem("a_" + n) for n in (
                "hs_ready", "pv_done", "ro_ready", "ex_ready", "el_ready"))
            LAST = B - 1
            block = ctx.enter_context(nc.Block())

            @block.sync
            def _(sp):
                def load(b):
                    for t in range(NT):
                        if not isinstance(b, int) or b * NT + t > 3:
                            hold(sp, nm_ready, b * NT + t - 3)
                        if t >= 4:
                            hold(sp, pool_looked, b * 4 + t - 3)
                        elif not isinstance(b, int) or b > 0:
                            hold(sp, act_looked, (b - 1) * 4 + t + 1)
                        sp.dma_start(ADJ[:, t % 4, :], adj[bass.ds(b, 1), t * P:(t + 1) * P, :].rearrange("o p i -> (o p) i")
                                     ).then_inc(adj_loaded[t % 4], 16)
                def load_x(b, loaded):
                    sp.dma_start(X[:, b * N:(b + 1) * N].rearrange("p (t d) -> p t d", t=NT),
                                 x[b].rearrange("(t p) d -> p t d", p=P)).then_inc(loaded, 16)

                load(0)
                load_x(1, x_second)
                load(1)
                for b in range(2, B):
                    load_x(b, x_rest)
                for dst, src in loads:
                    sp.dma_start(dst, src).then_inc(par_loaded, 16)
                with sp.Fori(2, B) as b:
                    load(b)

            @block.gpsimd
            def _(pool):
                step = Count()

                def look(b, t):
                    pool.wait_ge(adj_loaded[t], 16 * (b * (NT // 4) + 1))
                    if not isinstance(b, int) or b * 4 + t > 1:
                        hold(pool, added, b * 4 + t - 1)
                    nc.gpsimd.tensor_scalar(CL[:, t % 2, :], ADJ[:, t, :], 1048576.0, 1.0, ALU.min, ALU.max
                                            ).then_inc(pool_looked, 1)
                    pool.wait_ge(pool_looked, b * 4 + t + 1)
                    wait(pool, added, b * 4 + t)
                    nc.gpsimd.tensor_tensor(ones_or_more[:, :], ones_or_more[:, :], CL[:, t % 2, :], ALU.add
                                            ).then_inc(added, 1)

                def batch(b):
                    ln_root(pool, b, MV, RS, pstep, step, mv_ready, rs_ready, False)
                    for t in range(4):
                        look(b, t)

                batch(0)
                with pool.Fori(1, B) as b:
                    step.loop(b - 1, 1)
                    batch(b)
                step.end(B - 1)

            @block.tensor
            def _(pe):
                def turn_x(b, h):
                    pe.wait_ge(xn_ready, b + 1)
                    for t in range(4):
                        i = pe.transpose(M[h][:, t * P:(t + 1) * P], XN[:, bass.ts(4 * h + t, P)], ident[:, :])
                    i.then_inc(xnt_ps[h], 1)

                def project(b, h):
                    pe.wait_ge(xnt_ready[h], b + 1)
                    for t in range(4):
                        i = pe.matmul(M[h][:, t * P:(t + 1) * P], XNT[:, bass.ts(4 * h + t, P)], Wg[:, :], start=True, stop=True)
                    i.then_inc(h_ps[h], 1)

                def scores(b):
                    pe.wait_ge(h_ready[0], b + 1)
                    for t in range(NT):
                        i = pe.matmul(M[0][:, 2 * t:2 * t + 2], XNT[:, t * P:(t + 1) * P], WgT[:, :], start=True, stop=True)
                    i.then_inc(f12_ps, 1)

                def turn_f1(b):
                    pe.wait_ge(f2_ready, b + 1)
                    pe.wait_ge(h_ready[1], b + 1)
                    for t in range(NT):
                        i = pe.transpose(F1T[0:3, t * P:(t + 1) * P], F3[:, t, :], identb[:, :])
                    i.then_inc(f1t_ps, 1)

                def turn_el(b, h, used):
                    pe.wait_ge(el_ready, b + 1)
                    pe.wait_ge((f2_ready, f1r_ready)[h], used)
                    for t in range(4):
                        i = pe.transpose(M[h][:, t * P:(t + 1) * P], EL[:, bass.ts(4 * h + t, P)], ident[:, :])
                    i.then_inc(elt_ps[h], 1)

                def logits(b, c):
                    if c == 0:
                        hold(pe, f1r_ready, b + 1)
                        pe.wait_ge(nm_ready, b * NT + NT)
                    wait(pe, y_ready, b * NT + c - 1)
                    t = T[c % 2]
                    for h in range(2):
                        for r in range(4 * h, 4 * h + 4):
                            pe.matmul(t[:, r * P:(r + 1) * P], NM[:, bass.ds((b % 2) * NT * N + r * N + c * P, P)],
                                      blockI[:, :], start=(r % 4 == 0), stop=False)
                        i = pe.matmul(t[:, h * HALF:(h + 1) * HALF], ones3[:, :],
                                      F1R[:, bass.ds((b % 2) * N + h * HALF, HALF)], start=False, stop=True)
                    i.then_inc(t_ready, 1)

                def attend(b, c):
                    pe.wait_ge(hs_ready, b * NT + c + 1)
                    if c == 0:
                        wait(pe, ex_ready, b)
                    for h in range(2):
                        i = pe.matmul(O[:, h * HALF:(h + 1) * HALF], HS[:, c % 2, :], PR[:, c % 2, h * HALF:(h + 1) * HALF],
                                      start=(c == 0), stop=(c == NT - 1))
                    i.then_inc(pv_done, 1)

                def batch(b, first, last):
                    for c in range(NT):
                        logits(b, c)
                        if c >= 2:
                            attend(b, c - 2)
                        elif not first:
                            attend(b - 1, NT - 2 + c)
                        if not last:
                            if c in (2, 3):
                                turn_x(b + 1, c - 2)
                            if c in (4, 5):
                                project(b + 1, c - 4)
                            if c == 5:
                                scores(b + 1)
                            if c == 6:
                                turn_f1(b + 1)
                        if c == 7 and not first:
                            turn_el(b - 1, 0, b + 1 if last else b + 2)
                            turn_el(b - 1, 1, b + 1 if last else b + 2)

                for h in range(2):
                    turn_x(0, h)
                for h in range(2):
                    project(0, h)
                scores(0)
                turn_f1(0)
                batch(0, True, False)
                with pe.Fori(1, LAST) as b:
                    batch(b, False, False)
                batch(LAST, False, True)
                attend(LAST, NT - 2)
                attend(LAST, NT - 1)
                for h in range(2):
                    pe.wait_ge(x_added[h], LAST)
                    turn_el(LAST, h, B)

            @block.scalar
            def _(act):
                def copy_xnt(b, h):
                    act.wait_ge(xnt_ps[h], b + 1)
                    wait(act, f12_ps, b)
                    nc.scalar.copy(XNT[:, h * HALF:(h + 1) * HALF], M[h][:, :]).then_inc(xnt_ready[h], 1)

                def copy_h(b, h):
                    act.wait_ge(h_ps[h], b + 1)
                    wait(act, hs_ready, (b - 1) * NT)
                    nc.scalar.copy(H[:, bass.ds((b % 2) * N + h * HALF, HALF)], M[h][:, :]).then_inc(h_ready[h], 1)

                def relu(b, c):
                    act.wait_ge(t_ready, b * NT + c + 1)
                    if c == 0:
                        act.wait_ge(f2_ready, b + 1)
                    wait(act, y_ready, b * NT + c - 1)
                    nc.scalar.activation(R4[:, c % 2, :], T[c % 2][:, :], ACT.Relu, bias=F2[:, bass.ds((b % 2) * NT + c, 1)],
                                         scale=4.0).then_inc(r4_ready, 1)

                def prob(b, c):
                    act.wait_ge(shift_ready, b * NT + c + 1)
                    wait(act, pv_done, b * NT + c - 1)
                    nc.scalar.activation(PR[:, c % 2, :], Y[:, c % 2, :], ACT.Exp, bias=NMX[:, c:c + 1], scale=SLOPE,
                                         accum_out=Z[:, c:c + 1]).then_inc(pr_ready, 1)

                def look(b, t):
                    act.wait_ge(adj_loaded[t % 4], 16 * (b * (NT // 4) + 2))
                    wait(act, act_looked, b * 4 + t - 4)
                    nc.scalar.activation(seen[:, :], ADJ[:, t % 4, :], ACT.Relu, bias=minus1[:, :],
                                         accum_out=excess[:, bass.ds(b * 4 + t - 4, 1)]).then_inc(act_looked, 1)

                def outputs(b):
                    act.wait_ge(pv_done, b * NT + NT)
                    nc.scalar.activation(RO[:, :], O[:, :], ACT.Relu).then_inc(ro_ready, 1)
                    nc.scalar.activation(EX[:, :], O[:, :], ACT.Exp).then_inc(ex_ready, 1)

                def batch(b, first, last):
                    for c in range(NT):
                        relu(b, c)
                        if c > 0:
                            prob(b, c - 1)
                        elif not first:
                            prob(b - 1, NT - 1)
                        if c == 1 and not first:
                            outputs(b - 1)
                        if not last:
                            if c in (2, 3):
                                copy_xnt(b + 1, c - 2)
                            if c in (4, 5):
                                copy_h(b + 1, c - 4)
                            if c >= 4:
                                look(b + 1, c)

                for h in range(2):
                    copy_xnt(0, h)
                for h in range(2):
                    copy_h(0, h)
                for t in range(4, NT):
                    look(0, t)
                batch(0, True, False)
                with act.Fori(1, LAST) as b:
                    batch(b, False, False)
                batch(LAST, False, True)
                prob(LAST, NT - 1)
                outputs(LAST)

            @block.vector
            def _(dve):
                step = Count()

                def convert(b, t):
                    dve.wait_ge(adj_loaded[t % 4], 16 * (b * (NT // 4) + t // 4 + 1))
                    if t == 0:
                        wait(dve, t_ready, (b - 1) * NT)
                    nc.vector.tensor_scalar(NM[:, bass.ds((b % 2) * NT * N + t * N, N)], ADJ[:, t % 4, :], 0.0, None,
                                            ALU.is_le).then_inc(nm_ready, 1)

                def parts(b):
                    dve.wait_ge(f12_ps, b + 1)
                    wait(dve, f1t_ps, b)
                    v = M[0][:, 0:2 * NT].rearrange("p (t k) -> p t k", k=2)
                    nc.vector.tensor_copy(F3[:, :, 0], v[:, :, 0]).then_inc(dstep, 1)
                    dve.wait_ge(dstep, step.next())
                    nc.vector.tensor_tensor(FR[:, :], v[:, :, 0], F3[:, :, 0], ALU.subtract).then_inc(dstep, 1)
                    dve.wait_ge(dstep, step.next())
                    nc.vector.tensor_copy(F3[:, :, 1], FR[:, :]).then_inc(dstep, 1)
                    dve.wait_ge(dstep, step.next())
                    nc.vector.tensor_tensor(F3[:, :, 2], FR[:, :], F3[:, :, 1], ALU.subtract)
                    wait(dve, r4_ready, (b - 1) * NT)
                    nc.vector.tensor_scalar(F2[:, bass.ds((b % 2) * NT, NT)], v[:, :, 1], 4.0, None, ALU.mult).then_inc(f2_ready, 1)

                def copy_f1(b):
                    dve.wait_ge(f1t_ps, b + 1)
                    wait(dve, t_ready, (b - 1) * NT)
                    nc.vector.tensor_copy(F1R[:, bass.ds((b % 2) * N, N)], F1T[0:3, 0:N]).then_inc(f1r_ready, 1)

                def shift(b, c):
                    if not isinstance(b, int) or b * NT + c > 1:
                        hold(dve, pr_ready, b * NT + c - 1)
                    hold(dve, r4_ready, b * NT + c + 1)
                    nc.vector.tensor_tensor_reduce(Y[:, c % 2, :], T[c % 2][:, :], R4[:, c % 2, :], 1.0, -3.0e38, ALU.add,
                                                   ALU.max, MX[:, c:c + 1]).then_inc(y_ready, 1)
                    dve.wait_ge(y_ready, b * NT + c + 1)
                    nc.vector.tensor_scalar(NMX[:, c:c + 1], MX[:, c:c + 1], -SLOPE, None, ALU.mult).then_inc(shift_ready, 1)

                def share(b, c):
                    dve.wait_ge(pr_ready, b * NT + c + 1)
                    nc.vector.reciprocal(RZ[:, c:c + 1], Z[:, c:c + 1]).then_inc(dstep, 1)
                    dve.wait_ge(dstep, step.next())
                    if c == 0:
                        dve.wait_ge(h_ready[1], b + 1)
                    wait(dve, pv_done, b * NT + c - 1)
                    nc.vector.tensor_scalar(HS[:, c % 2, :], H[:, bass.ds((b % 2) * N + c * P, P)], RZ[:, c:c + 1], None,
                                            ALU.mult).then_inc(hs_ready, 1)

                def elu(b):
                    dve.wait_ge(ex_ready, b + 1)
                    nc.vector.scalar_tensor_tensor(out=EL[:, :], in0=EX[:, :], scalar=1.0, in1=RO[:, :], op0=ALU.min,
                                                   op1=ALU.add).then_inc(el_ready, 1)

                def add(b):
                    for h in range(2):
                        dve.wait_ge(elt_ps[h], b + 1)
                        xb = X[:, bass.ds(b * N + h * HALF, HALF)]
                        nc.vector.scalar_tensor_tensor(out=xb, in0=M[h][:, :], scalar=-1.0, in1=xb, op0=ALU.add,
                                                       op1=ALU.add).then_inc(x_added[h], 1)

                def stats(b):
                    ln_stats(dve, b, ST, MV, dstep, step, mv_ready)

                def norm(b):
                    if not isinstance(b, int) or b > 0:
                        dve.wait_ge(xnt_ps[1], b)
                    ln_apply(dve, b, MV, RS[:, 1, :], XN, 0, rs_ready, xn_ready)

                def batch(b, first, last):
                    for c in range(NT):
                        if not last and c == 6:
                            parts(b + 1)
                        if not last and c == 7:
                            copy_f1(b + 1)
                        shift(b, c)
                        if c > 0:
                            share(b, c - 1)
                        elif not first:
                            share(b - 1, NT - 1)
                        if c == 2 and not first:
                            elu(b - 1)
                        if not last:
                            convert(b + 1, c)
                            if c == 0:
                                stats(b + 1)
                            if c == 1:
                                norm(b + 1)
                    if not first:
                        add(b - 1)

                dve.wait_ge(x_first, 16)
                stats(0)
                norm(0)
                for t in range(4):
                    convert(0, t)
                parts(0)
                copy_f1(0)
                for t in range(4, NT):
                    convert(0, t)
                dve.wait_ge(x_second, 16)
                batch(0, True, False)
                dve.wait_ge(x_rest, 16 * (B - 2))
                with dve.Fori(1, LAST) as b:
                    step.loop(b - 1, 12)
                    batch(b, False, False)
                step.end(LAST - 1)
                batch(LAST, False, True)
                share(LAST, NT - 1)
                elu(LAST)
                add(LAST)

        with ExitStack() as ctx:
            var, half, diff, prod = (sb(n, [P, 2 * E], ctx=ctx) for n in ("bn_var", "bn_half", "bn_diff", "bn_prod"))
            ps = ctx.enter_context(nc.psum_tensor("ps_par", [P, HALF], F32))
            lcol, lone, most = sb("lcol", [P, 1], ctx=ctx), sb("lone", [1, 1], ctx=ctx), sb("most", [P, 2], ctx=ctx)
            lcol_ready, lrow_ps = sem("lcol_ready"), sem("lrow_ps")
            pl = ctx.enter_context(nc.psum_tensor("ps_largest", [1, HALF], F32))
            pcol_ps, var_ready, root_ready, qstep = sem("pcol_ps"), sem("var_ready"), sem("root_ready"), sem("par_step")
            block = ctx.enter_context(nc.Block())

            @block.tensor
            def _(pe):
                pe.wait_ge(par_loaded, 16 * len(loads))
                pe.transpose(ps[:, 0:R], prow[:, :], ident[0:R, 0:R]).then_inc(pcol_ps, 1)
                pe.wait_ge(lcol_ready, 1)
                pe.transpose(pl[:, 0:P], lcol[:, :], ident[:, :]).then_inc(lrow_ps, 1)

            @block.gpsimd
            def _(pool):
                nc.gpsimd.memset(half[:, :], -0.5).then_inc(root_ready, 1)
                pool.wait_ge(root_ready, 1)
                pool.wait_ge(var_ready, 2)
                nc.gpsimd.tensor_tensor(var[:, :], var[:, :], half[:, :], ALU.pow).then_inc(root_ready, 1)

            @block.vector
            def _(dve):
                c = Count()
                nc.vector.tensor_reduce(most[:, 0:1], ones_or_more[:, :], AX_X, ALU.max).then_inc(qstep, 1)
                nc.vector.tensor_reduce(most[:, 1:2], excess[:, :], AX_X, ALU.max).then_inc(qstep, 1)
                c.next()
                dve.wait_ge(qstep, c.next())
                nc.vector.scalar_tensor_tensor(out=lcol[:, :], in0=most[:, 0:1], scalar=-float(B * NT // 2), in1=most[:, 1:2],
                                               op0=ALU.add, op1=ALU.max).then_inc(lcol_ready, 1)
                dve.wait_ge(pcol_ps, 1)
                nc.vector.tensor_copy(pcol[:, :], ps[:, 0:R]).then_inc(qstep, 1)
                dve.wait_ge(qstep, c.next())

                def col(n):
                    return pcol[:, at[f"L1_ffn_{n}"]:at[f"L1_ffn_{n}"] + E]

                for k in range(2):
                    nc.vector.tensor_scalar(var[:, k * E:(k + 1) * E], col(f"v{k + 1}"), BN_EPS, None, ALU.add
                                            ).then_inc(var_ready, 1)
                dve.wait_ge(lrow_ps, 1)
                nc.vector.tensor_reduce(lone[:, :], pl[:, 0:P], AX_X, ALU.max).then_inc(qstep, 1)
                dve.wait_ge(qstep, c.next())
                nc.vector.tensor_scalar(flag[:, :], lone[:, :], 0.0, None, ALU.is_gt)
                dve.wait_ge(root_ready, 2)
                for k in range(2):
                    u, w = diff[:, k * E:(k + 1) * E], prod[:, k * E:(k + 1) * E]
                    s, t = bn[:, 2 * k * E:(2 * k + 1) * E], bn[:, (2 * k + 1) * E:(2 * k + 2) * E]
                    nc.vector.tensor_tensor(s, col(f"g{k + 1}"), var[:, k * E:(k + 1) * E], ALU.mult).then_inc(qstep, 1)
                    nc.vector.tensor_tensor(u, col(f"b{k + 1}"), col(f"m{k + 1}"), ALU.subtract).then_inc(qstep, 1)
                    c.next()
                    dve.wait_ge(qstep, c.next())
                    nc.vector.tensor_tensor(w, u, s, ALU.mult).then_inc(qstep, 1)
                    dve.wait_ge(qstep, c.next())
                    nc.vector.tensor_tensor(t, w, col(f"be{k + 1}"), ALU.add)

        with ExitStack() as ctx:
            def tile(name, shape, dt=F32):
                return sb(name, shape, dt, ctx)

            ST, MV, RS = tile("bST", [P, NT, 6]), tile("bMV", [P, NT, 2]), tile("bRS", [P, 7, NT])
            XN = tile("bXN", [P, N])
            XT = tile("bXT", [P, 2 * N])
            LT = tile("LT", [E, N])
            LG, Q, OH1, OH2, L2, W8, WR = (tile(n, [P, NT, E]) for n in ("LG", "Q", "OH1", "OH2", "L2", "W8", "WR"))
            m1, m2, k1, dd, ex, s1, w1, w2 = (tile(n, [P, NT]) for n in ("m1", "m2", "k1", "dd", "ex", "s1", "w1", "w2"))
            W3 = tile("W3", [P, NT, 3 * E], BF16)
            WT3 = tile("WT3", [3 * E, 2 * N], BF16)
            WT8 = tile("WT8", [E, 2 * N])
            G, GW = tile("G", [P, 2, HALF]), tile("GW", [P, 4, HALF])
            YS = tile("YS", [P, 2, HALF])
            U, WB, Y, M = ([ctx.enter_context(nc.psum_tensor(f"b{n}{i}", [P, HALF], F32)) for i in range(2)]
                           for n in ("U", "WB", "Y", "M"))
            W3T = M[0][:, :].bitcast(BF16)
            mv_ready, rs_ready, xn_ready, dstep, pstep = (sem("b_" + n) for n in (
                "mv_ready", "rs_ready", "xn_ready", "dve_step", "pool_step"))
            xt_ps, xt_ready, rt_ps, rt_ready, wt8_ps, wt8_ready, ys_ready, yt_ps, x_added = (
                [sem(f"b_{n}{h}") for h in range(2)] for n in (
                    "xt_ps", "xt_ready", "rt_ps", "rt_ready", "wt8_ps", "wt8_ready", "ys_ready", "yt_ps", "x_added"))
            lg_ps, lg_ready, dd_ready, ex_ready, w_ready, w3t_ps, wt3_ready, u_ready, g_ready, wb_ready, gw_ready, y_mm = (
                sem("b_" + n) for n in ("lg_ps", "lg_ready", "dd_ready", "ex_ready", "w_ready", "w3t_ps", "wt3_ready",
                                        "u_ready", "g_ready", "wb_ready", "gw_ready", "y_mm"))
            S = 2 * E * HC
            G_RING, GW_RING = 2, 4
            block = ctx.enter_context(nc.Block())

            @block.gpsimd
            def _(pool):
                step = Count()
                ln_root(pool, 0, MV, RS, pstep, step, mv_ready, rs_ready, True)
                with pool.Fori(1, B) as b:
                    step.loop(b - 1, 6)
                    ln_root(pool, b, MV, RS, pstep, step, mv_ready, rs_ready, True)
                step.end(B - 1)

            @block.tensor
            def _(pe):
                pe.sem_inc(y_mm, GW_RING)

                def turn_x(b, h):
                    pe.wait_ge(xn_ready, b + 1)
                    for t in range(4):
                        i = pe.transpose(M[h][:, t * P:(t + 1) * P], XN[:, bass.ts(4 * h + t, P)], ident[:, :])
                    i.then_inc(xt_ps[h], 1)

                def route(b, h):
                    hold(pe, xt_ready[h], b + 1)
                    pe.matmul(M[h][0:E, :], Wr0[:, :], XT[:, bass.ds((b % 2) * N + h * HALF, HALF)], start=True, stop=True
                              ).then_inc(rt_ps[h], 1)

                def turn_logits(b):
                    hold(pe, rt_ready[0], b + 1)
                    hold(pe, rt_ready[1], b + 1)
                    for t in range(NT):
                        i = pe.transpose(M[0][:, t * E:(t + 1) * E], LT[:, t * P:(t + 1) * P], ident[0:E, 0:E])
                    i.then_inc(lg_ps, 1)

                def turn_w3(b):
                    pe.wait_ge(w_ready, b + 1)
                    for t in range(NT):
                        i = pe.transpose(W3T[0:3 * E, t * P:(t + 1) * P], W3[:, t, :], identb[:, :])
                    i.then_inc(w3t_ps, 1)

                def turn_w8(b, h):
                    pe.wait_ge(wt3_ready, b + 1)
                    for t in range(4):
                        i = pe.transpose(M[h][0:E, t * P:(t + 1) * P], W8[:, 4 * h + t, :], ident[:, :])
                    i.then_inc(wt8_ps[h], 1)

                def turn_y(b, q, wt8):
                    pe.wait_ge(ys_ready[q], b + 1)
                    hold(pe, wt8_ready[q], wt8)
                    for t in range(4):
                        i = pe.transpose(M[q][:, t * P:(t + 1) * P], YS[:, q, t * P:(t + 1) * P], ident[:, :])
                    i.then_inc(yt_ps[q], 1)

                def hidden(b, s):
                    q, e, hc = s // (E * HC), s // HC % E, s % HC
                    half = bass.ds((b % 2) * N + q * HALF, HALF)
                    pe.wait_ge(g_ready, b * S + s + 1)
                    pe.matmul(U[s % 2][:, :], W1[:, e * HID + hc * P:e * HID + (hc + 1) * P], XT[:, half],
                              start=True, stop=True).then_inc(u_ready, 1)
                    if hc == 0:
                        hold(pe, gw_ready, b * S + s + 1)
                        pe.matmul(WB[e % 2][:, :], pick[:, e * P:(e + 1) * P], WT3[:, half],
                                  start=True, stop=True).then_inc(wb_ready, 1)

                def project(b, s):
                    q, e, hc = s // (E * HC), s // HC % E, s % HC
                    if s % (E * HC) == 0:
                        pe.matmul(Y[q][:, :], b20[:, :], WT8[:, bass.ds((b % 2) * N + q * HALF, HALF)],
                                  start=True, stop=False)
                    hold(pe, gw_ready, b * S + s + 1 + G_RING)
                    pe.matmul(Y[q][:, :], W2[:, (e * HC + hc) * P:(e * HC + hc + 1) * P], GW[:, s % 4, :],
                              start=False, stop=(s % (E * HC) == E * HC - 1)).then_inc(y_mm, 1)

                def batch(b, last):
                    for s in range(S + 2):
                        if s < S:
                            hidden(b, s)
                        if s >= 2:
                            project(b, s - 2)
                        if not last:
                            if s in (4, 5):
                                turn_x(b + 1, s - 4)
                            if s in (7, 8):
                                route(b + 1, s - 7)
                            if s == 10:
                                turn_logits(b + 1)
                            if s == 18:
                                turn_w3(b + 1)
                            if s in (20, 21):
                                turn_w8(b + 1, s - 20)
                        if s == S // 2 + 7:
                            turn_y(b, 0, b + 1 if last else b + 2)
                    turn_y(b, 1, b + 1 if last else b + 2)

                for h in range(2):
                    turn_x(0, h)
                for h in range(2):
                    route(0, h)
                turn_logits(0)
                turn_w3(0)
                for h in range(2):
                    turn_w8(0, h)
                hold(pe, wt8_ready[0], 1)
                hold(pe, wt8_ready[1], 1)
                with pe.Fori(0, B - 1) as b:
                    batch(b, False)
                batch(B - 1, True)

            @block.scalar
            def _(act):
                act.sem_inc(g_ready, G_RING)

                def copy_xt(b, h):
                    act.wait_ge(xt_ps[h], b + 1)
                    wait(act, y_mm, (b - 1) * S + GW_RING)
                    nc.scalar.activation(XT[:, bass.ds((b % 2) * N + h * HALF, HALF)], M[h][:, :], ACT.Identity,
                                         bias=pcol[:, at["L0_ffn_beta"]:at["L0_ffn_beta"] + 1],
                                         scale=pcol[:, at["L0_ffn_gamma"]:at["L0_ffn_gamma"] + 1]).then_inc(xt_ready[h], 1)

                def copy_route(b, h):
                    act.wait_ge(rt_ps[h], b + 1)
                    wait(act, lg_ps, b)
                    nc.scalar.copy(LT[:, h * HALF:(h + 1) * HALF], M[h][0:E, :]).then_inc(rt_ready[h], 1)

                def exp_second(b):
                    act.wait_ge(dd_ready, b + 1)
                    nc.scalar.activation(ex[:, :], dd[:, :], ACT.Exp).then_inc(ex_ready, 1)

                def copy_w8(b, h):
                    act.wait_ge(wt8_ps[h], b + 1)
                    nc.scalar.copy(WT8[:, bass.ds((b % 2) * N + h * HALF, HALF)], M[h][0:E, :]).then_inc(wt8_ready[h], 1)

                def gelu(b, s):
                    e, hc = s // HC % E, s % HC
                    act.wait_ge(gw_ready, b * S + s + 1)
                    act.wait_ge(u_ready, b * S + s + 1)
                    nc.scalar.activation(G[:, s % 2, :], U[s % 2][:, :], ACT.Gelu,
                                         bias=pcol[:, at["L0_ffn_b1"] + e * HC + hc:at["L0_ffn_b1"] + e * HC + hc + 1]
                                         ).then_inc(g_ready, 1)

                def copy_y(b, q):
                    act.wait_ge(y_mm, b * S + (q + 1) * E * HC + GW_RING)
                    nc.scalar.copy(YS[:, q, :], Y[q][:, :]).then_inc(ys_ready[q], 1)

                def batch(b, last):
                    for s in range(S):
                        gelu(b, s)
                        if not last:
                            if s in (4, 5):
                                copy_xt(b + 1, s - 4)
                            if s in (7, 8):
                                copy_route(b + 1, s - 7)
                            if s == 14:
                                exp_second(b + 1)
                            if s in (20, 21):
                                copy_w8(b + 1, s - 20)
                        if s == S // 2 + 4:
                            copy_y(b, 0)
                    copy_y(b, 1)

                for h in range(2):
                    copy_xt(0, h)
                for h in range(2):
                    copy_route(0, h)
                exp_second(0)
                for h in range(2):
                    copy_w8(0, h)
                with act.Fori(0, B - 1) as b:
                    batch(b, False)
                batch(B - 1, True)

            @block.vector
            def _(dve):
                dve.sem_inc(gw_ready, G_RING)
                step = Count()

                def op(f, *a, **k):
                    f(*a, **k).then_inc(dstep, 1)
                    hold(dve, dstep, step.next())

                def wide(v):
                    return v[:, :].unsqueeze(2).to_broadcast([P, NT, E])

                def norm(b):
                    if not isinstance(b, int) or b > 0:
                        dve.wait_ge(xt_ps[1], b)
                    ln_apply(dve, b, MV, RS[:, 6, :], XN, 0, rs_ready, xn_ready)

                def first_max(logits, top, onehot):
                    v = nc.vector
                    op(v.tensor_reduce, top[:, :], logits, AX_X, ALU.max)
                    op(v.tensor_tensor, Q[:, :, :], logits, wide(top), ALU.is_equal)
                    op(v.tensor_tensor, Q[:, :, :], Q[:, :, :], order[:, :].unsqueeze(1).to_broadcast([P, NT, E]), ALU.mult)
                    op(v.tensor_reduce, k1[:, :], Q[:, :, :], AX_X, ALU.max)
                    op(v.tensor_tensor, onehot, Q[:, :, :], wide(k1), ALU.is_equal)

                def choose(b):
                    v = nc.vector
                    dve.wait_ge(lg_ps, b + 1)
                    op(v.tensor_tensor, LG[:, :, :], M[0][:, 0:NT * E].rearrange("p (t e) -> p t e", e=E),
                       br0[:, :].unsqueeze(1).to_broadcast([P, NT, E]), ALU.add)
                    first_max(LG[:, :, :], m1, OH1[:, :, :])
                    op(v.scalar_tensor_tensor, out=L2[:, :, :], in0=OH1[:, :, :], scalar=-1e30, in1=LG[:, :, :],
                       op0=ALU.mult, op1=ALU.add)
                    first_max(L2[:, :, :], m2, OH2[:, :, :])
                    v.tensor_tensor(dd[:, :], m2[:, :], m1[:, :], ALU.subtract).then_inc(dd_ready, 1)

                def weigh(b):
                    v = nc.vector
                    hold(dve, ex_ready, b + 1)
                    wait(dve, wt8_ps[1], b)
                    op(v.tensor_scalar, s1[:, :], ex[:, :], 1.0, None, ALU.add)
                    op(v.reciprocal, w1[:, :], s1[:, :])
                    op(v.tensor_tensor, w2[:, :], ex[:, :], w1[:, :], ALU.mult)
                    op(v.tensor_tensor, W8[:, :, :], OH1[:, :, :], wide(w1), ALU.mult)
                    op(v.tensor_tensor, Q[:, :, :], OH2[:, :, :], wide(w2), ALU.mult)
                    op(v.tensor_tensor, W8[:, :, :], W8[:, :, :], Q[:, :, :], ALU.add)
                    op(v.tensor_copy, W3[:, :, 0:E], W8[:, :, :])
                    op(v.tensor_tensor, WR[:, :, :], W8[:, :, :], W3[:, :, 0:E], ALU.subtract)
                    op(v.tensor_copy, W3[:, :, E:2 * E], WR[:, :, :])
                    v.tensor_tensor(W3[:, :, 2 * E:3 * E], WR[:, :, :], W3[:, :, E:2 * E], ALU.subtract).then_inc(w_ready, 1)

                def copy_w3(b):
                    dve.wait_ge(w3t_ps, b + 1)
                    nc.vector.tensor_copy(WT3[:, bass.ds((b % 2) * N, N)], W3T[0:3 * E, 0:N]).then_inc(wt3_ready, 1)

                def times_weight(b, s):
                    if s % HC == 0:
                        dve.wait_ge(wb_ready, b * 2 * E + s // HC + 1)
                    dve.wait_ge(y_mm, b * S + s + 1)
                    dve.wait_ge(g_ready, b * S + s + 1 + G_RING)
                    nc.vector.tensor_tensor(GW[:, s % 4, :], G[:, s % 2, :], WB[s // HC % 2][:, :], ALU.mult
                                            ).then_inc(gw_ready, 1)

                def add(b, q):
                    dve.wait_ge(yt_ps[q], b + 1)
                    xb = X[:, bass.ds(b * N + q * HALF, HALF)]
                    nc.vector.tensor_tensor(xb, M[q][:, :], xb, ALU.add).then_inc(x_added[q], 1)

                def batch(b, last):
                    for s in range(S):
                        times_weight(b, s)
                        if not last:
                            if s == 0:
                                ln_stats(dve, b + 1, ST, MV, dstep, step, mv_ready)
                            if s == 2:
                                norm(b + 1)
                            if s == 10:
                                choose(b + 1)
                            if s == 15:
                                weigh(b + 1)
                            if s == 18:
                                copy_w3(b + 1)
                        if s == S // 2 + 8:
                            add(b, 0)
                    add(b, 1)

                ln_stats(dve, 0, ST, MV, dstep, step, mv_ready)
                norm(0)
                choose(0)
                weigh(0)
                copy_w3(0)
                with dve.Fori(0, B - 1) as b:
                    step.loop(b, 22)
                    batch(b, False)
                step.end(B - 1)
                batch(B - 1, True)

        shared_sems = {}

        def either(name):
            if name not in shared_sems:
                shared_sems[name] = sem("c_" + name)
            return shared_sems[name]

        def edge_attention(kinds, ctx, pre):
            def tile(name, shape, dt=F32):
                return sb(pre + name, shape, dt, ctx)

            ADJ = tile("ADJ", [P, 4, N], I32)
            NK = tile("NK", [P, 2, kinds, N], BF16)
            AK = tile("AK", [P, 2, kinds, P])
            ST, MV, RS = tile("ST", [P, NT, 6]), tile("MV", [P, NT, 2]), tile("RS", [P, 2, NT])
            XN = tile("XN", [P, N])
            XB, XT = tile("XB", [P, 2 * N]), tile("XT", [P, 2 * N])
            ACC = tile("ACC", [P, 2, N]) if kinds > 1 else None
            R4, Y, PR, PT = (tile(n, [P, 2, N]) for n in ("R4", "Y", "PR", "PT"))
            MX, NMX, Z, RZ = (tile(n, [P, 2]) for n in ("MX", "NMX", "Z", "RZ"))
            T = [ctx.enter_context(nc.psum_tensor(f"{pre}T{i}", [P, N], F32)) for i in range(2)]
            TP = [ctx.enter_context(nc.psum_tensor(f"{pre}TP{i}", [P, HALF], F32)) for i in range(2)]
            O = ctx.enter_context(nc.psum_tensor(pre + "O", [P, HALF], F32))
            M = ctx.enter_context(nc.psum_tensor(pre + "M", [P, HALF], F32))
            (mv_ready, rs_ready, xn_ready, dstep, pstep, xt_ps, xt_ready, made, t_ready, t_read, acc_ready, r4_ready, y_ready,
             shift_ready, pr_ready, pv_done, x_added, xb_ready) = (either(n) for n in (
                 "mv_ready", "rs_ready", "xn_ready", "dve_step", "pool_step", "xt_ps", "xt_ready", "made", "t_ready",
                 "t_read", "acc_ready", "r4_ready", "y_ready", "shift_ready", "pr_ready", "pv_done", "x_added", "xb_ready"))
            tp_ps, tp_read = ([either(f"{n}{h}") for h in range(2)] for n in ("tp_ps", "tp_read"))
            loaded = [either(f"adj_loaded{i}") for i in range(4)]
            K = kinds
            LAST = B - 1
            block = ctx.enter_context(nc.Block())

            @block.sync
            def _(sp):
                def load(b):
                    for t in range(NT):
                        wait(sp, made, b * NT + t - 3)
                        sp.dma_start(ADJ[:, t % 4, :], adj[bass.ds(b, 1), t * P:(t + 1) * P, :].rearrange("o p i -> (o p) i")
                                     ).then_inc(loaded[t % 4], 16)
                load(0)
                with sp.Fori(1, B) as b:
                    load(b)

            @block.gpsimd
            def _(pool):
                step = Count()

                def batch(b):
                    ln_root(pool, b, MV, RS, pstep, step, mv_ready, rs_ready, False)
                    pool.wait_ge(xn_ready, b + 1)
                    nc.gpsimd.tensor_copy(XB[:, bass.ds((b % 2) * N, N)], XN[:, :]).then_inc(xb_ready, 1)

                batch(0)
                with pool.Fori(1, B) as b:
                    step.loop(b - 1, 1)
                    batch(b)
                step.end(B - 1)

            @block.tensor
            def _(pe):
                def turn_x(b, h):
                    pe.wait_ge(xn_ready, b + 1)
                    wait(pe, xt_ready, 2 * b + h)
                    for t in range(4):
                        i = pe.transpose(M[:, t * P:(t + 1) * P], XN[:, bass.ts(4 * h + t, P)], ident[:, :])
                    i.then_inc(xt_ps, 1)

                def scores(b, r):
                    g = b * NT + r
                    hold(pe, made, g + 1)
                    for k in range(K):
                        t = T[k % 2] if K > 1 else T[r % 2]
                        if not isinstance(g, int) or g * K + k > 1:
                            hold(pe, t_read, g * K + k - 1)
                        for h in range(2):
                            pe.matmul(t[:, h * HALF:(h + 1) * HALF], AK[:, r % 2, k, :],
                                      XT[:, bass.ds((b % 2) * N + h * HALF, HALF)], start=True, stop=False)
                            i = pe.matmul(t[:, h * HALF:(h + 1) * HALF], blockI[:, :], NK[:, r % 2, k, h * HALF:(h + 1) * HALF],
                                          start=False, stop=True)
                        i.then_inc(t_ready, 1)

                def turn_p(b, r):
                    pe.wait_ge(pr_ready, b * NT + r + 1)
                    for h in range(2):
                        wait(pe, tp_read[h], b * NT + r)
                        for c in range(4):
                            i = pe.transpose(TP[h][:, c * P:(c + 1) * P], PR[:, r % 2, (4 * h + c) * P:(4 * h + c + 1) * P],
                                             ident[:, :])
                        i.then_inc(tp_ps[h], 1)

                def attend(b, r):
                    if r == 0:
                        hold(pe, xb_ready, b + 1)
                    hold(pe, x_added, b * NT + r)
                    for h in range(2):
                        hold(pe, tp_read[h], b * NT + r + 1)
                        for c in range(4 * h, 4 * h + 4):
                            i = pe.matmul(O[:, 0:P], PT[:, r % 2, c * P:(c + 1) * P], XB[:, bass.ds((b % 2) * N + c * P, P)],
                                          start=(c == 0), stop=(c == NT - 1))
                    i.then_inc(pv_done, 1)

                def batch(b, first, last):
                    for r in range(NT):
                        scores(b, r)
                        if r >= 1:
                            turn_p(b, r - 1)
                        elif not first:
                            turn_p(b - 1, NT - 1)
                        if r >= 2:
                            attend(b, r - 2)
                        elif not first:
                            attend(b - 1, NT - 2 + r)
                        if not last and r in (4, 5):
                            turn_x(b + 1, r - 4)

                for h in range(2):
                    turn_x(0, h)
                batch(0, True, False)
                with pe.Fori(1, LAST) as b:
                    batch(b, False, False)
                batch(LAST, False, True)
                turn_p(LAST, NT - 1)
                attend(LAST, NT - 2)
                attend(LAST, NT - 1)

            @block.scalar
            def _(act):
                def copy_xt(b, h):
                    act.wait_ge(xt_ps, 2 * b + h + 1)
                    wait(act, t_ready, (b - 1) * NT * K)
                    wait(act, made, (b - 1) * NT)
                    nc.scalar.copy(XT[:, bass.ds((b % 2) * N + h * HALF, HALF)], M[:, :]).then_inc(xt_ready, 1)

                def relu(b, r):
                    g = b * NT + r
                    wait(act, y_ready, g - 1)
                    if K > 1:
                        act.wait_ge(t_ready, g * K + 1)
                        nc.scalar.copy(ACC[:, r % 2, :], T[0][:, :]).then_inc(t_read, 1)
                        act.wait_ge(acc_ready, g * (K - 1) + K - 1)
                        nc.scalar.activation(R4[:, r % 2, :], ACC[:, r % 2, :], ACT.Relu, scale=4.0).then_inc(r4_ready, 1)
                    else:
                        act.wait_ge(t_ready, g + 1)
                        nc.scalar.activation(R4[:, r % 2, :], T[r % 2][:, :], ACT.Relu, scale=4.0).then_inc(r4_ready, 1)

                def prob(b, r):
                    g = b * NT + r
                    act.wait_ge(shift_ready, g + 1)
                    wait(act, tp_ps[1], g - 1)
                    wait(act, x_added, g - 1)
                    nc.scalar.activation(PR[:, r % 2, :], Y[:, r % 2, :], ACT.Exp, bias=NMX[:, r % 2:r % 2 + 1], scale=SLOPE,
                                         accum_out=Z[:, r % 2:r % 2 + 1]).then_inc(pr_ready, 1)

                def copy_p(b, r):
                    g = b * NT + r
                    act.wait_ge(tp_ps[0], g + 1)
                    wait(act, pv_done, g - 1)
                    nc.scalar.copy(PT[:, r % 2, 0:HALF], TP[0][:, :]).then_inc(tp_read[0], 1)

                def batch(b, first, last):
                    for r in range(NT):
                        relu(b, r)
                        if r >= 1:
                            copy_p(b, r - 1)
                        elif not first:
                            copy_p(b - 1, NT - 1)
                        prob(b, r)
                        if not last and r in (4, 5):
                            copy_xt(b + 1, r - 4)

                for h in range(2):
                    copy_xt(0, h)
                batch(0, True, False)
                with act.Fori(1, LAST) as b:
                    batch(b, False, False)
                batch(LAST, False, True)
                copy_p(LAST, NT - 1)

            @block.vector
            def _(dve):
                step = Count()

                def make(b, r):
                    g = b * NT + r
                    if r == 0:
                        dve.wait_ge(xt_ready, 2 * b + 2)
                    wait(dve, t_ready, (g - 1) * K)
                    for k in range(K):
                        nc.vector.tensor_scalar(AK[:, r % 2, k, :], XT[:, bass.ds((b % 2) * N + r * P, P)],
                                                pcol[:, at[f"L1_gnn_a{k}"]:at[f"L1_gnn_a{k}"] + 1], None, ALU.mult)
                    dve.wait_ge(loaded[r % 4], 16 * (b * (NT // 4) + r // 4 + 1))
                    for k in range(K):
                        i = nc.vector.tensor_scalar(NK[:, r % 2, k, :], ADJ[:, r % 4, :], float(k + 1), None, ALU.not_equal)
                    i.then_inc(made, 1)

                def shift(b, r):
                    g = b * NT + r
                    for k in range(1, K):
                        hold(dve, t_read, g * K + k)
                        dve.wait_ge(t_ready, g * K + k + 1)
                        nc.vector.tensor_tensor(ACC[:, r % 2, :], ACC[:, r % 2, :], T[k % 2][:, :], ALU.max).then_inc(t_read, 1)
                        hold(dve, t_read, g * K + k + 1)
                        dve.sem_inc(acc_ready, 1)
                    if not isinstance(g, int) or g > 1:
                        hold(dve, pr_ready, g - 1)
                    hold(dve, r4_ready, g + 1)
                    i = nc.vector.tensor_tensor_reduce(Y[:, r % 2, :], T[r % 2][:, :] if K == 1 else ACC[:, r % 2, :],
                                                       R4[:, r % 2, :], 1.0, -3.0e38, ALU.add, ALU.max, MX[:, r % 2:r % 2 + 1])
                    i.then_inc(y_ready, 1)
                    hold(dve, y_ready, g + 1)
                    if K == 1:
                        dve.sem_inc(t_read, 1)
                    nc.vector.tensor_scalar(NMX[:, r % 2:r % 2 + 1], MX[:, r % 2:r % 2 + 1], -SLOPE, None, ALU.mult
                                            ).then_inc(shift_ready, 1)

                def copy_p(b, r):
                    g = b * NT + r
                    dve.wait_ge(tp_ps[1], g + 1)
                    wait(dve, pv_done, g - 1)
                    nc.vector.tensor_copy(PT[:, r % 2, HALF:N], TP[1][:, :]).then_inc(tp_read[1], 1)

                def add(b, r):
                    g = b * NT + r
                    nc.vector.reciprocal(RZ[:, r % 2:r % 2 + 1], Z[:, r % 2:r % 2 + 1]).then_inc(dstep, 1)
                    dve.wait_ge(dstep, step.next())
                    dve.wait_ge(pv_done, g + 1)
                    xb = X[:, bass.ds(b * N + r * P, P)]
                    nc.vector.scalar_tensor_tensor(out=xb, in0=O[:, 0:P], scalar=RZ[:, r % 2:r % 2 + 1], in1=xb,
                                                   op0=ALU.mult, op1=ALU.add).then_inc(x_added, 1)

                def norm(b):
                    if not isinstance(b, int) or b > 0:
                        dve.wait_ge(xt_ps, 2 * b)
                        dve.wait_ge(xb_ready, b)
                    ln_apply(dve, b, MV, RS[:, 1, :], XN, 0, rs_ready, xn_ready)

                def batch(b, first, last):
                    for r in range(NT):
                        if not (last and r == NT - 1):
                            make(b + (r + 1) // NT, (r + 1) % NT)
                        shift(b, r)
                        if r >= 1:
                            copy_p(b, r - 1)
                        elif not first:
                            copy_p(b - 1, NT - 1)
                        if r >= 2:
                            add(b, r - 2)
                        elif not first:
                            add(b - 1, NT - 2 + r)
                        if not last:
                            if r == 1:
                                ln_stats(dve, b + 1, ST, MV, dstep, step, mv_ready)
                            if r == 3:
                                norm(b + 1)

                ln_stats(dve, 0, ST, MV, dstep, step, mv_ready)
                norm(0)
                make(0, 0)
                batch(0, True, False)
                with dve.Fori(1, LAST) as b:
                    step.loop(b - 1, 9)
                    batch(b, False, False)
                step.end(LAST - 1)
                batch(LAST, False, True)
                copy_p(LAST, NT - 1)
                add(LAST, NT - 2)
                add(LAST, NT - 1)

        several = nc.values_load(flag[:, :], min_val=0, max_val=1)
        with nc.If(several > 0):
            with ExitStack() as ctx:
                edge_attention(4, ctx, "g_")
        with nc.Else():
            with ExitStack() as ctx:
                edge_attention(1, ctx, "f_")

        with ExitStack() as last_layer:
            def tile(name, shape, dt=F32, ctx=last_layer):
                return sb(name, shape, dt, ctx)

            XT = tile("dXT", [P, B * N])
            WT8 = tile("dWT8", [E, N])
            WBC = tile("WBC", [P, E, N])

            with ExitStack() as ctx:
                ST, MV, RS = (tile(n, s, F32, ctx) for n, s in (("dST", [P, NT, 6]), ("dMV", [P, NT, 2]), ("dRS", [P, 2, NT])))
                XN, FT = tile("dXN", [P, N], F32, ctx), tile("FT", [P, N], F32, ctx)
                LG, EX, W8, WR = (tile("d" + n, [P, NT, E], F32, ctx) for n in ("LG", "EX", "W8", "WR"))
                mx, sm, rs = (tile("d" + n, [P, NT], F32, ctx) for n in ("mx", "sm", "rs"))
                W3 = tile("dW3", [P, NT, 3 * E], BF16, ctx)
                WT3 = tile("dWT3", [3 * E, N], BF16, ctx)
                M = [ctx.enter_context(nc.psum_tensor(f"dM{i}", [P, HALF], F32)) for i in range(2)]
                BC = [ctx.enter_context(nc.psum_tensor(f"BC{i}", [P, HALF], F32)) for i in range(2)]
                W3T = M[0][:, :].bitcast(BF16)
                (mv_ready, rs_ready, xn_ready, dstep, pstep, ft_ready, lg_ps, lg_ready, ex_ready, w_ready, w3t_ps,
                 wt3_ready, bc_ps, bc_act, bc_dve) = (sem("d_" + n) for n in (
                     "mv_ready", "rs_ready", "xn_ready", "dve_step", "pool_step", "ft_ready", "lg_ps", "lg_ready",
                     "ex_ready", "w_ready", "w3t_ps", "wt3_ready", "bc_ps", "bc_act", "bc_dve"))
                xt_ps, xt_ready, wt8_ps = ([sem(f"d_{n}{h}") for h in range(2)] for n in ("xt_ps", "xt_ready", "wt8_ps"))
                wt8_done = sem("d_wt8_done")
                block = ctx.enter_context(nc.Block())

                @block.gpsimd
                def _(pool):
                    step = Count()
                    with pool.Fori(0, B) as b:
                        step.loop(b, 1)
                        ln_root(pool, b, MV, RS, pstep, step, mv_ready, rs_ready, False)
                    step.end(B)
                    for b in range(B):
                        for h in range(2):
                            pool.wait_ge(xt_ready[h], b + 1)
                        v = XT[:, b * N:(b + 1) * N]
                        if b == 1:
                            nc.gpsimd.tensor_tensor(FT[:, :], XT[:, 0:N], v, ALU.add).then_inc(ft_ready, 1)
                        elif b > 1:
                            pool.wait_ge(ft_ready, b - 1)
                            nc.gpsimd.tensor_tensor(FT[:, :], FT[:, :], v, ALU.add).then_inc(ft_ready, 1)

                @block.tensor
                def _(pe):
                    def turn_x(b):
                        pe.wait_ge(xn_ready, b + 1)
                        for h in range(2):
                            wait(pe, xt_ready[h], b)
                            for t in range(4):
                                i = pe.transpose(M[h][:, t * P:(t + 1) * P], XN[:, bass.ts(4 * h + t, P)], ident[:, :])
                            i.then_inc(xt_ps[h], 1)

                    turn_x(0)
                    with pe.Fori(1, B) as b:
                        turn_x(b)
                    pe.wait_ge(ft_ready, B - 1)
                    for t in range(NT):
                        i = pe.matmul(M[0][:, t * E:(t + 1) * E], FT[:, t * P:(t + 1) * P], Wr1[:, :], start=True, stop=True)
                    i.then_inc(lg_ps, 1)
                    pe.wait_ge(w_ready, 1)
                    for t in range(NT):
                        i = pe.transpose(W3T[0:3 * E, t * P:(t + 1) * P], W3[:, t, :], identb[:, :])
                    i.then_inc(w3t_ps, 1)
                    pe.wait_ge(wt3_ready, 1)
                    for h in range(2):
                        for t in range(4):
                            i = pe.transpose(M[h][0:E, t * P:(t + 1) * P], W8[:, 4 * h + t, :], ident[:, :])
                        i.then_inc(wt8_ps[h], 1)
                    for k in range(2 * E):
                        wait(pe, (bc_act, bc_dve)[k % 2], k // 2)
                        pe.matmul(BC[k % 2][:, :], pick[:, k // 2 * P:(k // 2 + 1) * P],
                                  WT3[:, k % 2 * HALF:(k % 2 + 1) * HALF], start=True, stop=True).then_inc(bc_ps, 1)

                @block.scalar
                def _(act):
                    with act.Fori(0, B) as b:
                        for h in range(2):
                            act.wait_ge(xt_ps[h], b + 1)
                            nc.scalar.copy(XT[:, bass.ds(b * N + h * HALF, HALF)], M[h][:, :]).then_inc(xt_ready[h], 1)
                    act.wait_ge(lg_ready, 1)
                    nc.scalar.activation(EX[:, :, :], LG[:, :, :], ACT.Exp).then_inc(ex_ready, 1)
                    for h in range(2):
                        act.wait_ge(wt8_ps[h], 1)
                        nc.scalar.copy(WT8[:, h * HALF:(h + 1) * HALF], M[h][0:E, :]).then_inc(wt8_done, 1)
                    for e in range(E):
                        act.wait_ge(bc_ps, 2 * e + 1)
                        nc.scalar.copy(WBC[:, e, 0:HALF], BC[0][:, :]).then_inc(bc_act, 1)

                @block.vector
                def _(dve):
                    step = Count()
                    v = nc.vector

                    def op(f, *a, **k):
                        f(*a, **k).then_inc(dstep, 1)
                        dve.wait_ge(dstep, step.next())

                    def wide(t):
                        return t[:, :].unsqueeze(2).to_broadcast([P, NT, E])

                    def norm(b):
                        ln_stats(dve, b, ST, MV, dstep, step, mv_ready)
                        wait(dve, xt_ps[1], b)
                        ln_apply(dve, b, MV, RS[:, 1, :], XN, 0, rs_ready, xn_ready)

                    norm(0)
                    with dve.Fori(1, B) as b:
                        step.loop(b - 1, 1)
                        norm(b)
                    step.end(B - 1)
                    dve.wait_ge(lg_ps, 1)
                    op(v.scalar_tensor_tensor, out=LG[:, :, :], in0=M[0][:, 0:NT * E].rearrange("p (t e) -> p t e", e=E),
                       scalar=1.0 / B, in1=br1[:, :].unsqueeze(1).to_broadcast([P, NT, E]), op0=ALU.mult, op1=ALU.add)
                    op(v.tensor_reduce, mx[:, :], LG[:, :, :], AX_X, ALU.max)
                    v.tensor_tensor(LG[:, :, :], LG[:, :, :], wide(mx), ALU.subtract).then_inc(lg_ready, 1)
                    dve.wait_ge(ex_ready, 1)
                    op(v.tensor_reduce, sm[:, :], EX[:, :, :], AX_X, ALU.add)
                    op(v.reciprocal, rs[:, :], sm[:, :])
                    op(v.tensor_tensor, W8[:, :, :], EX[:, :, :], wide(rs), ALU.mult)
                    op(v.tensor_copy, W3[:, :, 0:E], W8[:, :, :])
                    op(v.tensor_tensor, WR[:, :, :], W8[:, :, :], W3[:, :, 0:E], ALU.subtract)
                    op(v.tensor_copy, W3[:, :, E:2 * E], WR[:, :, :])
                    v.tensor_tensor(W3[:, :, 2 * E:3 * E], WR[:, :, :], W3[:, :, E:2 * E], ALU.subtract).then_inc(w_ready, 1)
                    dve.wait_ge(w3t_ps, 1)
                    v.tensor_copy(WT3[:, :], W3T[0:3 * E, 0:N]).then_inc(wt3_ready, 1)
                    for e in range(E):
                        dve.wait_ge(bc_ps, 2 * e + 2)
                        v.tensor_copy(WBC[:, e, HALF:N], BC[1][:, :]).then_inc(bc_dve, 1)

            with ExitStack() as ctx:
                H1, H2, GW, YS = (tile(n, [P, 2, HALF], F32, ctx) for n in ("H1", "H2", "dGW", "dYS"))
                U1, U2, Y, M = ([ctx.enter_context(nc.psum_tensor(f"e{n}{i}", [P, HALF], F32)) for i in range(2)]
                                for n in ("U1", "U2", "Y", "M"))
                u1_ready, h1_ready, u2_ready, h2_ready, gw_ready, y_mm = (sem("e_" + n) for n in (
                    "u1_ready", "h1_ready", "u2_ready", "h2_ready", "gw_ready", "y_mm"))
                ys_ready, yt_ps, x_added, stored = ([sem(f"e_{n}{h}") for h in range(2)] for n in (
                    "ys_ready", "yt_ps", "x_added", "stored"))
                S = 2 * E
                AGO = 3
                block = ctx.enter_context(nc.Block())

                @block.sync
                def _(sp):
                    with sp.Fori(0, B) as b:
                        for q in range(2):
                            sp.wait_ge(x_added[q], b + 1)
                            sp.dma_start(out[bass.ds(b, 1), q * HALF:(q + 1) * HALF, :].rearrange("o (t p) d -> p (o t) d", p=P),
                                         X[:, bass.ds(b * N + q * HALF, HALF)].rearrange("p (t d) -> p t d", d=P)
                                         ).then_inc(stored[q], 16)
                    for q in range(2):
                        sp.wait_ge(stored[q], 16 * B)

                @block.tensor
                def _(pe):
                    def first(b, s):
                        wait(pe, h1_ready, b * S + s - 1)
                        pe.matmul(U1[s % 2][:, :], V1[:, s % E * P:(s % E + 1) * P], XT[:, bass.ds(b * N + s // E * HALF, HALF)],
                                  start=True, stop=True).then_inc(u1_ready, 1)

                    def second(b, s):
                        pe.wait_ge(h1_ready, b * S + s + 1)
                        wait(pe, h2_ready, b * S + s - 1)
                        pe.matmul(U2[s % 2][:, :], V2[:, s % E * P:(s % E + 1) * P], H1[:, s % 2, :],
                                  start=True, stop=True).then_inc(u2_ready, 1)

                    def third(b, s):
                        q, e = s // E, s % E
                        if e == 0:
                            wait(pe, ys_ready[q], b)
                            pe.matmul(Y[q][:, :], bo1[:, :], WT8[:, q * HALF:(q + 1) * HALF], start=True, stop=False)
                        pe.wait_ge(gw_ready, b * S + s + 1)
                        pe.matmul(Y[q][:, :], Vo[:, e * P:(e + 1) * P], GW[:, s % 2, :], start=False, stop=(e == E - 1)
                                  ).then_inc(y_mm, 1)

                    def turn_y(b, q):
                        pe.wait_ge(ys_ready[q], b + 1)
                        for t in range(4):
                            i = pe.transpose(M[q][:, t * P:(t + 1) * P], YS[:, q, t * P:(t + 1) * P], ident[:, :])
                        i.then_inc(yt_ps[q], 1)

                    def batch(b, start):
                        for s in range(S):
                            first(b, s)
                            if s >= AGO:
                                third(b, s - AGO)
                            elif not start:
                                third(b - 1, S + s - AGO)
                            if s >= 1:
                                second(b, s - 1)
                            elif not start:
                                second(b - 1, S - 1)
                            if s == 5 and not start:
                                turn_y(b - 1, 1)
                            if s == 13:
                                turn_y(b, 0)

                    batch(0, True)
                    with pe.Fori(1, B) as b:
                        batch(b, False)
                    second(B - 1, S - 1)
                    for s in range(S - AGO, S):
                        third(B - 1, s)
                    turn_y(B - 1, 1)

                @block.scalar
                def _(act):
                    def relu1(b, s):
                        act.wait_ge(u1_ready, b * S + s + 1)
                        wait(act, u2_ready, b * S + s - 1)
                        e = s % E
                        nc.scalar.activation(H1[:, s % 2, :], U1[s % 2][:, :], ACT.Relu, bias=bn[:, E + e:E + e + 1],
                                             scale=bn[:, e:e + 1]).then_inc(h1_ready, 1)

                    def relu2(b, s):
                        act.wait_ge(u2_ready, b * S + s + 1)
                        wait(act, gw_ready, b * S + s - 1)
                        e = s % E
                        nc.scalar.activation(H2[:, s % 2, :], U2[s % 2][:, :], ACT.Relu, bias=bn[:, 3 * E + e:3 * E + e + 1],
                                             scale=bn[:, 2 * E + e:2 * E + e + 1]).then_inc(h2_ready, 1)

                    def copy_y(b, q):
                        act.wait_ge(y_mm, b * S + (q + 1) * E)
                        nc.scalar.copy(YS[:, q, :], Y[q][:, :]).then_inc(ys_ready[q], 1)

                    def batch(b, start):
                        for s in range(S):
                            relu1(b, s)
                            if s >= 1:
                                relu2(b, s - 1)
                            elif not start:
                                relu2(b - 1, S - 1)
                            if s == 3 and not start:
                                copy_y(b - 1, 1)
                            if s == 11:
                                copy_y(b, 0)

                    batch(0, True)
                    with act.Fori(1, B) as b:
                        batch(b, False)
                    relu2(B - 1, S - 1)
                    copy_y(B - 1, 1)

                @block.vector
                def _(dve):
                    def weight(b, s):
                        q, e = s // E, s % E
                        dve.wait_ge(h2_ready, b * S + s + 1)
                        wait(dve, y_mm, b * S + s - 1)
                        nc.vector.tensor_tensor(GW[:, s % 2, :], H2[:, s % 2, :], WBC[:, e, q * HALF:(q + 1) * HALF],
                                                ALU.mult).then_inc(gw_ready, 1)

                    def add(b, q):
                        dve.wait_ge(yt_ps[q], b + 1)
                        xb = X[:, bass.ds(b * N + q * HALF, HALF)]
                        nc.vector.tensor_tensor(xb, M[q][:, :], xb, ALU.add).then_inc(x_added[q], 1)

                    def batch(b, start):
                        for s in range(S):
                            weight(b, s)
                            if s == 5 and not start:
                                add(b - 1, 1)
                            if s == 13:
                                add(b, 0)

                    batch(0, True)
                    with dve.Fori(1, B) as b:
                        batch(b, False)
                    add(B - 1, 1)



_PARAMS = (["L0_gnn_W", "L0_gnn_a"] + [f"L0_ffn_{n}" for n in ("gamma", "beta", "Wr", "br", "W1", "b1", "W2", "b2")]
           + [f"L1_gnn_a{k}" for k in range(4)]
           + [f"L1_ffn_{n}" for n in ("Wr", "br", "W1", "b1", "g1", "be1", "m1", "v1", "W2", "b2", "g2", "be2", "m2", "v2",
                                      "Wo", "bo")])


def kernel(**inputs):
    import numpy as np
    import concourse.bacc as bacc
    from concourse.bass_utils import run_bass_kernel_spmd

    nc = bacc.Bacc("TRN2", target_bir_lowering=False, num_devices=1)
    arrays, given = {}, {}
    for name in ["x", "adj"] + _PARAMS:
        a = np.ascontiguousarray(inputs[name])
        arrays[f"in_{name}"] = a
        given[name] = nc.dram_tensor(f"in_{name}", a.shape, mybir.dt.from_np(a.dtype), kind="ExternalInput").ap()
    x, adj = given.pop("x"), given.pop("adj")
    out = nc.dram_tensor("out_x", x.shape, F32, kind="ExternalOutput").ap()
    program(nc, x, adj, given, out)
    return run_bass_kernel_spmd(nc, [arrays], core_ids=[0]).results[0]["out_x"]
```

```python
from contextlib import ExitStack

import concourse.bass as bass
from concourse import mybir

F32 = mybir.dt.float32
BF16 = mybir.dt.bfloat16
I32 = mybir.dt.int32
ALU = mybir.AluOpType
ACT = mybir.ActivationFunctionType
AX_X = mybir.AxisListType.X

P = 128
HALF = 512
SLOPE = 0.2
BLOCKED = -float(2 ** 55)
EPS = 1e-5
BN_EPS = 1e-3


class Count:

    def __init__(self):
        self.base, self.n = 0, 0

    def next(self):
        self.n += 1
        return self.base + self.n

    def now(self):
        return self.base + self.n

    def loop(self, turn, per):
        self.start, self.per = self.base + self.n, per
        self.base, self.n = self.start + turn * per, 0

    def end(self, turns):
        assert self.n == self.per, (self.n, self.per)
        self.base, self.n = self.start + turns * self.per, 0


def wait(eng, sem, value):
    if not isinstance(value, int) or value > 0:
        eng.wait_ge(sem, value)


def program(nc, x, adj, p, out):
    B, N, D = x.shape
    NT = N // P
    E = p["L0_ffn_W1"].shape[0]
    HID = p["L0_ffn_W1"].shape[2]
    HC = HID // P
    assert D == P and N == 2 * HALF and HID == 2 * P and E * HID == 2 * N and E * P == N and N == NT * P

    with ExitStack() as whole:
        sems = []

        def sem(name):
            sems.append(name)
            return whole.enter_context(nc.semaphore(name))

        def sb(name, shape, dt=F32, ctx=whole):
            return ctx.enter_context(nc.sbuf_tensor(name, shape, dt))

        X = sb("X", [P, B * N])
        ident = sb("ident", [P, P])
        identb = sb("identb", [P, P], BF16)
        blockI = sb("blockI", [P, P], BF16)
        ones3 = sb("ones3", [3, P], BF16)
        pick = sb("pick", [3 * E, E * P], BF16)
        minus_half = sb("minus_half", [P, B * NT])
        eps_all = sb("eps_all", [P, B * NT])
        half8, eps8 = minus_half[:, 0:NT], eps_all[:, 0:NT]
        order = sb("order", [P, E])
        Wg = sb("Wg", [P, P])
        WgT = sb("WgT", [P, 2])
        W1 = sb("W1", [P, E * HID])
        W2 = sb("W2", [P, E * HC * P])
        Wr0 = sb("Wr0", [P, E])
        br0 = sb("br0", [P, E])
        b20 = sb("b20", [P, E * P])
        V1 = sb("V1", [P, E * P])
        V2 = sb("V2", [P, E * P])
        Vo = sb("Vo", [P, E * P])
        Wr1 = sb("Wr1", [P, E])
        br1 = sb("br1", [P, E])
        bo1 = sb("bo1", [E, P])
        names = ([("L0_ffn_b1", E * HC), ("L0_ffn_gamma", 1), ("L0_ffn_beta", 1)]
                 + [(f"L1_gnn_a{k}", 1) for k in range(4)]
                 + [(f"L1_ffn_{n}", E) for n in ("b1", "g1", "be1", "m1", "v1", "b2", "g2", "be2", "m2", "v2")])
        at, R = {}, 0
        for n, rows in names:
            at[n] = R
            R += rows
        prow = sb("prow", [R, P])
        pcol = sb("pcol", [P, R])
        bn = sb("bn", [P, 4 * E])

        MEAN, SPREAD, ROOT = (sb(n, [P, B * NT]) for n in ("MEAN", "SPREAD", "ROOT"))

        flag = sb("flag", [1, 1], I32)
        ones_or_more = sb("ones_or_more", [P, N])
        excess = sb("excess", [P, B * NT // 2])
        minus1 = sb("minus1", [P, 1])
        held = sem("held")
        x_first, x_second, x_rest, par_loaded = sem("x_first"), sem("x_second"), sem("x_rest"), sem("par_loaded")
        adj_loaded = [sem(f"adj_loaded{i}") for i in range(4)]

        loads = [(W1[:, :].rearrange("d (e h) -> d e h", e=E), p["L0_ffn_W1"].rearrange("e d h -> d e h")),
                 (W2[:, :].rearrange("h (e c d) -> h e c d", e=E, c=HC),
                  p["L0_ffn_W2"].rearrange("e (c h) d -> h e c d", c=HC)),
                 (Wr0[:, :], p["L0_ffn_Wr"]),
                 (br0[:, :], p["L0_ffn_br"].rearrange("(o e) -> o e", o=1).to_broadcast([P, E])),
                 (b20[:, :], p["L0_ffn_b2"].rearrange("(o e) d -> o (e d)", o=1).to_broadcast([P, E * P])),
                 (V1[:, :].rearrange("d (e h) -> d e h", e=E), p["L1_ffn_W1"].rearrange("e d h -> d e h")),
                 (V2[:, :].rearrange("d (e h) -> d e h", e=E), p["L1_ffn_W2"].rearrange("e d h -> d e h")),
                 (Vo[:, :].rearrange("d (e h) -> d e h", e=E), p["L1_ffn_Wo"].rearrange("e d h -> d e h")),
                 (Wr1[:, :], p["L1_ffn_Wr"]),
                 (br1[:, :], p["L1_ffn_br"].rearrange("(o e) -> o e", o=1).to_broadcast([P, E])),
                 (bo1[:, :], p["L1_ffn_bo"])]
        for n, k in names:
            src = p[n]
            if n == "L0_ffn_b1":
                src = src.rearrange("e (c h) -> (e c) h", h=P)
            elif k == 1:
                src = src.rearrange("(o h) -> o h", o=1)
            loads.append((prow[at[n]:at[n] + k, :], src))

        with ExitStack() as ctx:
            A12 = sb("A12", [P, 2 * P], ctx=ctx)
            junk = sb("junk", [P, P], ctx=ctx)
            gat_loaded, cstep = sem("gat_loaded"), sem("const_step")
            block = ctx.enter_context(nc.Block())

            @block.sync
            def _(sp):
                sp.dma_start(X[:, 0:N].rearrange("p (t d) -> p t d", t=NT),
                             x[0].rearrange("(t p) d -> p t d", p=P)).then_inc(x_first, 16)
                sp.dma_start(Wg[:, :], p["L0_gnn_W"]).then_inc(gat_loaded, 16)
                sp.dma_start(A12[:, :], p["L0_gnn_a"].rearrange("k o -> o k").to_broadcast([P, 2 * P])
                             ).then_inc(gat_loaded, 16)

            @block.gpsimd
            def _(pool):
                c = Count()
                for tile, value in ((ident, 0.0), (identb, 0.0), (blockI, 0.0), (pick, 0.0), (ones3, 1.0), (minus_half, -0.5), (eps_all, EPS), (minus1, -1.0), (ones_or_more, 0.0),
                                    *((order[:, e:e + 1], float(E - e)) for e in range(E))):
                    nc.gpsimd.memset(tile[:, :], value).then_inc(cstep, 1)
                    c.next()
                pool.wait_ge(cstep, c.now())
                for tile, fill in ((ident, 1.0), (identb, 1.0), (blockI, BLOCKED)):
                    nc.gpsimd.affine_select(out=tile[:, :], in_=tile[:, :], compare_op=ALU.not_equal, fill=fill,
                                            base=0, pattern=[[-1, P]], channel_multiplier=1).then_inc(cstep, 1)
                    c.next()
                v = pick[:, :].rearrange("r (e m) -> r e m", e=E)
                for k in range(3):
                    nc.gpsimd.affine_select(out=v, in_=v, compare_op=ALU.not_equal, fill=1.0, base=-k * E,
                                            pattern=[[-1, E], [0, P]], channel_multiplier=1).then_inc(cstep, 1)
                    pool.wait_ge(cstep, c.next())

            @block.vector
            def _(dve):
                dve.wait_ge(gat_loaded, 32)
                for k in range(2):
                    nc.vector.tensor_tensor_reduce(junk[:, :], Wg[:, :], A12[:, k * P:(k + 1) * P], 1.0, 0.0, ALU.mult,
                                                   ALU.add, WgT[:, k:k + 1]).then_inc(gat_loaded, 1)
                    dve.wait_ge(gat_loaded, 33 + k)

        def hold(eng, s, value):
            eng.wait_ge(s, value)
            eng.sem_inc(held, 1)

        def ln_stats(dve, b, ST, MV, stepsem, step, mv_ready):
            for t in range(NT):
                i = nc.vector.bn_stats(ST[:, t, :], X[:, bass.ds(b * N + t * P, P)])
            i.then_inc(stepsem, 1)
            hold(dve, stepsem, step.next())
            for t in range(NT):
                i = nc.vector.bn_aggr(MV[:, t, :], ST[:, t, :])
            i.then_inc(mv_ready, 1)

        def ln_root(pool, b, MV, RS, stepsem, step, mv_ready, rs_ready, twice):
            pool.wait_ge(mv_ready, b + 1)
            var = MV[:, :, 1]

            def op(*a):
                nc.gpsimd.tensor_tensor(*a).then_inc(stepsem, 1)
                pool.wait_ge(stepsem, step.next())
            op(RS[:, 0, :], var, eps8, ALU.add)
            if not twice:
                nc.gpsimd.tensor_tensor(RS[:, 1, :], RS[:, 0, :], half8, ALU.pow).then_inc(rs_ready, 1)
                return
            op(RS[:, 1, :], RS[:, 0, :], half8, ALU.pow)
            op(RS[:, 2, :], RS[:, 1, :], RS[:, 1, :], ALU.mult)
            op(RS[:, 3, :], RS[:, 2, :], var, ALU.mult)
            op(RS[:, 4, :], RS[:, 3, :], eps8, ALU.add)
            op(RS[:, 5, :], RS[:, 4, :], half8, ALU.pow)
            nc.gpsimd.tensor_tensor(RS[:, 6, :], RS[:, 5, :], RS[:, 1, :], ALU.mult).then_inc(rs_ready, 1)

        def ln_apply(dve, b, MV, rs, XN, xn_at, rs_ready, xn_ready):
            dve.wait_ge(rs_ready, b + 1)
            for t in range(NT):
                i = nc.vector.tensor_scalar(XN[:, bass.ds(xn_at + t * P, P)], X[:, bass.ds(b * N + t * P, P)],
                                            MV[:, t, 0:1], rs[:, t:t + 1], ALU.subtract, ALU.mult)
            i.then_inc(xn_ready, 1)

        with ExitStack() as ctx:
            def tile(name, shape, dt=F32):
                return sb(name, shape, dt, ctx)

            ADJ = tile("ADJ", [P, 4, N], I32)
            NM = tile("NM", [P, 2 * NT * N], BF16)
            ST, MV, RS = tile("ST", [P, NT, 6]), tile("MV", [P, NT, 2]), tile("RS", [P, 7, NT])
            XN, XNT = tile("XN", [P, N]), tile("XNT", [P, N])
            H = tile("H", [P, 2 * N])
            F2 = tile("F2", [P, 2 * NT])
            F3 = tile("F3", [P, NT, 3], BF16)
            FR = tile("FR", [P, NT])
            F1R = tile("F1R", [3, 2 * N], BF16)
            R4, Y, PR = tile("R4", [P, 2, N]), tile("Y", [P, 2, N]), tile("PR", [P, 2, N])
            MX, NMX, Z, RZ = tile("MX", [P, NT]), tile("NMX", [P, NT]), tile("Z", [P, NT]), tile("RZ", [P, NT])
            HS = tile("HS", [P, 2, P])
            RO, EX, EL = tile("RO", [P, N]), tile("EX", [P, N]), tile("EL", [P, N])
            T = [ctx.enter_context(nc.psum_tensor(f"T{i}", [P, N], F32)) for i in range(2)]
            O = ctx.enter_context(nc.psum_tensor("O", [P, N], F32))
            M = [ctx.enter_context(nc.psum_tensor(f"M{i}", [P, HALF], F32)) for i in range(2)]
            F1T = M[1][:, :].bitcast(BF16)

            mv_ready, rs_ready, xn_ready, dstep, pstep = (sem("a_" + n) for n in (
                "mv_ready", "rs_ready", "xn_ready", "dve_step", "pool_step"))
            xnt_ps, xnt_ready, h_ps, h_ready, elt_ps, x_added = ([sem(f"a_{n}{h}") for h in range(2)] for n in (
                "xnt_ps", "xnt_ready", "h_ps", "h_ready", "elt_ps", "x_added"))
            f12_ps, f2_ready, f1t_ps, f1r_ready, nm_ready, t_ready, r4_ready, y_ready, shift_ready, pr_ready = (
                sem("a_" + n) for n in ("f12_ps", "f2_ready", "f1t_ps", "f1r_ready", "nm_ready", "t_ready", "r4_ready",
                                        "y_ready", "shift_ready", "pr_ready"))
            MVN = tile("MVN", [P, NT, 2])
            spread_ready = sem("a_spread_ready")
            CL = tile("CL", [P, 2, N])
            seen = tile("seen", [P, N], BF16)
            pool_looked, act_looked, added = sem("a_pool_looked"), sem("a_act_looked"), sem("a_added")
            hs_ready, pv_done, ro_ready, ex_ready, el_ready = (sem("a_" + n) for n in (
                "hs_ready", "pv_done", "ro_ready", "ex_ready", "el_ready"))
            LAST = B - 1
            block = ctx.enter_context(nc.Block())

            @block.sync
            def _(sp):
                def load(b):
                    for t in range(NT):
                        if not isinstance(b, int) or b * NT + t > 3:
                            hold(sp, nm_ready, b * NT + t - 3)
                        if t >= 4:
                            hold(sp, pool_looked, b * 4 + t - 3)
                        elif not isinstance(b, int) or b > 0:
                            hold(sp, act_looked, (b - 1) * 4 + t + 1)
                        sp.dma_start(ADJ[:, t % 4, :], adj[bass.ds(b, 1), t * P:(t + 1) * P, :].rearrange("o p i -> (o p) i")
                                     ).then_inc(adj_loaded[t % 4], 16)
                def load_x(b, loaded):
                    sp.dma_start(X[:, b * N:(b + 1) * N].rearrange("p (t d) -> p t d", t=NT),
                                 x[b].rearrange("(t p) d -> p t d", p=P)).then_inc(loaded, 16)

                load(0)
                load_x(1, x_second)
                load(1)
                for b in range(2, B):
                    load_x(b, x_rest)
                for dst, src in loads:
                    sp.dma_start(dst, src).then_inc(par_loaded, 16)
                with sp.Fori(2, B) as b:
                    load(b)

            @block.gpsimd
            def _(pool):
                step = Count()

                def look(b, t):
                    pool.wait_ge(adj_loaded[t], 16 * (b * (NT // 4) + 1))
                    if not isinstance(b, int) or b * 4 + t > 1:
                        hold(pool, added, b * 4 + t - 1)
                    nc.gpsimd.tensor_scalar(CL[:, t % 2, :], ADJ[:, t, :], 1048576.0, 1.0, ALU.min, ALU.max
                                            ).then_inc(pool_looked, 1)
                    pool.wait_ge(pool_looked, b * 4 + t + 1)
                    wait(pool, added, b * 4 + t)
                    nc.gpsimd.tensor_tensor(ones_or_more[:, :], ones_or_more[:, :], CL[:, t % 2, :], ALU.add
                                            ).then_inc(added, 1)

                def batch(b):
                    ln_root(pool, b, MV, RS, pstep, step, mv_ready, rs_ready, False)
                    for t in range(4):
                        look(b, t)

                def root_next(b):
                    pool.wait_ge(spread_ready, b + 1)
                    nc.gpsimd.tensor_tensor(ROOT[:, bass.ds(b * NT, NT)], SPREAD[:, bass.ds(b * NT, NT)], half8, ALU.pow)

                for b in range(3):
                    batch(b)
                with pool.Fori(3, B) as b:
                    step.loop(b - 3, 1)
                    root_next(b - 3)
                    batch(b)
                step.end(B - 3)
                for b in range(B - 3, B):
                    root_next(b)

            @block.tensor
            def _(pe):
                def turn_x(b, h):
                    pe.wait_ge(xn_ready, b + 1)
                    for t in range(4):
                        i = pe.transpose(M[h][:, t * P:(t + 1) * P], XN[:, bass.ts(4 * h + t, P)], ident[:, :])
                    i.then_inc(xnt_ps[h], 1)

                def project(b, h):
                    pe.wait_ge(xnt_ready[h], b + 1)
                    for t in range(4):
                        i = pe.matmul(M[h][:, t * P:(t + 1) * P], XNT[:, bass.ts(4 * h + t, P)], Wg[:, :], start=True, stop=True)
                    i.then_inc(h_ps[h], 1)

                def scores(b):
                    pe.wait_ge(h_ready[0], b + 1)
                    for t in range(NT):
                        i = pe.matmul(M[0][:, 2 * t:2 * t + 2], XNT[:, t * P:(t + 1) * P], WgT[:, :], start=True, stop=True)
                    i.then_inc(f12_ps, 1)

                def turn_f1(b):
                    pe.wait_ge(f2_ready, b + 1)
                    pe.wait_ge(h_ready[1], b + 1)
                    for t in range(NT):
                        i = pe.transpose(F1T[0:3, t * P:(t + 1) * P], F3[:, t, :], identb[:, :])
                    i.then_inc(f1t_ps, 1)

                def turn_el(b, h, used):
                    pe.wait_ge(el_ready, b + 1)
                    pe.wait_ge((f2_ready, f1r_ready)[h], used)
                    for t in range(4):
                        i = pe.transpose(M[h][:, t * P:(t + 1) * P], EL[:, bass.ts(4 * h + t, P)], ident[:, :])
                    i.then_inc(elt_ps[h], 1)

                def logits(b, c):
                    if c == 0:
                        hold(pe, f1r_ready, b + 1)
                        pe.wait_ge(nm_ready, b * NT + NT)
                    wait(pe, y_ready, b * NT + c - 1)
                    t = T[c % 2]
                    for h in range(2):
                        for r in range(4 * h, 4 * h + 4):
                            pe.matmul(t[:, r * P:(r + 1) * P], NM[:, bass.ds((b % 2) * NT * N + r * N + c * P, P)],
                                      blockI[:, :], start=(r % 4 == 0), stop=False)
                        i = pe.matmul(t[:, h * HALF:(h + 1) * HALF], ones3[:, :],
                                      F1R[:, bass.ds((b % 2) * N + h * HALF, HALF)], start=False, stop=True)
                    i.then_inc(t_ready, 1)

                def attend(b, c):
                    pe.wait_ge(hs_ready, b * NT + c + 1)
                    if c == 0:
                        wait(pe, ex_ready, b)
                    for h in range(2):
                        i = pe.matmul(O[:, h * HALF:(h + 1) * HALF], HS[:, c % 2, :], PR[:, c % 2, h * HALF:(h + 1) * HALF],
                                      start=(c == 0), stop=(c == NT - 1))
                    i.then_inc(pv_done, 1)

                def batch(b, first, last):
                    for c in range(NT):
                        logits(b, c)
                        if c >= 2:
                            attend(b, c - 2)
                        elif not first:
                            attend(b - 1, NT - 2 + c)
                        if not last:
                            if c in (2, 3):
                                turn_x(b + 1, c - 2)
                            if c in (4, 5):
                                project(b + 1, c - 4)
                            if c == 5:
                                scores(b + 1)
                            if c == 6:
                                turn_f1(b + 1)
                        if c == 7 and not first:
                            turn_el(b - 1, 0, b + 1 if last else b + 2)
                            turn_el(b - 1, 1, b + 1 if last else b + 2)

                for h in range(2):
                    turn_x(0, h)
                for h in range(2):
                    project(0, h)
                scores(0)
                turn_f1(0)
                batch(0, True, False)
                with pe.Fori(1, LAST) as b:
                    batch(b, False, False)
                batch(LAST, False, True)
                attend(LAST, NT - 2)
                attend(LAST, NT - 1)
                for h in range(2):
                    pe.wait_ge(x_added[h], LAST)
                    turn_el(LAST, h, B)

            @block.scalar
            def _(act):
                def copy_xnt(b, h):
                    act.wait_ge(xnt_ps[h], b + 1)
                    wait(act, f12_ps, b)
                    nc.scalar.copy(XNT[:, h * HALF:(h + 1) * HALF], M[h][:, :]).then_inc(xnt_ready[h], 1)

                def copy_h(b, h):
                    act.wait_ge(h_ps[h], b + 1)
                    wait(act, hs_ready, (b - 1) * NT)
                    nc.scalar.copy(H[:, bass.ds((b % 2) * N + h * HALF, HALF)], M[h][:, :]).then_inc(h_ready[h], 1)

                def relu(b, c):
                    act.wait_ge(t_ready, b * NT + c + 1)
                    if c == 0:
                        act.wait_ge(f2_ready, b + 1)
                    wait(act, y_ready, b * NT + c - 1)
                    nc.scalar.activation(R4[:, c % 2, :], T[c % 2][:, :], ACT.Relu, bias=F2[:, bass.ds((b % 2) * NT + c, 1)],
                                         scale=4.0).then_inc(r4_ready, 1)

                def prob(b, c):
                    act.wait_ge(shift_ready, b * NT + c + 1)
                    wait(act, pv_done, b * NT + c - 1)
                    nc.scalar.activation(PR[:, c % 2, :], Y[:, c % 2, :], ACT.Exp, bias=NMX[:, c:c + 1], scale=SLOPE,
                                         accum_out=Z[:, c:c + 1]).then_inc(pr_ready, 1)

                def look(b, t):
                    act.wait_ge(adj_loaded[t % 4], 16 * (b * (NT // 4) + 2))
                    wait(act, act_looked, b * 4 + t - 4)
                    nc.scalar.activation(seen[:, :], ADJ[:, t % 4, :], ACT.Relu, bias=minus1[:, :],
                                         accum_out=excess[:, bass.ds(b * 4 + t - 4, 1)]).then_inc(act_looked, 1)

                def outputs(b):
                    act.wait_ge(pv_done, b * NT + NT)
                    nc.scalar.activation(RO[:, :], O[:, :], ACT.Relu).then_inc(ro_ready, 1)
                    nc.scalar.activation(EX[:, :], O[:, :], ACT.Exp).then_inc(ex_ready, 1)

                def batch(b, first, last):
                    for c in range(NT):
                        relu(b, c)
                        if c > 0:
                            prob(b, c - 1)
                        elif not first:
                            prob(b - 1, NT - 1)
                        if c == 1 and not first:
                            outputs(b - 1)
                        if not last:
                            if c in (2, 3):
                                copy_xnt(b + 1, c - 2)
                            if c in (4, 5):
                                copy_h(b + 1, c - 4)
                            if c >= 4:
                                look(b + 1, c)

                for h in range(2):
                    copy_xnt(0, h)
                for h in range(2):
                    copy_h(0, h)
                for t in range(4, NT):
                    look(0, t)
                batch(0, True, False)
                with act.Fori(1, LAST) as b:
                    batch(b, False, False)
                batch(LAST, False, True)
                prob(LAST, NT - 1)
                outputs(LAST)

            @block.vector
            def _(dve):
                step = Count()

                def convert(b, t):
                    dve.wait_ge(adj_loaded[t % 4], 16 * (b * (NT // 4) + t // 4 + 1))
                    if t == 0:
                        wait(dve, t_ready, (b - 1) * NT)
                    nc.vector.tensor_scalar(NM[:, bass.ds((b % 2) * NT * N + t * N, N)], ADJ[:, t % 4, :], 0.0, None,
                                            ALU.is_le).then_inc(nm_ready, 1)

                def parts(b):
                    dve.wait_ge(f12_ps, b + 1)
                    wait(dve, f1t_ps, b)
                    v = M[0][:, 0:2 * NT].rearrange("p (t k) -> p t k", k=2)
                    nc.vector.tensor_copy(F3[:, :, 0], v[:, :, 0]).then_inc(dstep, 1)
                    dve.wait_ge(dstep, step.next())
                    nc.vector.tensor_tensor(FR[:, :], v[:, :, 0], F3[:, :, 0], ALU.subtract).then_inc(dstep, 1)
                    dve.wait_ge(dstep, step.next())
                    nc.vector.tensor_copy(F3[:, :, 1], FR[:, :]).then_inc(dstep, 1)
                    dve.wait_ge(dstep, step.next())
                    nc.vector.tensor_tensor(F3[:, :, 2], FR[:, :], F3[:, :, 1], ALU.subtract)
                    wait(dve, r4_ready, (b - 1) * NT)
                    nc.vector.tensor_scalar(F2[:, bass.ds((b % 2) * NT, NT)], v[:, :, 1], 4.0, None, ALU.mult).then_inc(f2_ready, 1)

                def copy_f1(b):
                    dve.wait_ge(f1t_ps, b + 1)
                    wait(dve, t_ready, (b - 1) * NT)
                    nc.vector.tensor_copy(F1R[:, bass.ds((b % 2) * N, N)], F1T[0:3, 0:N]).then_inc(f1r_ready, 1)

                def shift(b, c):
                    if not isinstance(b, int) or b * NT + c > 1:
                        hold(dve, pr_ready, b * NT + c - 1)
                    hold(dve, r4_ready, b * NT + c + 1)
                    nc.vector.tensor_tensor_reduce(Y[:, c % 2, :], T[c % 2][:, :], R4[:, c % 2, :], 1.0, -3.0e38, ALU.add,
                                                   ALU.max, MX[:, c:c + 1]).then_inc(y_ready, 1)
                    dve.wait_ge(y_ready, b * NT + c + 1)
                    nc.vector.tensor_scalar(NMX[:, c:c + 1], MX[:, c:c + 1], -SLOPE, None, ALU.mult).then_inc(shift_ready, 1)

                def share(b, c):
                    dve.wait_ge(pr_ready, b * NT + c + 1)
                    nc.vector.reciprocal(RZ[:, c:c + 1], Z[:, c:c + 1]).then_inc(dstep, 1)
                    dve.wait_ge(dstep, step.next())
                    if c == 0:
                        dve.wait_ge(h_ready[1], b + 1)
                    wait(dve, pv_done, b * NT + c - 1)
                    nc.vector.tensor_scalar(HS[:, c % 2, :], H[:, bass.ds((b % 2) * N + c * P, P)], RZ[:, c:c + 1], None,
                                            ALU.mult).then_inc(hs_ready, 1)

                def elu(b):
                    dve.wait_ge(ex_ready, b + 1)
                    nc.vector.scalar_tensor_tensor(out=EL[:, :], in0=EX[:, :], scalar=1.0, in1=RO[:, :], op0=ALU.min,
                                                   op1=ALU.add).then_inc(el_ready, 1)

                def add(b):
                    for h in range(2):
                        dve.wait_ge(elt_ps[h], b + 1)
                        xb = X[:, bass.ds(b * N + h * HALF, HALF)]
                        nc.vector.scalar_tensor_tensor(out=xb, in0=M[h][:, :], scalar=-1.0, in1=xb, op0=ALU.add,
                                                       op1=ALU.add).then_inc(x_added[h], 1)

                def stats(b):
                    ln_stats(dve, b, ST, MV, dstep, step, mv_ready)

                def norm(b):
                    if not isinstance(b, int) or b > 0:
                        dve.wait_ge(xnt_ps[1], b)
                    ln_apply(dve, b, MV, RS[:, 1, :], XN, 0, rs_ready, xn_ready)

                def stats_next(b):
                    for h in range(2):
                        hold(dve, x_added[h], b + 1)
                    for t in range(NT):
                        i = nc.vector.bn_stats(ST[:, t, :], X[:, bass.ds(b * N + t * P, P)])
                    i.then_inc(dstep, 1)
                    hold(dve, dstep, step.next())
                    for t in range(NT):
                        i = nc.vector.bn_aggr(MVN[:, t, :], ST[:, t, :])
                    i.then_inc(dstep, 1)
                    hold(dve, dstep, step.next())
                    nc.vector.tensor_copy(MEAN[:, bass.ds(b * NT, NT)], MVN[:, :, 0])
                    nc.vector.tensor_scalar(SPREAD[:, bass.ds(b * NT, NT)], MVN[:, :, 1], 1.0 + EPS, EPS * EPS, ALU.mult, ALU.add
                                            ).then_inc(spread_ready, 1)

                def batch(b, first, last):
                    for c in range(NT):
                        if not last and c == 6:
                            parts(b + 1)
                        if not last and c == 7:
                            copy_f1(b + 1)
                        shift(b, c)
                        if c > 0:
                            share(b, c - 1)
                        elif not first:
                            share(b - 1, NT - 1)
                        if c == 2 and not first:
                            elu(b - 1)
                        if not last:
                            convert(b + 1, c)
                            if c == 0:
                                stats(b + 1)
                            if c == 1:
                                norm(b + 1)
                    if not first:
                        add(b - 1)
                        stats_next(b - 1)

                dve.wait_ge(x_first, 16)
                stats(0)
                norm(0)
                for t in range(4):
                    convert(0, t)
                parts(0)
                copy_f1(0)
                for t in range(4, NT):
                    convert(0, t)
                dve.wait_ge(x_second, 16)
                batch(0, True, False)
                dve.wait_ge(x_rest, 16 * (B - 2))
                with dve.Fori(1, LAST) as b:
                    step.loop(b - 1, 14)
                    batch(b, False, False)
                step.end(LAST - 1)
                batch(LAST, False, True)
                share(LAST, NT - 1)
                elu(LAST)
                add(LAST)
                stats_next(LAST)

        CHOSEN, SHARE, ROW = (sb(n, [P, B * 2 * NT]) for n in ("CHOSEN", "SHARE", "ROW"))
        ROW_I = sb("ROW_I", [P, B * 2 * NT], I32)
        NB = 2 * B * N // HALF + E - 1
        FROM, EXPERT = (sb(n, [1, NB], I32) for n in ("FROM", "EXPERT"))

        with ExitStack() as ctx:
            var, half, diff, prod = (sb(n, [P, 2 * E], ctx=ctx) for n in ("bn_var", "bn_half", "bn_diff", "bn_prod"))
            ps = ctx.enter_context(nc.psum_tensor("ps_par", [P, HALF], F32))
            lcol, lone, most = sb("lcol", [P, 1], ctx=ctx), sb("lone", [1, 1], ctx=ctx), sb("most", [P, 2], ctx=ctx)
            lcol_ready, lrow_ps = sem("lcol_ready"), sem("lrow_ps")
            pl = ctx.enter_context(nc.psum_tensor("ps_largest", [1, HALF], F32))
            pcol_ps, var_ready, root_ready, qstep = sem("pcol_ps"), sem("var_ready"), sem("root_ready"), sem("par_step")
            block = ctx.enter_context(nc.Block())

            @block.tensor
            def _(pe):
                pe.wait_ge(par_loaded, 16 * len(loads))
                pe.transpose(ps[:, 0:R], prow[:, :], ident[0:R, 0:R]).then_inc(pcol_ps, 1)
                pe.wait_ge(lcol_ready, 1)
                pe.transpose(pl[:, 0:P], lcol[:, :], ident[:, :]).then_inc(lrow_ps, 1)

            @block.gpsimd
            def _(pool):
                nc.gpsimd.memset(half[:, :], -0.5).then_inc(root_ready, 1)
                pool.wait_ge(root_ready, 1)
                pool.wait_ge(var_ready, 2)
                nc.gpsimd.tensor_tensor(var[:, :], var[:, :], half[:, :], ALU.pow).then_inc(root_ready, 1)

            @block.vector
            def _(dve):
                c = Count()
                nc.vector.tensor_reduce(most[:, 0:1], ones_or_more[:, :], AX_X, ALU.max).then_inc(qstep, 1)
                nc.vector.tensor_reduce(most[:, 1:2], excess[:, :], AX_X, ALU.max).then_inc(qstep, 1)
                c.next()
                dve.wait_ge(qstep, c.next())
                nc.vector.scalar_tensor_tensor(out=lcol[:, :], in0=most[:, 0:1], scalar=-float(B * NT // 2), in1=most[:, 1:2],
                                               op0=ALU.add, op1=ALU.max).then_inc(lcol_ready, 1)
                dve.wait_ge(pcol_ps, 1)
                nc.vector.tensor_copy(pcol[:, :], ps[:, 0:R]).then_inc(qstep, 1)
                dve.wait_ge(qstep, c.next())

                def col(n):
                    return pcol[:, at[f"L1_ffn_{n}"]:at[f"L1_ffn_{n}"] + E]

                for k in range(2):
                    nc.vector.tensor_scalar(var[:, k * E:(k + 1) * E], col(f"v{k + 1}"), BN_EPS, None, ALU.add
                                            ).then_inc(var_ready, 1)
                dve.wait_ge(lrow_ps, 1)
                nc.vector.tensor_reduce(lone[:, :], pl[:, 0:P], AX_X, ALU.max).then_inc(qstep, 1)
                dve.wait_ge(qstep, c.next())
                nc.vector.tensor_scalar(flag[:, :], lone[:, :], 0.0, None, ALU.is_gt)
                dve.wait_ge(root_ready, 2)
                for k in range(2):
                    u, w = diff[:, k * E:(k + 1) * E], prod[:, k * E:(k + 1) * E]
                    s, t = bn[:, 2 * k * E:(2 * k + 1) * E], bn[:, (2 * k + 1) * E:(2 * k + 2) * E]
                    nc.vector.tensor_tensor(s, col(f"g{k + 1}"), var[:, k * E:(k + 1) * E], ALU.mult).then_inc(qstep, 1)
                    nc.vector.tensor_tensor(u, col(f"b{k + 1}"), col(f"m{k + 1}"), ALU.subtract).then_inc(qstep, 1)
                    c.next()
                    dve.wait_ge(qstep, c.next())
                    nc.vector.tensor_tensor(w, u, s, ALU.mult).then_inc(qstep, 1)
                    dve.wait_ge(qstep, c.next())
                    nc.vector.tensor_tensor(t, w, col(f"be{k + 1}"), ALU.add)

        BLOCK = HALF
        SEATS = B * N + BLOCK
        SPARE = E * SEATS
        sorted_x = nc.dram_tensor("sorted_x", [E * SEATS + BLOCK, P], F32).ap()
        sorted_y = nc.dram_tensor("sorted_y", [NB * BLOCK, P], F32).ap()
        assert P % E == 0 and P // E * BLOCK >= B * N
        PER = P // E
        with ExitStack() as ctx:
            def tile(name, shape, dt=F32):
                return sb(name, shape, dt, ctx)

            XN = tile("bXN", [P, 2, N])
            XT = tile("bXT", [P, N])
            LG, Q, OH1, OH2, L2, SEAT = (tile(n, [P, NT, E]) for n in ("LG", "Q", "OH1", "OH2", "L2", "SEAT"))
            m1, m2, k1, dd, ex, s1 = (tile(n, [P, NT]) for n in ("m1", "m2", "k1", "dd", "ex", "s1"))
            CH = tile("CH", [P, NT + 1, E], BF16)
            NEXT = tile("NEXT", [P, E])
            AT = tile("AT", [P, 2, NT])
            AT_I = [tile(f"AT_I{q}", [P, 2 * NT], I32) for q in range(2)]
            before, ones = tile("before", [P, P], BF16), tile("ones", [P, P], BF16)
            zero = tile("zero", [P, BLOCK])
            mine, upto = tile("mine", [P, E]), tile("upto", [P, E])
            ip, ik = tile("ip", [P, 1], I32), tile("ik", [P, NB], I32)
            rowno, kth, hot = tile("rowno", [P, 1]), tile("kth", [P, NB]), tile("hot", [P, NB])
            pf, ef, used, got, rel = (tile(n, [P, 1]) for n in ("pf", "ef", "used", "got", "rel"))
            ubf, below = tile("ubf", [P, 1], BF16), tile("below", [P, E], BF16)
            pick8, shift8 = tile("pick8", [P, E]), tile("shift8", [P, E])
            tail = tile("tail", [1, E], I32)
            TMP = tile("TMP", [P, B * 2 * NT])
            M = [ctx.enter_context(nc.psum_tensor(f"bM{i}", [P, HALF], F32)) for i in range(2)]
            L, RK, TB, TC = (ctx.enter_context(nc.psum_tensor(n, [P, HALF], F32)) for n in ("bL", "bRK", "bTB", "bTC"))
            (xn_ready, xt_ps, xt_ready, lg_ps, dd_ready, ex_ready, ch_ready, rk_ps, at_ready, dstep, istep, masks,
             used_ready, rank_ps, hot_ready, table_ps, tail_ready, tails, zero_ready,
             before_ready) = (sem("b_" + n) for n in (
                 "xn_ready", "xt_ps", "xt_ready", "lg_ps", "dd_ready", "ex_ready", "ch_ready", "rk_ps", "at_ready",
                 "dve_step", "pool_step", "masks", "used_ready", "rank_ps", "hot_ready", "table_ps", "tail_ready", "tails",
                 "zero_ready", "before_ready"))
            sent = [sem(f"b_sent{q}") for q in range(2)]
            block = ctx.enter_context(nc.Block())
            EACH = 16 * 2 * NT

            @block.sync
            def _(sp):
                sp.wait_ge(zero_ready, 1)
                v = zero[:, :].rearrange("p (t d) -> p t d", d=P)
                sp.dma_start(sorted_x[SPARE:SPARE + BLOCK, :].rearrange("(p t) d -> p t d", p=P), v).then_inc(tails, 16)
                sp.wait_ge(tail_ready, 1)
                for e in range(E):
                    row = sp.value_load(tail[0:1, e:e + 1], min_val=e * SEATS, max_val=e * SEATS + B * N)
                    sp.dma_start(sorted_x[bass.ds(row, BLOCK), :].rearrange("(p t) d -> p t d", p=P), v).then_inc(tails, 16)
                sp.wait_ge(tails, 16 * (E + 1))

            @block.gpsimd
            def _(pool):
                step = Count()

                def op(f, *a, **k):
                    f(*a, **k).then_inc(istep, 1)
                    pool.wait_ge(istep, step.next())

                g = nc.gpsimd
                g.memset(zero[:, :], 0.0).then_inc(zero_ready, 1)
                op(g.memset, ones[:, :], 1.0)
                g.affine_select(out=before[:, :], in_=ones[:, :], compare_op=ALU.is_gt, fill=0.0, base=0,
                                pattern=[[1, P]], channel_multiplier=-1).then_inc(before_ready, 1)
                op(g.memset, mine[:, :], 1.0)
                op(g.affine_select, out=upto[:, :], in_=mine[:, :], compare_op=ALU.is_ge, fill=0.0, base=-1,
                   pattern=[[PER, E]], channel_multiplier=-1)
                op(g.affine_select, out=mine[:, :], in_=mine[:, :], compare_op=ALU.is_ge, fill=0.0, base=0,
                   pattern=[[-PER, E]], channel_multiplier=1)
                op(g.affine_select, out=mine[:, :], in_=mine[:, :], compare_op=ALU.is_ge, fill=0.0, base=PER - 1,
                   pattern=[[PER, E]], channel_multiplier=-1)
                op(g.iota, ip[:, :], [[0, 1]], base=0, channel_multiplier=1)
                op(g.iota, ik[:, :], [[1, NB]], base=0, channel_multiplier=0)
                g.tensor_copy(pf[:, :], ip[:, :]).then_inc(masks, 1)
                g.tensor_copy(kth[:, :], ik[:, :]).then_inc(masks, 1)

                def send(i, q):
                    hold(pool, at_ready, 2 * i + q + 1)
                    for k in range(2):
                        for t in range(NT):
                            nc.gpsimd.indirect_dma_start(
                                sorted_x, bass.IndirectOffsetOnAxis(ap=AT_I[q][:, k * NT + t:k * NT + t + 1], axis=0),
                                XN[:, q, t * P:(t + 1) * P], None).then_inc(sent[q], 16)

                with pool.Fori(0, B // 2) as i:
                    for q in range(2):
                        send(i, q)
                for q in range(2):
                    pool.wait_ge(sent[q], B // 2 * EACH)

            @block.tensor
            def _(pe):
                def route(b, q):
                    hold(pe, xn_ready, b + 1)
                    for h in range(2):
                        for t in range(4):
                            i = pe.transpose(M[h][:, t * P:(t + 1) * P], XN[:, q, (4 * h + t) * P:(4 * h + t + 1) * P], ident[:, :])
                        i.then_inc(xt_ps, 1)
                    for h in range(2):
                        hold(pe, xt_ready, 2 * b + h + 1)
                        for t in range(4 * h, 4 * h + 4):
                            i = pe.matmul(L[:, t * E:(t + 1) * E], XT[:, t * P:(t + 1) * P], Wr0[:, :], start=True, stop=True)
                    i.then_inc(lg_ps, 1)

                def rank(b):
                    hold(pe, ch_ready, b + 1)
                    pe.matmul(RK[:, 0:(NT + 1) * E], before[:, :], CH[:, :, :], start=True, stop=False)
                    for t in range(NT):
                        later = NT - t
                        i = pe.matmul(RK[:, (t + 1) * E:(NT + 1) * E].rearrange("p (l e) -> p l e", e=E), ones[:, :],
                                      CH[:, t:t + 1, :].to_broadcast([P, later, E]), start=False, stop=(t == NT - 1))
                    i.then_inc(rk_ps, 1)

                pe.wait_ge(before_ready, 1)
                with pe.Fori(0, B // 2) as i:
                    for q in range(2):
                        route(2 * i + q, q)
                        rank(2 * i + q)
                pe.wait_ge(used_ready, 1)
                pe.matmul(TB[:, 0:1], before[:, :], ubf[:, :], start=True, stop=True)
                pe.matmul(TB[:, 1:1 + E], ones[:, :], below[:, :], start=True, stop=True).then_inc(rank_ps, 1)
                pe.wait_ge(hot_ready, 1)
                pe.matmul(TC[0:1, 0:NB], rel[:, :], hot[:, :], start=True, stop=True)
                pe.matmul(TC[0:1, NB:2 * NB], ef[:, :], hot[:, :], start=True, stop=True).then_inc(table_ps, 1)

            @block.scalar
            def _(act):
                with act.Fori(0, B) as b:
                    for h in range(2):
                        act.wait_ge(xt_ps, 2 * b + h + 1)
                        nc.scalar.activation(XT[:, h * HALF:(h + 1) * HALF], M[h][:, :], ACT.Identity,
                                             bias=pcol[:, at["L0_ffn_beta"]:at["L0_ffn_beta"] + 1],
                                             scale=pcol[:, at["L0_ffn_gamma"]:at["L0_ffn_gamma"] + 1]).then_inc(xt_ready, 1)
                    act.wait_ge(dd_ready, b + 1)
                    nc.scalar.activation(ex[:, :], dd[:, :], ACT.Exp).then_inc(ex_ready, 1)

            @block.vector
            def _(dve):
                step = Count()
                v = nc.vector

                def op(f, *a, **k):
                    f(*a, **k).then_inc(dstep, 1)
                    hold(dve, dstep, step.next())

                def wide(t):
                    return t.unsqueeze(2).to_broadcast([P, NT, E])

                def norm(i, q, again):
                    if again:
                        hold(dve, sent[q], i * EACH)
                    for t in range(NT):
                        at_ = (2 * i + q) * NT + t
                        n = v.tensor_scalar(XN[:, q, t * P:(t + 1) * P], X[:, bass.ds(at_ * P, P)], MEAN[:, bass.ds(at_, 1)],
                                            ROOT[:, bass.ds(at_, 1)], ALU.subtract, ALU.mult)
                    n.then_inc(xn_ready, 1)

                def first_max(logits, top, onehot, number):
                    op(v.tensor_reduce, top[:, :], logits, AX_X, ALU.max)
                    op(v.tensor_tensor, Q[:, :, :], logits, wide(top[:, :]), ALU.is_equal)
                    op(v.tensor_tensor, Q[:, :, :], Q[:, :, :], order[:, :].unsqueeze(1).to_broadcast([P, NT, E]), ALU.mult)
                    op(v.tensor_reduce, k1[:, :], Q[:, :, :], AX_X, ALU.max)
                    v.tensor_copy(number, k1[:, :])
                    op(v.tensor_tensor, onehot, Q[:, :, :], wide(k1[:, :]), ALU.is_equal)

                def choose(b):
                    hold(dve, lg_ps, b + 1)
                    op(v.tensor_tensor, LG[:, :, :], L[:, 0:NT * E].rearrange("p (t e) -> p t e", e=E),
                       br0[:, :].unsqueeze(1).to_broadcast([P, NT, E]), ALU.add)
                    first_max(LG[:, :, :], m1, OH1[:, :, :], CHOSEN[:, bass.ds(b * 2 * NT, NT)])
                    op(v.scalar_tensor_tensor, out=L2[:, :, :], in0=OH1[:, :, :], scalar=-1e30, in1=LG[:, :, :],
                       op0=ALU.mult, op1=ALU.add)
                    first_max(L2[:, :, :], m2, OH2[:, :, :], CHOSEN[:, bass.ds(b * 2 * NT + NT, NT)])
                    v.tensor_tensor(CH[:, 0:NT, :], OH1[:, :, :], OH2[:, :, :], ALU.add).then_inc(ch_ready, 1)
                    v.tensor_tensor(dd[:, :], m2[:, :], m1[:, :], ALU.subtract).then_inc(dd_ready, 1)

                def seat(b, q):
                    hold(dve, rk_ps, b + 1)
                    op(v.tensor_tensor, SEAT[:, :, :], RK[:, 0:NT * E].rearrange("p (t e) -> p t e", e=E),
                       NEXT[:, :].unsqueeze(1).to_broadcast([P, NT, E]), ALU.add)
                    op(v.tensor_tensor, NEXT[:, :], NEXT[:, :], RK[:, NT * E:(NT + 1) * E], ALU.add)
                    for k, oh in enumerate((OH1, OH2)):
                        op(v.tensor_tensor, Q[:, :, :], SEAT[:, :, :], oh[:, :, :], ALU.mult)
                        op(v.tensor_reduce, AT[:, k, :], Q[:, :, :], AX_X, ALU.add)
                    v.tensor_copy(ROW[:, bass.ds(b * 2 * NT, 2 * NT)], AT[:, :, :].rearrange("p k t -> p (k t)"))
                    v.tensor_copy(AT_I[q][:, :], AT[:, :, :].rearrange("p k t -> p (k t)")).then_inc(at_ready, 1)
                    hold(dve, ex_ready, b + 1)
                    op(v.tensor_scalar, s1[:, :], ex[:, :], 1.0, None, ALU.add)
                    op(v.reciprocal, s1[:, :], s1[:, :])
                    v.tensor_copy(SHARE[:, bass.ds(b * 2 * NT, NT)], s1[:, :])
                    op(v.tensor_tensor, SHARE[:, bass.ds(b * 2 * NT + NT, NT)], ex[:, :], s1[:, :], ALU.mult)

                def tables():
                    v.tensor_copy(tail[:, :], NEXT[0:1, :]).then_inc(tail_ready, 1)
                    dve.wait_ge(masks, 2)
                    op(v.tensor_tensor, pick8[:, :], mine[:, :], order[:, :], ALU.mult)
                    op(v.tensor_reduce, got[:, :], pick8[:, :], AX_X, ALU.add)
                    op(v.tensor_scalar, ef[:, :], got[:, :], -1.0, float(E), ALU.mult, ALU.add)
                    op(v.tensor_scalar, rowno[:, :], ef[:, :], float(SEATS - PER * BLOCK), None, ALU.mult)
                    op(v.scalar_tensor_tensor, out=rowno[:, :], in0=pf[:, :], scalar=float(BLOCK), in1=rowno[:, :],
                       op0=ALU.mult, op1=ALU.add)
                    op(v.tensor_tensor, pick8[:, :], mine[:, :], NEXT[:, :], ALU.mult)
                    op(v.tensor_reduce, got[:, :], pick8[:, :], AX_X, ALU.add)
                    op(v.tensor_tensor, used[:, :], got[:, :], rowno[:, :], ALU.is_gt)
                    op(v.tensor_copy, ubf[:, :], used[:, :])
                    v.tensor_scalar(below[:, :], upto[:, :], used[:, :], None, ALU.mult).then_inc(used_ready, 1)
                    dve.wait_ge(rank_ps, 1)
                    op(v.tensor_copy, got[:, :], TB[:, 0:1])
                    v.tensor_scalar(rel[:, :], rowno[:, :], -float(SPARE), None, ALU.add)
                    v.tensor_scalar(hot[:, :], kth[:, :], got[:, :], used[:, :], ALU.is_equal, ALU.mult).then_inc(hot_ready, 1)
                    op(v.tensor_scalar, pick8[:, :], TB[:, 1:1 + E], float(BLOCK), -float(SPARE), ALU.mult, ALU.add)
                    op(v.scalar_tensor_tensor, out=shift8[:, :], in0=order[:, :], scalar=float(SEATS), in1=pick8[:, :],
                       op0=ALU.mult, op1=ALU.add)
                    for e in range(E):
                        op(v.tensor_scalar, TMP[:, :], CHOSEN[:, :], float(E - e), shift8[:, e:e + 1], ALU.is_equal, ALU.mult)
                        op(v.tensor_tensor, ROW[:, :], ROW[:, :], TMP[:, :], ALU.add)
                    v.tensor_copy(ROW_I[:, :], ROW[:, :])
                    dve.wait_ge(table_ps, 1)
                    v.tensor_scalar(FROM[:, :], TC[0:1, 0:NB], float(SPARE), None, ALU.add)
                    v.tensor_copy(EXPERT[:, :], TC[0:1, NB:2 * NB])

                def pair(i, first, last):
                    choose(2 * i)
                    seat(2 * i, 0)
                    norm(i, 1, not first)
                    choose(2 * i + 1)
                    seat(2 * i + 1, 1)
                    if not last:
                        norm(i + 1, 0, True)

                for e in range(E):
                    v.memset(NEXT[:, e:e + 1], float(e * SEATS))
                op(v.memset, CH[:, :, :], 0.0)
                norm(0, 0, False)
                pair(0, True, False)
                with dve.Fori(1, B // 2 - 1) as i:
                    step.loop(i - 1, 2 * (12 + 9))
                    pair(i, False, False)
                step.end(B // 2 - 2)
                pair(B // 2 - 1, False, True)
                tables()

        with ExitStack() as ctx:
            def tile(name, shape, dt=F32):
                return sb(name, shape, dt, ctx)

            XB, YB = tile("XB", [P, 2, 4, P]), tile("YB", [P, 2, 4, P])
            XT = tile("bbXT", [P, 2, BLOCK])
            G = tile("G", [P, 2, HC, BLOCK])
            W1E, W2E, B1E = tile("W1E", [P, 2, HID]), tile("W2E", [P, 2, HC * P]), tile("B1E", [P, 2, HC])
            U, Y, M = ([ctx.enter_context(nc.psum_tensor(f"b{n}{i}", [P, HALF], F32)) for i in range(2)]
                       for n in ("U", "Y", "N"))
            turned, xt_ready, w1_ready, w2_ready, u_ready, g_ready, y_ready, yb_ready = (sem("bb_" + n) for n in (
                "turned", "xt_ready", "w1_ready", "w2_ready", "u_ready", "g_ready", "y_ready", "yb_ready"))
            xb_loaded, yb_stored = ([sem(f"bb_{n}{q}") for q in range(2)] for n in ("xb_loaded", "yb_stored"))
            assert HC == 2 and NB % 2 == 1
            block = ctx.enter_context(nc.Block())

            def blocks(eng, do):
                for k in range(3):
                    do(k, k // 2, k % 2, False)
                with eng.Fori(2, (NB - 3) // 2 + 1) as i:
                    do(2 * i - 1, i - 1, 1, False)
                    do(2 * i, i, 0, False)
                do(NB - 2, (NB - 2) // 2, 1, False)
                do(NB - 1, (NB - 1) // 2, 0, True)

            @block.sync
            def _(sp):
                def load(k, i, q, last):
                    if not isinstance(k, int) or k >= 2:
                        hold(sp, turned, k - 1)
                    row = sp.value_load(FROM[0:1, bass.ds(k, 1)], min_val=0, max_val=SPARE)
                    sp.dma_start(XB[:, q, :, :], sorted_x[bass.ds(row, BLOCK), :].rearrange("(t p) d -> p t d", p=P)
                                 ).then_inc(xb_loaded[q], 16)

                blocks(sp, load)

            @block.gpsimd
            def _(pool):
                def store(k, i, q, last):
                    hold(pool, yb_ready, k + 1)
                    pool.dma_start(sorted_y[bass.ds(k * BLOCK, BLOCK), :].rearrange("(t p) d -> p t d", p=P), YB[:, q, :, :]
                                   ).then_inc(yb_stored[q], 16)

                blocks(pool, store)
                for q in range(2):
                    pool.wait_ge(yb_stored[q], 16 * ((NB + 1 - q) // 2))

            @block.tensor
            def _(pe):
                def turn(i, q):
                    hold(pe, xb_loaded[q], 16 * (i + 1))
                    for t in range(4):
                        j = pe.transpose(M[q][:, t * P:(t + 1) * P], XB[:, q, t, :], ident[:, :])
                    j.then_inc(turned, 1)

                def out(k, q):
                    hold(pe, g_ready, 2 * k + 2)
                    hold(pe, w2_ready, k + 1)
                    if not isinstance(k, int) or k >= 2:
                        hold(pe, yb_ready, k - 1)
                    for c in range(HC):
                        for t in range(4):
                            j = pe.matmul(Y[q][:, t * P:(t + 1) * P], G[:, q, c, t * P:(t + 1) * P], W2E[:, q, c * P:(c + 1) * P],
                                          start=(c == 0 and t == 0), stop=(c == HC - 1 and t == 3))
                    j.then_inc(y_ready, 1)

                def work(k, i, q, last):
                    hold(pe, xt_ready, k + 1)
                    hold(pe, w1_ready, k + 1)
                    for c in range(HC):
                        if not isinstance(k, int) or k >= 1:
                            hold(pe, g_ready, 2 * k - 1 + c)
                        pe.matmul(U[c][:, :], W1E[:, q, c * P:(c + 1) * P], XT[:, q, :], start=True, stop=True
                                  ).then_inc(u_ready, 1)
                    if not last:
                        turn(i + q, 1 - q)
                    if not isinstance(k, int) or k >= 1:
                        out(k - 1, 1 - q)

                turn(0, 0)
                blocks(pe, work)
                out(NB - 1, (NB - 1) % 2)

            @block.scalar
            def _(act):
                def copy_xt(k, q):
                    act.wait_ge(turned, k + 1)
                    nc.scalar.activation(XT[:, q, :], M[q][:, :], ACT.Identity,
                                         bias=pcol[:, at["L0_ffn_beta"]:at["L0_ffn_beta"] + 1],
                                         scale=pcol[:, at["L0_ffn_gamma"]:at["L0_ffn_gamma"] + 1]).then_inc(xt_ready, 1)

                def work(k, i, q, last):
                    for c in range(HC):
                        act.wait_ge(u_ready, 2 * k + c + 1)
                        if c == 0 and (not isinstance(k, int) or k >= 2):
                            act.wait_ge(y_ready, k - 1)
                        nc.scalar.activation(G[:, q, c, :], U[c][:, :], ACT.Gelu, bias=B1E[:, q, c:c + 1]).then_inc(g_ready, 1)
                    if not last:
                        copy_xt(k + 1, 1 - q)

                copy_xt(0, 0)
                blocks(act, work)

            @block.vector
            def _(dve):
                def first_weights(k, q):
                    if not isinstance(k, int) or k >= 2:
                        hold(dve, g_ready, 2 * k - 2)
                    e = dve.value_load(EXPERT[0:1, bass.ds(k, 1)], min_val=0, max_val=E - 1)
                    nc.vector.tensor_copy(B1E[:, q, :], pcol[:, bass.ds(e * HC + at["L0_ffn_b1"], HC)])
                    nc.vector.tensor_copy(W1E[:, q, :], W1[:, bass.ds(e * HID, HID)]).then_inc(w1_ready, 1)
                    return e

                def second_weights(k, q):
                    e = dve.value_load(EXPERT[0:1, bass.ds(k, 1)], min_val=0, max_val=E - 1)
                    nc.vector.tensor_copy(W2E[:, q, :], W2[:, bass.ds(e * HC * P, HC * P)]).then_inc(w2_ready, 1)

                def finish(k, i, q):
                    e = dve.value_load(EXPERT[0:1, bass.ds(k, 1)], min_val=0, max_val=E - 1)
                    hold(dve, y_ready, k + 1)
                    if not isinstance(k, int) or k >= 2:
                        hold(dve, yb_stored[q], 16 * i)
                    nc.vector.tensor_tensor(YB[:, q, :, :], Y[q][:, :].rearrange("p (t d) -> p t d", d=P),
                                            b20[:, bass.ds(e * P, P)].unsqueeze(1).to_broadcast([P, 4, P]), ALU.add
                                            ).then_inc(yb_ready, 1)

                def work(k, i, q, last):
                    if not last:
                        first_weights(k + 1, 1 - q)
                    if not isinstance(k, int) or k >= 1:
                        finish(k - 1, i + q - 1, 1 - q)
                    if not last:
                        second_weights(k + 1, 1 - q)

                first_weights(0, 0)
                second_weights(0, 0)
                blocks(dve, work)
                finish(NB - 1, (NB - 1) // 2, 0)

        shared_sems = {}

        def either(name):
            if name not in shared_sems:
                shared_sems[name] = sem("c_" + name)
            return shared_sems[name]

        def edge_attention(kinds, ctx, pre):
            def tile(name, shape, dt=F32):
                return sb(pre + name, shape, dt, ctx)

            ADJ = tile("ADJ", [P, 4, N], I32)
            NK = tile("NK", [P, 2, kinds, N], BF16)
            AK = tile("AK", [P, 2, kinds, P])
            ST, MV, RS = tile("ST", [P, NT, 6]), tile("MV", [P, NT, 2]), tile("RS", [P, 2, NT])
            MVN, RSN = tile("MVN", [P, NT, 2]), tile("RSN", [P, 2, NT])
            YG = W1[:, :].rearrange("p (k d) -> p k d", d=P)
            ROW_B = tile("ROW_B", [P, 2 * NT], I32)
            XN = tile("XN", [P, N])
            XNN = b20
            XB, XT = W2, tile("XT", [P, 2 * N])
            ACC = tile("ACC", [P, 2, N]) if kinds > 1 else None
            R4, Y, PR, PT = (tile(n, [P, 2, N]) for n in ("R4", "Y", "PR", "PT"))
            MX, NMX, Z, RZ = (tile(n, [P, 2]) for n in ("MX", "NMX", "Z", "RZ"))
            T = [ctx.enter_context(nc.psum_tensor(f"{pre}T{i}", [P, N], F32)) for i in range(2)]
            TP = [ctx.enter_context(nc.psum_tensor(f"{pre}TP{i}", [P, HALF], F32)) for i in range(2)]
            O = ctx.enter_context(nc.psum_tensor(pre + "O", [P, HALF], F32))
            M = ctx.enter_context(nc.psum_tensor(pre + "M", [P, HALF], F32))
            (mv_ready, rs_ready, xn_ready, dstep, pstep, xt_ps, xt_ready, made, t_ready, t_read, acc_ready, r4_ready, y_ready,
             shift_ready, pr_ready, pv_done, x_added, xb_ready, next_mv_ready, next_rs_ready, next_xn_ready, nt_ps, nt_ready,
             ft_ready, row_ready, gathered, joined) = (either(n) for n in (
                 "mv_ready", "rs_ready", "xn_ready", "dve_step", "pool_step", "xt_ps", "xt_ready", "made", "t_ready",
                 "t_read", "acc_ready", "r4_ready", "y_ready", "shift_ready", "pr_ready", "pv_done", "x_added", "xb_ready",
                 "next_mv_ready", "next_rs_ready", "next_xn_ready", "nt_ps", "nt_ready", "ft_ready", "row_ready",
                 "gathered", "joined"))
            tp_ps, tp_read = ([either(f"{n}{h}") for h in range(2)] for n in ("tp_ps", "tp_read"))
            loaded = [either(f"adj_loaded{i}") for i in range(4)]
            K = kinds
            LAST = B - 1
            block = ctx.enter_context(nc.Block())

            @block.sync
            def _(sp):
                def load(b):
                    for t in range(NT):
                        wait(sp, made, b * NT + t - 3)
                        sp.dma_start(ADJ[:, t % 4, :], adj[bass.ds(b, 1), t * P:(t + 1) * P, :].rearrange("o p i -> (o p) i")
                                     ).then_inc(loaded[t % 4], 16)
                load(0)
                with sp.Fori(1, B) as b:
                    load(b)

            @block.gpsimd
            def _(pool):
                step = Count()

                def batch(b):
                    ln_root(pool, b, MV, RS, pstep, step, mv_ready, rs_ready, False)
                    pool.wait_ge(xn_ready, b + 1)
                    nc.gpsimd.tensor_copy(XB[:, bass.ds((b % 2) * N, N)], XN[:, :]).then_inc(xb_ready, 1)

                def root_next(b):
                    ln_root(pool, b, MVN, RSN, pstep, step, next_mv_ready, next_rs_ready, False)

                def feature(b):
                    pool.wait_ge(nt_ready, 2 * b + 2)
                    hold(pool, ft_ready, b + 1)
                    nc.gpsimd.tensor_tensor(FT[:, :], FT[:, :], XTN[:, bass.ds(b * N, N)], ALU.add).then_inc(ft_ready, 1)

                def gather(b):
                    if not isinstance(b, int) or b > 0:
                        hold(pool, joined, b)
                    nc.gpsimd.tensor_copy(ROW_B[:, :], ROW_I[:, bass.ds(b * 2 * NT, 2 * NT)]).then_inc(row_ready, 1)
                    hold(pool, row_ready, b + 1)
                    for t in range(2 * NT):
                        nc.gpsimd.indirect_dma_start(YG[:, t, :], None, sorted_y,
                                                     bass.IndirectOffsetOnAxis(ap=ROW_B[:, t:t + 1], axis=0)
                                                     ).then_inc(gathered, 16)

                gather(0)
                nc.gpsimd.memset(FT[:, :], 0.0).then_inc(ft_ready, 1)
                batch(0)
                gather(1)
                batch(1)
                gather(2)
                with pool.Fori(2, B - 1) as b:
                    step.loop(b - 2, 2)
                    root_next(b - 2)
                    batch(b)
                    gather(b + 1)
                    feature(b - 2)
                step.end(B - 3)
                root_next(B - 3)
                batch(B - 1)
                feature(B - 3)
                for b in (B - 2, B - 1):
                    root_next(b)
                    feature(b)
                pool.wait_ge(ft_ready, B + 1)

            @block.tensor
            def _(pe):
                def turn_x(b, h):
                    pe.wait_ge(xn_ready, b + 1)
                    if h == 1 or (isinstance(b, int) and b == 1):
                        hold(pe, xt_ready, 2 * b + h)
                    elif not isinstance(b, int) or b > 1:
                        hold(pe, nt_ready, 2 * b - 2)
                    for t in range(4):
                        i = pe.transpose(M[:, t * P:(t + 1) * P], XN[:, bass.ts(4 * h + t, P)], ident[:, :])
                    i.then_inc(xt_ps, 1)

                def turn_next(b, h, turned):
                    pe.wait_ge(next_xn_ready, b + 1)
                    if h == 0:
                        hold(pe, xt_ready, turned)
                    else:
                        hold(pe, nt_ready, 2 * b + 1)
                    for t in range(4):
                        i = pe.transpose(M[:, t * P:(t + 1) * P], XNN[:, bass.ts(4 * h + t, P)], ident[:, :])
                    i.then_inc(nt_ps, 1)

                def scores(b, r):
                    g = b * NT + r
                    hold(pe, made, g + 1)
                    for k in range(K):
                        t = T[k % 2] if K > 1 else T[r % 2]
                        if not isinstance(g, int) or g * K + k > 1:
                            hold(pe, t_read, g * K + k - 1)
                        for h in range(2):
                            pe.matmul(t[:, h * HALF:(h + 1) * HALF], AK[:, r % 2, k, :],
                                      XT[:, bass.ds((b % 2) * N + h * HALF, HALF)], start=True, stop=False)
                            i = pe.matmul(t[:, h * HALF:(h + 1) * HALF], blockI[:, :], NK[:, r % 2, k, h * HALF:(h + 1) * HALF],
                                          start=False, stop=True)
                        i.then_inc(t_ready, 1)

                def turn_p(b, r):
                    pe.wait_ge(pr_ready, b * NT + r + 1)
                    for h in range(2):
                        wait(pe, tp_read[h], b * NT + r)
                        for c in range(4):
                            i = pe.transpose(TP[h][:, c * P:(c + 1) * P], PR[:, r % 2, (4 * h + c) * P:(4 * h + c + 1) * P],
                                             ident[:, :])
                        i.then_inc(tp_ps[h], 1)

                def attend(b, r):
                    if r == 0:
                        hold(pe, xb_ready, b + 1)
                    hold(pe, x_added, b * NT + r)
                    for h in range(2):
                        hold(pe, tp_read[h], b * NT + r + 1)
                        for c in range(4 * h, 4 * h + 4):
                            i = pe.matmul(O[:, 0:P], PT[:, r % 2, c * P:(c + 1) * P], XB[:, bass.ds((b % 2) * N + c * P, P)],
                                          start=(c == 0), stop=(c == NT - 1))
                    i.then_inc(pv_done, 1)

                def batch(b, first, last):
                    for r in range(NT):
                        scores(b, r)
                        if r >= 1:
                            turn_p(b, r - 1)
                        elif not first:
                            turn_p(b - 1, NT - 1)
                        if r >= 2:
                            attend(b, r - 2)
                        elif not first:
                            attend(b - 1, NT - 2 + r)
                        if not first and r in (3, 4):
                            turn_next(b - 1, r - 3, 2 * b + 2)
                        if not last and r in (5, 6):
                            turn_x(b + 1, r - 5)

                for h in range(2):
                    turn_x(0, h)
                batch(0, True, False)
                with pe.Fori(1, LAST) as b:
                    batch(b, False, False)
                batch(LAST, False, True)
                turn_p(LAST, NT - 1)
                attend(LAST, NT - 2)
                attend(LAST, NT - 1)
                for h in range(2):
                    turn_next(LAST, h, 2 * B)

            @block.scalar
            def _(act):
                def copy_xt(b, h):
                    act.wait_ge(xt_ps, 2 * b + h + 1)
                    wait(act, t_ready, (b - 1) * NT * K)
                    wait(act, made, (b - 1) * NT)
                    nc.scalar.copy(XT[:, bass.ds((b % 2) * N + h * HALF, HALF)], M[:, :]).then_inc(xt_ready, 1)

                def copy_next(b, h):
                    act.wait_ge(nt_ps, 2 * b + h + 1)
                    nc.scalar.copy(XTN[:, bass.ds(b * N + h * HALF, HALF)], M[:, :]).then_inc(nt_ready, 1)

                def relu(b, r):
                    g = b * NT + r
                    wait(act, y_ready, g - 1)
                    if K > 1:
                        act.wait_ge(t_ready, g * K + 1)
                        nc.scalar.copy(ACC[:, r % 2, :], T[0][:, :]).then_inc(t_read, 1)
                        act.wait_ge(acc_ready, g * (K - 1) + K - 1)
                        nc.scalar.activation(R4[:, r % 2, :], ACC[:, r % 2, :], ACT.Relu, scale=4.0).then_inc(r4_ready, 1)
                    else:
                        act.wait_ge(t_ready, g + 1)
                        nc.scalar.activation(R4[:, r % 2, :], T[r % 2][:, :], ACT.Relu, scale=4.0).then_inc(r4_ready, 1)

                def prob(b, r):
                    g = b * NT + r
                    act.wait_ge(shift_ready, g + 1)
                    wait(act, tp_ps[1], g - 1)
                    wait(act, x_added, g - 1)
                    nc.scalar.activation(PR[:, r % 2, :], Y[:, r % 2, :], ACT.Exp, bias=NMX[:, r % 2:r % 2 + 1], scale=SLOPE,
                                         accum_out=Z[:, r % 2:r % 2 + 1]).then_inc(pr_ready, 1)

                def copy_p(b, r):
                    g = b * NT + r
                    act.wait_ge(tp_ps[0], g + 1)
                    wait(act, pv_done, g - 1)
                    nc.scalar.copy(PT[:, r % 2, 0:HALF], TP[0][:, :]).then_inc(tp_read[0], 1)

                def batch(b, first, last):
                    for r in range(NT):
                        relu(b, r)
                        if r >= 1:
                            copy_p(b, r - 1)
                        elif not first:
                            copy_p(b - 1, NT - 1)
                        prob(b, r)
                        if not first and r in (3, 4):
                            copy_next(b - 1, r - 3)
                        if not last and r in (5, 6):
                            copy_xt(b + 1, r - 5)

                for h in range(2):
                    copy_xt(0, h)
                batch(0, True, False)
                with act.Fori(1, LAST) as b:
                    batch(b, False, False)
                batch(LAST, False, True)
                copy_p(LAST, NT - 1)
                for h in range(2):
                    copy_next(LAST, h)

            @block.vector
            def _(dve):
                step = Count()

                def make(b, r):
                    g = b * NT + r
                    if r == 0:
                        dve.wait_ge(xt_ready, 2 * b + 2)
                    wait(dve, t_ready, (g - 1) * K)
                    for k in range(K):
                        nc.vector.tensor_scalar(AK[:, r % 2, k, :], XT[:, bass.ds((b % 2) * N + r * P, P)],
                                                pcol[:, at[f"L1_gnn_a{k}"]:at[f"L1_gnn_a{k}"] + 1], None, ALU.mult)
                    dve.wait_ge(loaded[r % 4], 16 * (b * (NT // 4) + r // 4 + 1))
                    for k in range(K):
                        i = nc.vector.tensor_scalar(NK[:, r % 2, k, :], ADJ[:, r % 4, :], float(k + 1), None, ALU.not_equal)
                    i.then_inc(made, 1)

                def shift(b, r):
                    g = b * NT + r
                    for k in range(1, K):
                        hold(dve, t_read, g * K + k)
                        dve.wait_ge(t_ready, g * K + k + 1)
                        nc.vector.tensor_tensor(ACC[:, r % 2, :], ACC[:, r % 2, :], T[k % 2][:, :], ALU.max).then_inc(t_read, 1)
                        hold(dve, t_read, g * K + k + 1)
                        dve.sem_inc(acc_ready, 1)
                    if not isinstance(g, int) or g > 1:
                        hold(dve, pr_ready, g - 1)
                    hold(dve, r4_ready, g + 1)
                    i = nc.vector.tensor_tensor_reduce(Y[:, r % 2, :], T[r % 2][:, :] if K == 1 else ACC[:, r % 2, :],
                                                       R4[:, r % 2, :], 1.0, -3.0e38, ALU.add, ALU.max, MX[:, r % 2:r % 2 + 1])
                    i.then_inc(y_ready, 1)
                    hold(dve, y_ready, g + 1)
                    if K == 1:
                        dve.sem_inc(t_read, 1)
                    nc.vector.tensor_scalar(NMX[:, r % 2:r % 2 + 1], MX[:, r % 2:r % 2 + 1], -SLOPE, None, ALU.mult
                                            ).then_inc(shift_ready, 1)

                def copy_p(b, r):
                    g = b * NT + r
                    dve.wait_ge(tp_ps[1], g + 1)
                    wait(dve, pv_done, g - 1)
                    nc.vector.tensor_copy(PT[:, r % 2, HALF:N], TP[1][:, :]).then_inc(tp_read[1], 1)

                def add(b, r):
                    g = b * NT + r
                    nc.vector.reciprocal(RZ[:, r % 2:r % 2 + 1], Z[:, r % 2:r % 2 + 1]).then_inc(dstep, 1)
                    dve.wait_ge(dstep, step.next())
                    dve.wait_ge(pv_done, g + 1)
                    xb = X[:, bass.ds(b * N + r * P, P)]
                    nc.vector.scalar_tensor_tensor(out=xb, in0=O[:, 0:P], scalar=RZ[:, r % 2:r % 2 + 1], in1=xb,
                                                   op0=ALU.mult, op1=ALU.add).then_inc(x_added, 1)

                def norm(b):
                    if not isinstance(b, int) or b > 0:
                        dve.wait_ge(xt_ps, 2 * b)
                        dve.wait_ge(xb_ready, b)
                    ln_apply(dve, b, MV, RS[:, 1, :], XN, 0, rs_ready, xn_ready)

                def join(b):
                    hold(dve, gathered, 16 * 2 * NT * (b + 1))
                    for k in range(2):
                        for t in range(NT):
                            xb = X[:, bass.ds((b * NT + t) * P, P)]
                            i = nc.vector.scalar_tensor_tensor(out=xb, in0=YG[:, k * NT + t, :],
                                                               scalar=SHARE[:, bass.ds((b * 2 + k) * NT + t, 1)], in1=xb,
                                                               op0=ALU.mult, op1=ALU.add)
                        if k == 0:
                            i.then_inc(dstep, 1)
                            hold(dve, dstep, step.next())
                    i.then_inc(joined, 1)
                    hold(dve, joined, b + 1)

                def stats_next(b):
                    hold(dve, x_added, (b + 1) * NT)
                    ln_stats(dve, b, ST, MVN, dstep, step, next_mv_ready)

                def norm_next(b):
                    ln_apply(dve, b, MVN, RSN[:, 1, :], XNN, 0, next_rs_ready, next_xn_ready)

                def batch(b, first, last):
                    for r in range(NT):
                        if not (last and r == NT - 1):
                            make(b + (r + 1) // NT, (r + 1) % NT)
                        shift(b, r)
                        if r >= 1:
                            copy_p(b, r - 1)
                        elif not first:
                            copy_p(b - 1, NT - 1)
                        if r >= 2:
                            add(b, r - 2)
                        elif not first:
                            add(b - 1, NT - 2 + r)
                        if not first:
                            if r == 1:
                                stats_next(b - 1)
                            if r == 2:
                                norm_next(b - 1)
                        if not last:
                            if r == 2:
                                join(b + 1)
                            if r == 3:
                                ln_stats(dve, b + 1, ST, MV, dstep, step, mv_ready)
                            if r == 4:
                                norm(b + 1)

                join(0)
                ln_stats(dve, 0, ST, MV, dstep, step, mv_ready)
                norm(0)
                make(0, 0)
                batch(0, True, False)
                with dve.Fori(1, LAST) as b:
                    step.loop(b - 1, 11)
                    batch(b, False, False)
                step.end(LAST - 1)
                batch(LAST, False, True)
                copy_p(LAST, NT - 1)
                add(LAST, NT - 2)
                add(LAST, NT - 1)
                stats_next(LAST)
                dve.wait_ge(nt_ps, 2 * LAST)
                norm_next(LAST)

        XTN = sb("XTN", [P, B * N])
        FT = sb("FT", [P, N])
        several = nc.values_load(flag[:, :], min_val=0, max_val=1)
        with nc.If(several > 0):
            with ExitStack() as ctx:
                edge_attention(4, ctx, "g_")
        with nc.Else():
            with ExitStack() as ctx:
                edge_attention(1, ctx, "f_")

        with ExitStack() as last_layer:
            def tile(name, shape, dt=F32, ctx=last_layer):
                return sb(name, shape, dt, ctx)

            WT8 = tile("dWT8", [E, N])
            WBC = tile("WBC", [P, E, N])

            with ExitStack() as ctx:
                LG, EX, W8, WR = (tile("d" + n, [P, NT, E], F32, ctx) for n in ("LG", "EX", "W8", "WR"))
                mx, sm, rs = (tile("d" + n, [P, NT], F32, ctx) for n in ("mx", "sm", "rs"))
                W3 = tile("dW3", [P, NT, 3 * E], BF16, ctx)
                WT3 = tile("dWT3", [3 * E, N], BF16, ctx)
                M = [ctx.enter_context(nc.psum_tensor(f"dM{i}", [P, HALF], F32)) for i in range(2)]
                BC = [ctx.enter_context(nc.psum_tensor(f"BC{i}", [P, HALF], F32)) for i in range(2)]
                W3T = M[0][:, :].bitcast(BF16)
                (dstep, lg_ps, lg_ready, ex_ready, w_ready, w3t_ps,
                 wt3_ready, bc_ps, bc_act, bc_dve) = (sem("d_" + n) for n in (
                     "dve_step", "lg_ps", "lg_ready",
                     "ex_ready", "w_ready", "w3t_ps", "wt3_ready", "bc_ps", "bc_act", "bc_dve"))
                wt8_ps = [sem(f"d_wt8_ps{h}") for h in range(2)]
                wt8_done = sem("d_wt8_done")
                block = ctx.enter_context(nc.Block())

                @block.tensor
                def _(pe):
                    for t in range(NT):
                        i = pe.matmul(M[0][:, t * E:(t + 1) * E], FT[:, t * P:(t + 1) * P], Wr1[:, :], start=True, stop=True)
                    i.then_inc(lg_ps, 1)
                    pe.wait_ge(w_ready, 1)
                    for t in range(NT):
                        i = pe.transpose(W3T[0:3 * E, t * P:(t + 1) * P], W3[:, t, :], identb[:, :])
                    i.then_inc(w3t_ps, 1)
                    pe.wait_ge(wt3_ready, 1)
                    for h in range(2):
                        for t in range(4):
                            i = pe.transpose(M[h][0:E, t * P:(t + 1) * P], W8[:, 4 * h + t, :], ident[:, :])
                        i.then_inc(wt8_ps[h], 1)
                    for k in range(2 * E):
                        wait(pe, (bc_act, bc_dve)[k % 2], k // 2)
                        pe.matmul(BC[k % 2][:, :], pick[:, k // 2 * P:(k // 2 + 1) * P],
                                  WT3[:, k % 2 * HALF:(k % 2 + 1) * HALF], start=True, stop=True).then_inc(bc_ps, 1)

                @block.scalar
                def _(act):
                    act.wait_ge(lg_ready, 1)
                    nc.scalar.activation(EX[:, :, :], LG[:, :, :], ACT.Exp).then_inc(ex_ready, 1)
                    for h in range(2):
                        act.wait_ge(wt8_ps[h], 1)
                        nc.scalar.copy(WT8[:, h * HALF:(h + 1) * HALF], M[h][0:E, :]).then_inc(wt8_done, 1)
                    for e in range(E):
                        act.wait_ge(bc_ps, 2 * e + 1)
                        nc.scalar.copy(WBC[:, e, 0:HALF], BC[0][:, :]).then_inc(bc_act, 1)

                @block.vector
                def _(dve):
                    step = Count()
                    v = nc.vector

                    def op(f, *a, **k):
                        f(*a, **k).then_inc(dstep, 1)
                        dve.wait_ge(dstep, step.next())

                    def wide(t):
                        return t[:, :].unsqueeze(2).to_broadcast([P, NT, E])

                    dve.wait_ge(lg_ps, 1)
                    op(v.scalar_tensor_tensor, out=LG[:, :, :], in0=M[0][:, 0:NT * E].rearrange("p (t e) -> p t e", e=E),
                       scalar=1.0 / B, in1=br1[:, :].unsqueeze(1).to_broadcast([P, NT, E]), op0=ALU.mult, op1=ALU.add)
                    op(v.tensor_reduce, mx[:, :], LG[:, :, :], AX_X, ALU.max)
                    v.tensor_tensor(LG[:, :, :], LG[:, :, :], wide(mx), ALU.subtract).then_inc(lg_ready, 1)
                    dve.wait_ge(ex_ready, 1)
                    op(v.tensor_reduce, sm[:, :], EX[:, :, :], AX_X, ALU.add)
                    op(v.reciprocal, rs[:, :], sm[:, :])
                    op(v.tensor_tensor, W8[:, :, :], EX[:, :, :], wide(rs), ALU.mult)
                    op(v.tensor_copy, W3[:, :, 0:E], W8[:, :, :])
                    op(v.tensor_tensor, WR[:, :, :], W8[:, :, :], W3[:, :, 0:E], ALU.subtract)
                    op(v.tensor_copy, W3[:, :, E:2 * E], WR[:, :, :])
                    v.tensor_tensor(W3[:, :, 2 * E:3 * E], WR[:, :, :], W3[:, :, E:2 * E], ALU.subtract).then_inc(w_ready, 1)
                    dve.wait_ge(w3t_ps, 1)
                    v.tensor_copy(WT3[:, :], W3T[0:3 * E, 0:N]).then_inc(wt3_ready, 1)
                    for e in range(E):
                        dve.wait_ge(bc_ps, 2 * e + 2)
                        v.tensor_copy(WBC[:, e, HALF:N], BC[1][:, :]).then_inc(bc_dve, 1)

            with ExitStack() as ctx:
                H1, H2, GW, YS = (tile(n, [P, 2, HALF], F32, ctx) for n in ("H1", "H2", "dGW", "dYS"))
                U1, U2, Y, M = ([ctx.enter_context(nc.psum_tensor(f"e{n}{i}", [P, HALF], F32)) for i in range(2)]
                                for n in ("U1", "U2", "Y", "M"))
                u1_ready, h1_ready, u2_ready, h2_ready, gw_ready, y_mm = (sem("e_" + n) for n in (
                    "u1_ready", "h1_ready", "u2_ready", "h2_ready", "gw_ready", "y_mm"))
                ys_ready, yt_ps, x_added, stored = ([sem(f"e_{n}{h}") for h in range(2)] for n in (
                    "ys_ready", "yt_ps", "x_added", "stored"))
                S = 2 * E
                AGO = 3
                block = ctx.enter_context(nc.Block())

                @block.sync
                def _(sp):
                    with sp.Fori(0, B) as b:
                        for q in range(2):
                            sp.wait_ge(x_added[q], b + 1)
                            sp.dma_start(out[bass.ds(b, 1), q * HALF:(q + 1) * HALF, :].rearrange("o (t p) d -> p (o t) d", p=P),
                                         X[:, bass.ds(b * N + q * HALF, HALF)].rearrange("p (t d) -> p t d", d=P)
                                         ).then_inc(stored[q], 16)
                    for q in range(2):
                        sp.wait_ge(stored[q], 16 * B)

                @block.tensor
                def _(pe):
                    def first(b, s):
                        wait(pe, h1_ready, b * S + s - 1)
                        pe.matmul(U1[s % 2][:, :], V1[:, s % E * P:(s % E + 1) * P], XTN[:, bass.ds(b * N + s // E * HALF, HALF)],
                                  start=True, stop=True).then_inc(u1_ready, 1)

                    def second(b, s):
                        pe.wait_ge(h1_ready, b * S + s + 1)
                        wait(pe, h2_ready, b * S + s - 1)
                        pe.matmul(U2[s % 2][:, :], V2[:, s % E * P:(s % E + 1) * P], H1[:, s % 2, :],
                                  start=True, stop=True).then_inc(u2_ready, 1)

                    def third(b, s):
                        q, e = s // E, s % E
                        if e == 0:
                            wait(pe, ys_ready[q], b)
                            pe.matmul(Y[q][:, :], bo1[:, :], WT8[:, q * HALF:(q + 1) * HALF], start=True, stop=False)
                        pe.wait_ge(gw_ready, b * S + s + 1)
                        pe.matmul(Y[q][:, :], Vo[:, e * P:(e + 1) * P], GW[:, s % 2, :], start=False, stop=(e == E - 1)
                                  ).then_inc(y_mm, 1)

                    def turn_y(b, q):
                        pe.wait_ge(ys_ready[q], b + 1)
                        for t in range(4):
                            i = pe.transpose(M[q][:, t * P:(t + 1) * P], YS[:, q, t * P:(t + 1) * P], ident[:, :])
                        i.then_inc(yt_ps[q], 1)

                    def batch(b, start):
                        for s in range(S):
                            first(b, s)
                            if s >= AGO:
                                third(b, s - AGO)
                            elif not start:
                                third(b - 1, S + s - AGO)
                            if s >= 1:
                                second(b, s - 1)
                            elif not start:
                                second(b - 1, S - 1)
                            if s == 5 and not start:
                                turn_y(b - 1, 1)
                            if s == 13:
                                turn_y(b, 0)

                    batch(0, True)
                    with pe.Fori(1, B) as b:
                        batch(b, False)
                    second(B - 1, S - 1)
                    for s in range(S - AGO, S):
                        third(B - 1, s)
                    turn_y(B - 1, 1)

                @block.scalar
                def _(act):
                    def relu1(b, s):
                        act.wait_ge(u1_ready, b * S + s + 1)
                        wait(act, u2_ready, b * S + s - 1)
                        e = s % E
                        nc.scalar.activation(H1[:, s % 2, :], U1[s % 2][:, :], ACT.Relu, bias=bn[:, E + e:E + e + 1],
                                             scale=bn[:, e:e + 1]).then_inc(h1_ready, 1)

                    def relu2(b, s):
                        act.wait_ge(u2_ready, b * S + s + 1)
                        wait(act, gw_ready, b * S + s - 1)
                        e = s % E
                        nc.scalar.activation(H2[:, s % 2, :], U2[s % 2][:, :], ACT.Relu, bias=bn[:, 3 * E + e:3 * E + e + 1],
                                             scale=bn[:, 2 * E + e:2 * E + e + 1]).then_inc(h2_ready, 1)

                    def copy_y(b, q):
                        act.wait_ge(y_mm, b * S + (q + 1) * E)
                        nc.scalar.copy(YS[:, q, :], Y[q][:, :]).then_inc(ys_ready[q], 1)

                    def batch(b, start):
                        for s in range(S):
                            relu1(b, s)
                            if s >= 1:
                                relu2(b, s - 1)
                            elif not start:
                                relu2(b - 1, S - 1)
                            if s == 3 and not start:
                                copy_y(b - 1, 1)
                            if s == 11:
                                copy_y(b, 0)

                    batch(0, True)
                    with act.Fori(1, B) as b:
                        batch(b, False)
                    relu2(B - 1, S - 1)
                    copy_y(B - 1, 1)

                @block.vector
                def _(dve):
                    def weight(b, s):
                        q, e = s // E, s % E
                        dve.wait_ge(h2_ready, b * S + s + 1)
                        wait(dve, y_mm, b * S + s - 1)
                        nc.vector.tensor_tensor(GW[:, s % 2, :], H2[:, s % 2, :], WBC[:, e, q * HALF:(q + 1) * HALF],
                                                ALU.mult).then_inc(gw_ready, 1)

                    def add(b, q):
                        dve.wait_ge(yt_ps[q], b + 1)
                        xb = X[:, bass.ds(b * N + q * HALF, HALF)]
                        nc.vector.tensor_tensor(xb, M[q][:, :], xb, ALU.add).then_inc(x_added[q], 1)

                    def batch(b, start):
                        for s in range(S):
                            weight(b, s)
                            if s == 5 and not start:
                                add(b - 1, 1)
                            if s == 13:
                                add(b, 0)

                    batch(0, True)
                    with dve.Fori(1, B) as b:
                        batch(b, False)
                    add(B - 1, 1)



_PARAMS = (["L0_gnn_W", "L0_gnn_a"] + [f"L0_ffn_{n}" for n in ("gamma", "beta", "Wr", "br", "W1", "b1", "W2", "b2")]
           + [f"L1_gnn_a{k}" for k in range(4)]
           + [f"L1_ffn_{n}" for n in ("Wr", "br", "W1", "b1", "g1", "be1", "m1", "v1", "W2", "b2", "g2", "be2", "m2", "v2",
                                      "Wo", "bo")])


def kernel(**inputs):
    import numpy as np
    import concourse.bacc as bacc
    from concourse.bass_utils import run_bass_kernel_spmd

    nc = bacc.Bacc("TRN2", target_bir_lowering=False, num_devices=1)
    arrays, given = {}, {}
    for name in ["x", "adj"] + _PARAMS:
        a = np.ascontiguousarray(inputs[name])
        arrays[f"in_{name}"] = a
        given[name] = nc.dram_tensor(f"in_{name}", a.shape, mybir.dt.from_np(a.dtype), kind="ExternalInput").ap()
    x, adj = given.pop("x"), given.pop("adj")
    out = nc.dram_tensor("out_x", x.shape, F32, kind="ExternalOutput").ap()
    program(nc, x, adj, given, out)
    return run_bass_kernel_spmd(nc, [arrays], core_ids=[0]).results[0]["out_x"]
```

```python
from contextlib import ExitStack

import concourse.bass as bass
from concourse import mybir

F32 = mybir.dt.float32
BF16 = mybir.dt.bfloat16
I32 = mybir.dt.int32
ALU = mybir.AluOpType
ACT = mybir.ActivationFunctionType
AX_X = mybir.AxisListType.X

P = 128
HALF = 512
SLOPE = 0.2
BLOCKED = -float(2 ** 55)
EPS = 1e-5
BN_EPS = 1e-3


class Count:

    def __init__(self):
        self.base, self.n = 0, 0

    def next(self):
        self.n += 1
        return self.base + self.n

    def now(self):
        return self.base + self.n

    def loop(self, turn, per):
        self.start, self.per = self.base + self.n, per
        self.base, self.n = self.start + turn * per, 0

    def end(self, turns):
        assert self.n == self.per, (self.n, self.per)
        self.base, self.n = self.start + turns * self.per, 0


def wait(eng, sem, value):
    if not isinstance(value, int) or value > 0:
        eng.wait_ge(sem, value)


def reached(n, k):
    return not isinstance(n, int) or n >= k


def program(nc, x, adj, p, out):
    B, N, D = x.shape
    NT = N // P
    E = p["L0_ffn_W1"].shape[0]
    HID = p["L0_ffn_W1"].shape[2]
    HC = HID // P
    assert D == P and N == 2 * HALF and HID == 2 * P and E * HID == 2 * N and E * P == N and N == NT * P

    with ExitStack() as whole:
        def sem(name):
            return whole.enter_context(nc.semaphore(name))

        def sb(name, shape, dt=F32, ctx=whole):
            return ctx.enter_context(nc.sbuf_tensor(name, shape, dt))

        X = sb("X", [P, B * N])
        ident = sb("ident", [P, P])
        identb = sb("identb", [P, P], BF16)
        blockI = sb("blockI", [P, P], BF16)
        ones3 = sb("ones3", [3, P], BF16)
        pick = sb("pick", [3 * E, E * P], BF16)
        minus_half = sb("minus_half", [P, B * NT])
        eps_all = sb("eps_all", [P, B * NT])
        half8, eps8 = minus_half[:, 0:NT], eps_all[:, 0:NT]
        order = sb("order", [P, E])
        Wg = sb("Wg", [P, P])
        WgT = sb("WgT", [P, 2])
        W1 = sb("W1", [P, E * HID])
        W2 = sb("W2", [P, E * HC * P])
        Wr0 = sb("Wr0", [P, E])
        br0 = sb("br0", [P, E])
        b20 = sb("b20", [P, E * P])
        V1 = sb("V1", [P, E * P])
        V2 = sb("V2", [P, E * P])
        Vo = sb("Vo", [P, E * P])
        Wr1 = sb("Wr1", [P, E])
        br1 = sb("br1", [P, E])
        bo1 = sb("bo1", [E, P])
        names = ([("L0_ffn_b1", E * HC), ("L0_ffn_gamma", 1), ("L0_ffn_beta", 1)]
                 + [(f"L1_gnn_a{k}", 1) for k in range(4)]
                 + [(f"L1_ffn_{n}", E) for n in ("b1", "g1", "be1", "m1", "v1", "b2", "g2", "be2", "m2", "v2")])
        at, R = {}, 0
        for n, rows in names:
            at[n] = R
            R += rows
        prow = sb("prow", [R, P])
        pcol = sb("pcol", [P, R])
        bn = sb("bn", [P, 4 * E])

        MEAN, SPREAD, ROOT = (sb(n, [P, B * NT]) for n in ("MEAN", "SPREAD", "ROOT"))

        flag = sb("flag", [1, 1], I32)
        LP = 4
        LA = NT - LP
        ones_or_more = sb("ones_or_more", [P, N])
        excess = sb("excess", [P, B * LA])
        minus1 = sb("minus1", [P, 1])
        held = sem("held")
        x_first, x_second, x_rest, par_loaded = sem("x_first"), sem("x_second"), sem("x_rest"), sem("par_loaded")
        adj_loaded = [sem(f"adj_loaded{i}") for i in range(NT)]

        loads = [(W1[:, :].rearrange("d (e h) -> d e h", e=E), p["L0_ffn_W1"].rearrange("e d h -> d e h")),
                 (W2[:, :].rearrange("h (e c d) -> h e c d", e=E, c=HC),
                  p["L0_ffn_W2"].rearrange("e (c h) d -> h e c d", c=HC)),
                 (Wr0[:, :], p["L0_ffn_Wr"]),
                 (br0[:, :], p["L0_ffn_br"].rearrange("(o e) -> o e", o=1).to_broadcast([P, E])),
                 (b20[:, :], p["L0_ffn_b2"].rearrange("(o e) d -> o (e d)", o=1).to_broadcast([P, E * P])),
                 (V1[:, :].rearrange("d (e h) -> d e h", e=E), p["L1_ffn_W1"].rearrange("e d h -> d e h")),
                 (V2[:, :].rearrange("d (e h) -> d e h", e=E), p["L1_ffn_W2"].rearrange("e d h -> d e h")),
                 (Vo[:, :].rearrange("d (e h) -> d e h", e=E), p["L1_ffn_Wo"].rearrange("e d h -> d e h")),
                 (Wr1[:, :], p["L1_ffn_Wr"]),
                 (br1[:, :], p["L1_ffn_br"].rearrange("(o e) -> o e", o=1).to_broadcast([P, E])),
                 (bo1[:, :], p["L1_ffn_bo"])]
        for n, k in names:
            src = p[n]
            if n == "L0_ffn_b1":
                src = src.rearrange("e (c h) -> (e c) h", h=P)
            elif k == 1:
                src = src.rearrange("(o h) -> o h", o=1)
            loads.append((prow[at[n]:at[n] + k, :], src))

        with ExitStack() as ctx:
            A12 = sb("A12", [P, 2 * P], ctx=ctx)
            products = sb("products", [P, P], ctx=ctx)
            gat_loaded, cstep = sem("gat_loaded"), sem("const_step")
            block = ctx.enter_context(nc.Block())

            @block.sync
            def _(sp):
                sp.dma_start(X[:, 0:N].rearrange("p (t d) -> p t d", t=NT),
                             x[0].rearrange("(t p) d -> p t d", p=P)).then_inc(x_first, 16)
                sp.dma_start(Wg[:, :], p["L0_gnn_W"]).then_inc(gat_loaded, 16)
                sp.dma_start(A12[:, :], p["L0_gnn_a"].rearrange("k o -> o k").to_broadcast([P, 2 * P])
                             ).then_inc(gat_loaded, 16)

            @block.gpsimd
            def _(pool):
                c = Count()
                for tile, value in ((ident, 0.0), (identb, 0.0), (blockI, 0.0), (pick, 0.0), (ones3, 1.0),
                                    (minus_half, -0.5), (eps_all, EPS), (minus1, -1.0), (ones_or_more, 0.0),
                                    *((order[:, e:e + 1], float(E - e)) for e in range(E))):
                    nc.gpsimd.memset(tile[:, :], value).then_inc(cstep, 1)
                    c.next()
                pool.wait_ge(cstep, c.now())
                for tile, fill in ((ident, 1.0), (identb, 1.0), (blockI, BLOCKED)):
                    nc.gpsimd.affine_select(out=tile[:, :], in_=tile[:, :], compare_op=ALU.not_equal, fill=fill,
                                            base=0, pattern=[[-1, P]], channel_multiplier=1).then_inc(cstep, 1)
                    c.next()
                v = pick[:, :].rearrange("r (e m) -> r e m", e=E)
                for k in range(3):
                    nc.gpsimd.affine_select(out=v, in_=v, compare_op=ALU.not_equal, fill=1.0, base=-k * E,
                                            pattern=[[-1, E], [0, P]], channel_multiplier=1).then_inc(cstep, 1)
                    pool.wait_ge(cstep, c.next())

            @block.vector
            def _(dve):
                dve.wait_ge(gat_loaded, 32)
                for k in range(2):
                    nc.vector.tensor_tensor_reduce(products[:, :], Wg[:, :], A12[:, k * P:(k + 1) * P], 1.0, 0.0, ALU.mult,
                                                   ALU.add, WgT[:, k:k + 1]).then_inc(gat_loaded, 1)
                    dve.wait_ge(gat_loaded, 33 + k)

        def hold(eng, s, value):
            eng.wait_ge(s, value)
            eng.sem_inc(held, 1)

        def ln_stats(dve, b, ST, MV, stepsem, step, mv_ready):
            for t in range(NT):
                i = nc.vector.bn_stats(ST[:, t, :], X[:, bass.ds(b * N + t * P, P)])
            i.then_inc(stepsem, 1)
            hold(dve, stepsem, step.next())
            for t in range(NT):
                i = nc.vector.bn_aggr(MV[:, t, :], ST[:, t, :])
            i.then_inc(mv_ready, 1)

        def ln_root(pool, b, MV, RS, stepsem, step, mv_ready, rs_ready):
            pool.wait_ge(mv_ready, b + 1)
            nc.gpsimd.tensor_tensor(RS[:, 0, :], MV[:, :, 1], eps8, ALU.add).then_inc(stepsem, 1)
            pool.wait_ge(stepsem, step.next())
            nc.gpsimd.tensor_tensor(RS[:, 1, :], RS[:, 0, :], half8, ALU.pow).then_inc(rs_ready, 1)

        def ln_apply(dve, b, MV, rs, XN, xn_at, rs_ready, xn_ready):
            dve.wait_ge(rs_ready, b + 1)
            for t in range(NT):
                i = nc.vector.tensor_scalar(XN[:, bass.ds(xn_at + t * P, P)], X[:, bass.ds(b * N + t * P, P)],
                                            MV[:, t, 0:1], rs[:, t:t + 1], ALU.subtract, ALU.mult)
            i.then_inc(xn_ready, 1)

        with ExitStack() as ctx:
            def tile(name, shape, dt=F32):
                return sb(name, shape, dt, ctx)

            ADJ = tile("ADJ", [P, NT, N], I32)
            NM = tile("NM", [P, 2 * NT * N], BF16)
            ST, MV, RS = tile("ST", [P, NT, 6]), tile("MV", [P, NT, 2]), tile("RS", [P, 2, NT])
            XN, XNT = tile("XN", [P, N]), tile("XNT", [P, N])
            H = tile("H", [P, 2 * N])
            F2 = tile("F2", [P, 2 * NT])
            F3 = tile("F3", [P, NT, 3], BF16)
            FR = tile("FR", [P, NT])
            F1R = tile("F1R", [3, 2 * N], BF16)
            R4, Y, PR = tile("R4", [P, 2, N]), tile("Y", [P, 2, N]), tile("PR", [P, 2, N])
            MX, NMX, Z, RZ = tile("MX", [P, NT]), tile("NMX", [P, NT]), tile("Z", [P, NT]), tile("RZ", [P, NT])
            HS = tile("HS", [P, 2, P])
            RO, EX, EL = tile("RO", [P, N]), tile("EX", [P, N]), tile("EL", [P, N])
            T = [ctx.enter_context(nc.psum_tensor(f"T{i}", [P, N], F32)) for i in range(2)]
            O = ctx.enter_context(nc.psum_tensor("O", [P, N], F32))
            M = [ctx.enter_context(nc.psum_tensor(f"M{i}", [P, HALF], F32)) for i in range(2)]
            F1T = M[1][:, :].bitcast(BF16)

            mv_ready, rs_ready, xn_ready, dstep, pstep = (sem("a_" + n) for n in (
                "mv_ready", "rs_ready", "xn_ready", "dve_step", "pool_step"))
            xnt_ps, xnt_ready, h_ps, h_ready, elt_ps, x_added = ([sem(f"a_{n}{h}") for h in range(2)] for n in (
                "xnt_ps", "xnt_ready", "h_ps", "h_ready", "elt_ps", "x_added"))
            f12_ps, f2_ready, f1t_ps, f1r_ready, nm_ready, t_ready, r4_ready, y_ready, shift_ready, pr_ready = (
                sem("a_" + n) for n in ("f12_ps", "f2_ready", "f1t_ps", "f1r_ready", "nm_ready", "t_ready", "r4_ready",
                                        "y_ready", "shift_ready", "pr_ready"))
            MVN = tile("MVN", [P, NT, 2])
            spread_ready = sem("a_spread_ready")
            CL = tile("CL", [P, 2, N])
            seen = tile("seen", [P, N], BF16)
            pool_looked, act_looked, added = sem("a_pool_looked"), sem("a_act_looked"), sem("a_added")
            hs_ready, pv_done, ro_ready, ex_ready, el_ready = (sem("a_" + n) for n in (
                "hs_ready", "pv_done", "ro_ready", "ex_ready", "el_ready"))
            LAST = B - 1
            block = ctx.enter_context(nc.Block())

            @block.sync
            def _(sp):
                def load(b):
                    for t in range(NT):
                        if reached(b, 1):
                            hold(sp, nm_ready, (b - 1) * NT + t + 1)
                            if t < LP:
                                hold(sp, pool_looked, (b - 1) * LP + t + 1)
                            else:
                                hold(sp, act_looked, (b - 1) * LA + t - LP + 1)
                        sp.dma_start(ADJ[:, t, :], adj[bass.ds(b, 1), t * P:(t + 1) * P, :].rearrange("o p i -> (o p) i")
                                     ).then_inc(adj_loaded[t], 16)

                def load_x(b, loaded):
                    sp.dma_start(X[:, b * N:(b + 1) * N].rearrange("p (t d) -> p t d", t=NT),
                                 x[b].rearrange("(t p) d -> p t d", p=P)).then_inc(loaded, 16)

                load(0)
                load_x(1, x_second)
                for b in range(2, B):
                    load_x(b, x_rest)
                load(1)
                for dst, src in loads:
                    sp.dma_start(dst, src).then_inc(par_loaded, 16)
                with sp.Fori(2, B) as b:
                    load(b)

            @block.gpsimd
            def _(pool):
                step = Count()

                def look(b, t):
                    pool.wait_ge(adj_loaded[t], 16 * (b + 1))
                    if reached(b * LP + t, 2):
                        hold(pool, added, b * LP + t - 1)
                    nc.gpsimd.tensor_scalar(CL[:, t % 2, :], ADJ[:, t, :], 1048576.0, 1.0, ALU.min, ALU.max
                                            ).then_inc(pool_looked, 1)
                    pool.wait_ge(pool_looked, b * LP + t + 1)
                    wait(pool, added, b * LP + t)
                    nc.gpsimd.tensor_tensor(ones_or_more[:, :], ones_or_more[:, :], CL[:, t % 2, :], ALU.add
                                            ).then_inc(added, 1)

                def batch(b):
                    ln_root(pool, b, MV, RS, pstep, step, mv_ready, rs_ready)
                    for t in range(LP):
                        look(b, t)

                def root_next(b):
                    pool.wait_ge(spread_ready, b + 1)
                    nc.gpsimd.tensor_tensor(ROOT[:, bass.ds(b * NT, NT)], SPREAD[:, bass.ds(b * NT, NT)], half8, ALU.pow)

                for b in range(3):
                    batch(b)
                with pool.Fori(3, B) as b:
                    step.loop(b - 3, 1)
                    batch(b)
                    root_next(b - 3)
                step.end(B - 3)
                for b in range(B - 3, B):
                    root_next(b)

            @block.tensor
            def _(pe):
                def turn_x(b, h):
                    pe.wait_ge(xn_ready, b + 1)
                    for t in range(4):
                        i = pe.transpose(M[h][:, t * P:(t + 1) * P], XN[:, bass.ts(4 * h + t, P)], ident[:, :])
                    i.then_inc(xnt_ps[h], 1)

                def project(b, h):
                    pe.wait_ge(xnt_ready[h], b + 1)
                    for t in range(4):
                        i = pe.matmul(M[h][:, t * P:(t + 1) * P], XNT[:, bass.ts(4 * h + t, P)], Wg[:, :], start=True, stop=True)
                    i.then_inc(h_ps[h], 1)

                def scores(b):
                    pe.wait_ge(h_ready[0], b + 1)
                    for t in range(NT):
                        i = pe.matmul(M[0][:, 2 * t:2 * t + 2], XNT[:, t * P:(t + 1) * P], WgT[:, :], start=True, stop=True)
                    i.then_inc(f12_ps, 1)

                def turn_f1(b):
                    pe.wait_ge(f2_ready, b + 1)
                    pe.wait_ge(h_ready[1], b + 1)
                    for t in range(NT):
                        i = pe.transpose(F1T[0:3, t * P:(t + 1) * P], F3[:, t, :], identb[:, :])
                    i.then_inc(f1t_ps, 1)

                def turn_el(b, h, used):
                    pe.wait_ge(el_ready, b + 1)
                    pe.wait_ge((f2_ready, f1r_ready)[h], used)
                    for t in range(4):
                        i = pe.transpose(M[h][:, t * P:(t + 1) * P], EL[:, bass.ts(4 * h + t, P)], ident[:, :])
                    i.then_inc(elt_ps[h], 1)

                def logits(b, c):
                    if c == 0:
                        hold(pe, f1r_ready, b + 1)
                        pe.wait_ge(nm_ready, b * NT + NT)
                    wait(pe, y_ready, b * NT + c - 1)
                    t = T[c % 2]
                    for h in range(2):
                        for r in range(4 * h, 4 * h + 4):
                            pe.matmul(t[:, r * P:(r + 1) * P], NM[:, bass.ds((b % 2) * NT * N + r * N + c * P, P)],
                                      blockI[:, :], start=(r % 4 == 0), stop=False)
                        i = pe.matmul(t[:, h * HALF:(h + 1) * HALF], ones3[:, :],
                                      F1R[:, bass.ds((b % 2) * N + h * HALF, HALF)], start=False, stop=True)
                    i.then_inc(t_ready, 1)

                def attend(b, c):
                    pe.wait_ge(hs_ready, b * NT + c + 1)
                    if c == 0:
                        wait(pe, ex_ready, b)
                    for h in range(2):
                        i = pe.matmul(O[:, h * HALF:(h + 1) * HALF], HS[:, c % 2, :], PR[:, c % 2, h * HALF:(h + 1) * HALF],
                                      start=(c == 0), stop=(c == NT - 1))
                    i.then_inc(pv_done, 1)

                def batch(b, first, last):
                    for c in range(NT):
                        logits(b, c)
                        if c >= 2:
                            attend(b, c - 2)
                        elif not first:
                            attend(b - 1, NT - 2 + c)
                        for h in range(2):
                            if c == 2 and not last:
                                turn_x(b + 1, h)
                            if c == 3 and not last:
                                project(b + 1, h)
                            if c == 6 and not first:
                                turn_el(b - 1, h, b + 1 if last else b + 2)
                        if c == 4 and not last:
                            scores(b + 1)
                        if c == 5 and not last:
                            turn_f1(b + 1)

                for h in range(2):
                    turn_x(0, h)
                for h in range(2):
                    project(0, h)
                scores(0)
                turn_f1(0)
                batch(0, True, False)
                with pe.Fori(1, LAST) as b:
                    batch(b, False, False)
                batch(LAST, False, True)
                attend(LAST, NT - 2)
                attend(LAST, NT - 1)
                for h in range(2):
                    pe.wait_ge(x_added[h], LAST)
                    turn_el(LAST, h, B)

            @block.scalar
            def _(act):
                def copy_xnt(b, h):
                    act.wait_ge(xnt_ps[h], b + 1)
                    wait(act, f12_ps, b)
                    nc.scalar.copy(XNT[:, h * HALF:(h + 1) * HALF], M[h][:, :]).then_inc(xnt_ready[h], 1)

                def copy_h(b, h):
                    act.wait_ge(h_ps[h], b + 1)
                    wait(act, hs_ready, (b - 1) * NT)
                    nc.scalar.copy(H[:, bass.ds((b % 2) * N + h * HALF, HALF)], M[h][:, :]).then_inc(h_ready[h], 1)

                def relu(b, c):
                    act.wait_ge(t_ready, b * NT + c + 1)
                    if c == 0:
                        act.wait_ge(f2_ready, b + 1)
                    wait(act, y_ready, b * NT + c - 1)
                    nc.scalar.activation(R4[:, c % 2, :], T[c % 2][:, :], ACT.Relu, bias=F2[:, bass.ds((b % 2) * NT + c, 1)],
                                         scale=4.0).then_inc(r4_ready, 1)

                def prob(b, c):
                    act.wait_ge(shift_ready, b * NT + c + 1)
                    wait(act, pv_done, b * NT + c - 1)
                    nc.scalar.activation(PR[:, c % 2, :], Y[:, c % 2, :], ACT.Exp, bias=NMX[:, c:c + 1], scale=SLOPE,
                                         accum_out=Z[:, c:c + 1]).then_inc(pr_ready, 1)

                def look(b, t):
                    act.wait_ge(adj_loaded[t], 16 * (b + 1))
                    wait(act, act_looked, b * LA + t - LP)
                    nc.scalar.activation(seen[:, :], ADJ[:, t, :], ACT.Relu, bias=minus1[:, :],
                                         accum_out=excess[:, bass.ds(b * LA + t - LP, 1)]).then_inc(act_looked, 1)

                def outputs(b):
                    act.wait_ge(pv_done, b * NT + NT)
                    nc.scalar.activation(RO[:, :], O[:, :], ACT.Relu).then_inc(ro_ready, 1)
                    nc.scalar.activation(EX[:, :], O[:, :], ACT.Exp).then_inc(ex_ready, 1)

                def batch(b, first, last):
                    for c in range(NT):
                        relu(b, c)
                        if c > 0:
                            prob(b, c - 1)
                        elif not first:
                            prob(b - 1, NT - 1)
                        if c == 1 and not first:
                            outputs(b - 1)
                        if not last:
                            for h in range(2):
                                if c == 2:
                                    copy_xnt(b + 1, h)
                                if c == 3:
                                    copy_h(b + 1, h)
                            if c >= LP:
                                look(b + 1, c)

                for h in range(2):
                    copy_xnt(0, h)
                for h in range(2):
                    copy_h(0, h)
                for t in range(LP, NT):
                    look(0, t)
                batch(0, True, False)
                with act.Fori(1, LAST) as b:
                    batch(b, False, False)
                batch(LAST, False, True)
                prob(LAST, NT - 1)
                outputs(LAST)

            @block.vector
            def _(dve):
                step = Count()

                def convert(b, t):
                    dve.wait_ge(adj_loaded[t], 16 * (b + 1))
                    if t == 0:
                        wait(dve, t_ready, (b - 1) * NT)
                    nc.vector.tensor_scalar(NM[:, bass.ds((b % 2) * NT * N + t * N, N)], ADJ[:, t, :], 0.0, None,
                                            ALU.is_le).then_inc(nm_ready, 1)

                def parts(b):
                    dve.wait_ge(f12_ps, b + 1)
                    wait(dve, f1t_ps, b)
                    v = M[0][:, 0:2 * NT].rearrange("p (t k) -> p t k", k=2)
                    nc.vector.tensor_copy(F3[:, :, 0], v[:, :, 0]).then_inc(dstep, 1)
                    dve.wait_ge(dstep, step.next())
                    nc.vector.tensor_tensor(FR[:, :], v[:, :, 0], F3[:, :, 0], ALU.subtract).then_inc(dstep, 1)
                    dve.wait_ge(dstep, step.next())
                    nc.vector.tensor_copy(F3[:, :, 1], FR[:, :]).then_inc(dstep, 1)
                    dve.wait_ge(dstep, step.next())
                    nc.vector.tensor_tensor(F3[:, :, 2], FR[:, :], F3[:, :, 1], ALU.subtract)
                    wait(dve, r4_ready, (b - 1) * NT)
                    nc.vector.tensor_scalar(F2[:, bass.ds((b % 2) * NT, NT)], v[:, :, 1], 4.0, None, ALU.mult).then_inc(f2_ready, 1)

                def copy_f1(b):
                    dve.wait_ge(f1t_ps, b + 1)
                    wait(dve, t_ready, (b - 1) * NT)
                    nc.vector.tensor_copy(F1R[:, bass.ds((b % 2) * N, N)], F1T[0:3, 0:N]).then_inc(f1r_ready, 1)

                def shift(b, c):
                    if reached(b * NT + c, 2):
                        hold(dve, pr_ready, b * NT + c - 1)
                    hold(dve, r4_ready, b * NT + c + 1)
                    nc.vector.tensor_tensor_reduce(Y[:, c % 2, :], T[c % 2][:, :], R4[:, c % 2, :], 1.0, -3.0e38, ALU.add,
                                                   ALU.max, MX[:, c:c + 1]).then_inc(y_ready, 1)
                    dve.wait_ge(y_ready, b * NT + c + 1)
                    nc.vector.tensor_scalar(NMX[:, c:c + 1], MX[:, c:c + 1], -SLOPE, None, ALU.mult).then_inc(shift_ready, 1)

                def share(b, c):
                    dve.wait_ge(pr_ready, b * NT + c + 1)
                    nc.vector.reciprocal(RZ[:, c:c + 1], Z[:, c:c + 1]).then_inc(dstep, 1)
                    dve.wait_ge(dstep, step.next())
                    if c == 0:
                        dve.wait_ge(h_ready[1], b + 1)
                    wait(dve, pv_done, b * NT + c - 1)
                    nc.vector.tensor_scalar(HS[:, c % 2, :], H[:, bass.ds((b % 2) * N + c * P, P)], RZ[:, c:c + 1], None,
                                            ALU.mult).then_inc(hs_ready, 1)

                def elu(b):
                    dve.wait_ge(ex_ready, b + 1)
                    nc.vector.scalar_tensor_tensor(out=EL[:, :], in0=EX[:, :], scalar=1.0, in1=RO[:, :], op0=ALU.min,
                                                   op1=ALU.add).then_inc(el_ready, 1)

                def add(b):
                    for h in range(2):
                        dve.wait_ge(elt_ps[h], b + 1)
                        xb = X[:, bass.ds(b * N + h * HALF, HALF)]
                        nc.vector.scalar_tensor_tensor(out=xb, in0=M[h][:, :], scalar=-1.0, in1=xb, op0=ALU.add,
                                                       op1=ALU.add).then_inc(x_added[h], 1)

                def stats(b):
                    ln_stats(dve, b, ST, MV, dstep, step, mv_ready)

                def norm(b):
                    if reached(b, 1):
                        dve.wait_ge(xnt_ps[1], b)
                    ln_apply(dve, b, MV, RS[:, 1, :], XN, 0, rs_ready, xn_ready)

                def stats_next(b):
                    for h in range(2):
                        hold(dve, x_added[h], b + 1)
                    for t in range(NT):
                        i = nc.vector.bn_stats(ST[:, t, :], X[:, bass.ds(b * N + t * P, P)])
                    i.then_inc(dstep, 1)
                    hold(dve, dstep, step.next())
                    for t in range(NT):
                        i = nc.vector.bn_aggr(MVN[:, t, :], ST[:, t, :])
                    i.then_inc(dstep, 1)
                    hold(dve, dstep, step.next())
                    nc.vector.tensor_copy(MEAN[:, bass.ds(b * NT, NT)], MVN[:, :, 0])
                    nc.vector.tensor_scalar(SPREAD[:, bass.ds(b * NT, NT)], MVN[:, :, 1], 1.0 + EPS, EPS * EPS, ALU.mult, ALU.add
                                            ).then_inc(spread_ready, 1)

                def batch(b, first, second, last, last_but_one):
                    for c in range(NT):
                        if not last and c == 5:
                            parts(b + 1)
                        if not last and c == 6:
                            copy_f1(b + 1)
                        shift(b, c)
                        if c > 0:
                            share(b, c - 1)
                        elif not first:
                            share(b - 1, NT - 1)
                        if not first:
                            if c == 2 and not second:
                                stats_next(b - 2)
                            if c == 2:
                                elu(b - 1)
                            if c == 7:
                                add(b - 1)
                        if not last:
                            for t in ((0, 1), (), (2,), (3,), (4, 5), (6,), (7,), ())[c]:
                                convert(b + 1, t)
                            if c == 1:
                                norm(b + 1)
                            if c == 3 and not last_but_one:
                                stats(b + 2)

                dve.wait_ge(x_first, 16)
                stats(0)
                norm(0)
                dve.wait_ge(x_second, 16)
                stats(1)
                for t in range(4):
                    convert(0, t)
                parts(0)
                copy_f1(0)
                for t in range(4, NT):
                    convert(0, t)
                dve.wait_ge(x_rest, 16 * (B - 2))
                batch(0, True, False, False, False)
                batch(1, False, True, False, False)
                with dve.Fori(2, LAST - 1) as b:
                    step.loop(b - 2, 14)
                    batch(b, False, False, False, False)
                step.end(LAST - 3)
                batch(LAST - 1, False, False, False, True)
                batch(LAST, False, False, True, False)
                stats_next(LAST - 1)
                share(LAST, NT - 1)
                elu(LAST)
                add(LAST)
                stats_next(LAST)

        CHOSEN, SHARE, ROW = (sb(n, [P, B * 2 * NT]) for n in ("CHOSEN", "SHARE", "ROW"))
        ROW_I = sb("ROW_I", [P, B * 2 * NT], I32)
        NB = 2 * B * N // HALF + E - 1
        FROM, EXPERT = (sb(n, [1, NB], I32) for n in ("FROM", "EXPERT"))

        BLOCK = HALF
        SEATS = B * N + BLOCK
        SPARE = E * SEATS
        sorted_x = nc.dram_tensor("sorted_x", [E * SEATS + BLOCK, P], F32).ap()
        sorted_y = nc.dram_tensor("sorted_y", [NB * BLOCK, P], F32).ap()
        assert P % E == 0 and P // E * BLOCK >= B * N
        PER = P // E
        with ExitStack() as ctx:
            def tile(name, shape, dt=F32):
                return sb(name, shape, dt, ctx)

            XN = tile("bXN", [P, 2, N])
            XT = tile("bXT", [P, N])
            LG, Q, OH1, OH2, L2, SEAT = (tile(n, [P, NT, E]) for n in ("LG", "Q", "OH1", "OH2", "L2", "SEAT"))
            m1, m2, k1, dd, ex, s1 = (tile(n, [P, NT]) for n in ("m1", "m2", "k1", "dd", "ex", "s1"))
            CH = tile("CH", [P, NT + 1, E], BF16)
            NEXT = tile("NEXT", [P, E])
            AT = tile("AT", [P, 2, NT])
            AT_I = [tile(f"AT_I{q}", [P, 2 * NT], I32) for q in range(2)]
            before, ones = tile("before", [P, P], BF16), tile("ones", [P, P], BF16)
            zero = tile("zero", [P, BLOCK])
            mine, upto = tile("mine", [P, E]), tile("upto", [P, E])
            ip, ik = tile("ip", [P, 1], I32), tile("ik", [P, NB], I32)
            rowno, kth, hot = tile("rowno", [P, 1]), tile("kth", [P, NB]), tile("hot", [P, NB])
            pf, ef, used, got, rel = (tile(n, [P, 1]) for n in ("pf", "ef", "used", "got", "rel"))
            ubf, below = tile("ubf", [P, 1], BF16), tile("below", [P, E], BF16)
            pick8, shift8 = tile("pick8", [P, E]), tile("shift8", [P, E])
            tail = tile("tail", [1, E], I32)
            TMP = tile("TMP", [P, B * 2 * NT])
            M = [ctx.enter_context(nc.psum_tensor(f"bM{i}", [P, HALF], F32)) for i in range(2)]
            L, RK, TB, TC = (ctx.enter_context(nc.psum_tensor(n, [P, HALF], F32)) for n in ("bL", "bRK", "bTB", "bTC"))
            (xn_ready, xt_ps, xt_ready, lg_ps, dd_ready, ex_ready, ch_ready, rk_ps, at_ready, dstep, istep, masks,
             used_ready, rank_ps, hot_ready, table_ps, tail_ready, tails, zero_ready,
             before_ready) = (sem("b_" + n) for n in (
                 "xn_ready", "xt_ps", "xt_ready", "lg_ps", "dd_ready", "ex_ready", "ch_ready", "rk_ps", "at_ready",
                 "dve_step", "pool_step", "masks", "used_ready", "rank_ps", "hot_ready", "table_ps", "tail_ready", "tails",
                 "zero_ready", "before_ready"))
            sent = [sem(f"b_sent{q}") for q in range(2)]
            var, half, diff, prod = (tile(n, [P, 2 * E]) for n in ("bn_var", "bn_half", "bn_diff", "bn_prod"))
            lcol, lone, most = tile("lcol", [P, 1]), tile("lone", [1, 1]), tile("most", [P, 2])
            ps, pl = (ctx.enter_context(nc.psum_tensor(n, [P, HALF], F32)) for n in ("ps_par", "ps_largest"))
            lcol_ready, lrow_ps, pcol_ps, pcol_ready, var_ready, half_ready = (sem(n) for n in (
                "lcol_ready", "lrow_ps", "pcol_ps", "pcol_ready", "var_ready", "half_ready"))
            block = ctx.enter_context(nc.Block())
            EACH = 16 * 2 * NT

            @block.sync
            def _(sp):
                sp.wait_ge(zero_ready, 1)
                v = zero[:, :].rearrange("p (t d) -> p t d", d=P)
                sp.dma_start(sorted_x[SPARE:SPARE + BLOCK, :].rearrange("(p t) d -> p t d", p=P), v).then_inc(tails, 16)
                sp.wait_ge(tail_ready, 1)
                for e in range(E):
                    row = sp.value_load(tail[0:1, e:e + 1], min_val=e * SEATS, max_val=e * SEATS + B * N)
                    sp.dma_start(sorted_x[bass.ds(row, BLOCK), :].rearrange("(p t) d -> p t d", p=P), v).then_inc(tails, 16)
                sp.wait_ge(tails, 16 * (E + 1))

            @block.gpsimd
            def _(pool):
                step = Count()

                def op(f, *a, **k):
                    f(*a, **k).then_inc(istep, 1)
                    pool.wait_ge(istep, step.next())

                g = nc.gpsimd
                g.memset(zero[:, :], 0.0).then_inc(zero_ready, 1)
                g.memset(half[:, :], -0.5).then_inc(half_ready, 1)
                op(g.memset, ones[:, :], 1.0)
                g.affine_select(out=before[:, :], in_=ones[:, :], compare_op=ALU.is_gt, fill=0.0, base=0,
                                pattern=[[1, P]], channel_multiplier=-1).then_inc(before_ready, 1)
                op(g.memset, mine[:, :], 1.0)
                op(g.affine_select, out=upto[:, :], in_=mine[:, :], compare_op=ALU.is_ge, fill=0.0, base=-1,
                   pattern=[[PER, E]], channel_multiplier=-1)
                op(g.affine_select, out=mine[:, :], in_=mine[:, :], compare_op=ALU.is_ge, fill=0.0, base=0,
                   pattern=[[-PER, E]], channel_multiplier=1)
                op(g.affine_select, out=mine[:, :], in_=mine[:, :], compare_op=ALU.is_ge, fill=0.0, base=PER - 1,
                   pattern=[[PER, E]], channel_multiplier=-1)
                op(g.iota, ip[:, :], [[0, 1]], base=0, channel_multiplier=1)
                op(g.iota, ik[:, :], [[1, NB]], base=0, channel_multiplier=0)
                g.tensor_copy(pf[:, :], ip[:, :]).then_inc(masks, 1)
                g.tensor_copy(kth[:, :], ik[:, :]).then_inc(masks, 1)
                pool.wait_ge(half_ready, 1)
                pool.wait_ge(var_ready, 2)
                g.tensor_tensor(var[:, :], var[:, :], half[:, :], ALU.pow).then_inc(half_ready, 1)

                def send(i, q):
                    hold(pool, at_ready, 2 * i + q + 1)
                    for k in range(2):
                        for t in range(NT):
                            nc.gpsimd.indirect_dma_start(
                                sorted_x, bass.IndirectOffsetOnAxis(ap=AT_I[q][:, k * NT + t:k * NT + t + 1], axis=0),
                                XN[:, q, t * P:(t + 1) * P], None).then_inc(sent[q], 16)

                with pool.Fori(0, B // 2) as i:
                    for q in range(2):
                        send(i, q)
                for q in range(2):
                    pool.wait_ge(sent[q], B // 2 * EACH)

            @block.tensor
            def _(pe):
                def route(b, q):
                    hold(pe, xn_ready, b + 1)
                    for h in range(2):
                        for t in range(4):
                            i = pe.transpose(M[h][:, t * P:(t + 1) * P], XN[:, q, (4 * h + t) * P:(4 * h + t + 1) * P], ident[:, :])
                        i.then_inc(xt_ps, 1)
                    for h in range(2):
                        hold(pe, xt_ready, 2 * b + h + 1)
                        for t in range(4 * h, 4 * h + 4):
                            i = pe.matmul(L[:, t * E:(t + 1) * E], XT[:, t * P:(t + 1) * P], Wr0[:, :], start=True, stop=True)
                    i.then_inc(lg_ps, 1)

                def rank(b):
                    hold(pe, ch_ready, b + 1)
                    pe.matmul(RK[:, 0:(NT + 1) * E], before[:, :], CH[:, :, :], start=True, stop=False)
                    for t in range(NT):
                        later = NT - t
                        i = pe.matmul(RK[:, (t + 1) * E:(NT + 1) * E].rearrange("p (l e) -> p l e", e=E), ones[:, :],
                                      CH[:, t:t + 1, :].to_broadcast([P, later, E]), start=False, stop=(t == NT - 1))
                    i.then_inc(rk_ps, 1)

                pe.wait_ge(par_loaded, 16 * len(loads))
                pe.transpose(ps[:, 0:R], prow[:, :], ident[0:R, 0:R]).then_inc(pcol_ps, 1)
                pe.wait_ge(before_ready, 1)
                with pe.Fori(0, B // 2) as i:
                    for q in range(2):
                        route(2 * i + q, q)
                        rank(2 * i + q)
                pe.wait_ge(used_ready, 1)
                pe.matmul(TB[:, 0:1], before[:, :], ubf[:, :], start=True, stop=True)
                pe.matmul(TB[:, 1:1 + E], ones[:, :], below[:, :], start=True, stop=True).then_inc(rank_ps, 1)
                pe.wait_ge(hot_ready, 1)
                pe.matmul(TC[0:1, 0:NB], rel[:, :], hot[:, :], start=True, stop=True)
                pe.matmul(TC[0:1, NB:2 * NB], ef[:, :], hot[:, :], start=True, stop=True).then_inc(table_ps, 1)
                pe.wait_ge(lcol_ready, 1)
                pe.transpose(pl[0:1, 0:P], lcol[:, :], ident[:, :]).then_inc(lrow_ps, 1)

            @block.scalar
            def _(act):
                act.wait_ge(pcol_ready, 1)
                with act.Fori(0, B) as b:
                    for h in range(2):
                        act.wait_ge(xt_ps, 2 * b + h + 1)
                        nc.scalar.activation(XT[:, h * HALF:(h + 1) * HALF], M[h][:, :], ACT.Identity,
                                             bias=pcol[:, at["L0_ffn_beta"]:at["L0_ffn_beta"] + 1],
                                             scale=pcol[:, at["L0_ffn_gamma"]:at["L0_ffn_gamma"] + 1]).then_inc(xt_ready, 1)
                    act.wait_ge(dd_ready, b + 1)
                    nc.scalar.activation(ex[:, :], dd[:, :], ACT.Exp).then_inc(ex_ready, 1)

            @block.vector
            def _(dve):
                step = Count()
                v = nc.vector

                def op(f, *a, **k):
                    f(*a, **k).then_inc(dstep, 1)
                    hold(dve, dstep, step.next())

                def wide(t):
                    return t.unsqueeze(2).to_broadcast([P, NT, E])

                def norm(i, q, again):
                    if again:
                        hold(dve, sent[q], i * EACH)
                    for t in range(NT):
                        at_ = (2 * i + q) * NT + t
                        n = v.tensor_scalar(XN[:, q, t * P:(t + 1) * P], X[:, bass.ds(at_ * P, P)], MEAN[:, bass.ds(at_, 1)],
                                            ROOT[:, bass.ds(at_, 1)], ALU.subtract, ALU.mult)
                    n.then_inc(xn_ready, 1)

                def first_max(logits, top, onehot, number):
                    op(v.tensor_reduce, top[:, :], logits, AX_X, ALU.max)
                    op(v.tensor_tensor, Q[:, :, :], logits, wide(top[:, :]), ALU.is_equal)
                    op(v.tensor_tensor, Q[:, :, :], Q[:, :, :], order[:, :].unsqueeze(1).to_broadcast([P, NT, E]), ALU.mult)
                    op(v.tensor_reduce, k1[:, :], Q[:, :, :], AX_X, ALU.max)
                    v.tensor_copy(number, k1[:, :])
                    op(v.tensor_tensor, onehot, Q[:, :, :], wide(k1[:, :]), ALU.is_equal)

                def choose(b):
                    hold(dve, lg_ps, b + 1)
                    op(v.tensor_tensor, LG[:, :, :], L[:, 0:NT * E].rearrange("p (t e) -> p t e", e=E),
                       br0[:, :].unsqueeze(1).to_broadcast([P, NT, E]), ALU.add)
                    first_max(LG[:, :, :], m1, OH1[:, :, :], CHOSEN[:, bass.ds(b * 2 * NT, NT)])
                    op(v.scalar_tensor_tensor, out=L2[:, :, :], in0=OH1[:, :, :], scalar=-1e30, in1=LG[:, :, :],
                       op0=ALU.mult, op1=ALU.add)
                    first_max(L2[:, :, :], m2, OH2[:, :, :], CHOSEN[:, bass.ds(b * 2 * NT + NT, NT)])
                    v.tensor_tensor(CH[:, 0:NT, :], OH1[:, :, :], OH2[:, :, :], ALU.add).then_inc(ch_ready, 1)
                    v.tensor_tensor(dd[:, :], m2[:, :], m1[:, :], ALU.subtract).then_inc(dd_ready, 1)

                def seat(b, q):
                    hold(dve, rk_ps, b + 1)
                    op(v.tensor_tensor, SEAT[:, :, :], RK[:, 0:NT * E].rearrange("p (t e) -> p t e", e=E),
                       NEXT[:, :].unsqueeze(1).to_broadcast([P, NT, E]), ALU.add)
                    op(v.tensor_tensor, NEXT[:, :], NEXT[:, :], RK[:, NT * E:(NT + 1) * E], ALU.add)
                    for k, oh in enumerate((OH1, OH2)):
                        op(v.tensor_tensor, Q[:, :, :], SEAT[:, :, :], oh[:, :, :], ALU.mult)
                        op(v.tensor_reduce, AT[:, k, :], Q[:, :, :], AX_X, ALU.add)
                    v.tensor_copy(ROW[:, bass.ds(b * 2 * NT, 2 * NT)], AT[:, :, :].rearrange("p k t -> p (k t)"))
                    v.tensor_copy(AT_I[q][:, :], AT[:, :, :].rearrange("p k t -> p (k t)")).then_inc(at_ready, 1)
                    hold(dve, ex_ready, b + 1)
                    op(v.tensor_scalar, s1[:, :], ex[:, :], 1.0, None, ALU.add)
                    op(v.reciprocal, s1[:, :], s1[:, :])
                    v.tensor_copy(SHARE[:, bass.ds(b * 2 * NT, NT)], s1[:, :])
                    op(v.tensor_tensor, SHARE[:, bass.ds(b * 2 * NT + NT, NT)], ex[:, :], s1[:, :], ALU.mult)

                def tables():
                    v.tensor_copy(tail[:, :], NEXT[0:1, :]).then_inc(tail_ready, 1)
                    dve.wait_ge(masks, 2)
                    op(v.tensor_tensor, pick8[:, :], mine[:, :], order[:, :], ALU.mult)
                    op(v.tensor_reduce, got[:, :], pick8[:, :], AX_X, ALU.add)
                    op(v.tensor_scalar, ef[:, :], got[:, :], -1.0, float(E), ALU.mult, ALU.add)
                    op(v.tensor_scalar, rowno[:, :], ef[:, :], float(SEATS - PER * BLOCK), None, ALU.mult)
                    op(v.scalar_tensor_tensor, out=rowno[:, :], in0=pf[:, :], scalar=float(BLOCK), in1=rowno[:, :],
                       op0=ALU.mult, op1=ALU.add)
                    op(v.tensor_tensor, pick8[:, :], mine[:, :], NEXT[:, :], ALU.mult)
                    op(v.tensor_reduce, got[:, :], pick8[:, :], AX_X, ALU.add)
                    op(v.tensor_tensor, used[:, :], got[:, :], rowno[:, :], ALU.is_gt)
                    op(v.tensor_copy, ubf[:, :], used[:, :])
                    v.tensor_scalar(below[:, :], upto[:, :], used[:, :], None, ALU.mult).then_inc(used_ready, 1)
                    dve.wait_ge(rank_ps, 1)
                    op(v.tensor_copy, got[:, :], TB[:, 0:1])
                    v.tensor_scalar(rel[:, :], rowno[:, :], -float(SPARE), None, ALU.add)
                    v.tensor_scalar(hot[:, :], kth[:, :], got[:, :], used[:, :], ALU.is_equal, ALU.mult).then_inc(hot_ready, 1)
                    op(v.tensor_scalar, pick8[:, :], TB[:, 1:1 + E], float(BLOCK), -float(SPARE), ALU.mult, ALU.add)
                    op(v.scalar_tensor_tensor, out=shift8[:, :], in0=order[:, :], scalar=float(SEATS), in1=pick8[:, :],
                       op0=ALU.mult, op1=ALU.add)
                    for e in range(E):
                        op(v.tensor_scalar, TMP[:, :], CHOSEN[:, :], float(E - e), shift8[:, e:e + 1], ALU.is_equal, ALU.mult)
                        op(v.tensor_tensor, ROW[:, :], ROW[:, :], TMP[:, :], ALU.add)
                    v.tensor_copy(ROW_I[:, :], ROW[:, :])
                    dve.wait_ge(table_ps, 1)
                    v.tensor_scalar(FROM[:, :], TC[0:1, 0:NB], float(SPARE), None, ALU.add)
                    v.tensor_copy(EXPERT[:, :], TC[0:1, NB:2 * NB])

                def pair(i, first, last):
                    choose(2 * i)
                    seat(2 * i, 0)
                    norm(i, 1, not first)
                    choose(2 * i + 1)
                    seat(2 * i + 1, 1)
                    if not last:
                        norm(i + 1, 0, True)

                def largest():
                    v.tensor_reduce(most[:, 0:1], ones_or_more[:, :], AX_X, ALU.max)
                    op(v.tensor_reduce, most[:, 1:2], excess[:, :], AX_X, ALU.max)
                    v.scalar_tensor_tensor(out=lcol[:, :], in0=most[:, 0:1], scalar=-float(B * LP), in1=most[:, 1:2],
                                           op0=ALU.add, op1=ALU.max).then_inc(lcol_ready, 1)
                    dve.wait_ge(lrow_ps, 1)
                    op(v.tensor_reduce, lone[:, :], pl[0:1, 0:P], AX_X, ALU.max)
                    v.tensor_scalar(flag[:, :], lone[:, :], 0.0, None, ALU.is_gt)

                def col(n):
                    return pcol[:, at[f"L1_ffn_{n}"]:at[f"L1_ffn_{n}"] + E]

                def batch_norms():
                    dve.wait_ge(half_ready, 2)
                    for k in range(2):
                        u, w = diff[:, k * E:(k + 1) * E], prod[:, k * E:(k + 1) * E]
                        s, t = bn[:, 2 * k * E:(2 * k + 1) * E], bn[:, (2 * k + 1) * E:(2 * k + 2) * E]
                        op(v.tensor_tensor, u, col(f"b{k + 1}"), col(f"m{k + 1}"), ALU.subtract)
                        op(v.tensor_tensor, s, col(f"g{k + 1}"), var[:, k * E:(k + 1) * E], ALU.mult)
                        op(v.tensor_tensor, w, u, s, ALU.mult)
                        v.tensor_tensor(t, w, col(f"be{k + 1}"), ALU.add)

                norm(0, 0, False)
                dve.wait_ge(pcol_ps, 1)
                v.tensor_copy(pcol[:, :], ps[:, 0:R]).then_inc(pcol_ready, 1)
                dve.wait_ge(pcol_ready, 1)
                for k in range(2):
                    v.tensor_scalar(var[:, k * E:(k + 1) * E], col(f"v{k + 1}"), BN_EPS, None, ALU.add).then_inc(var_ready, 1)
                for e in range(E):
                    v.memset(NEXT[:, e:e + 1], float(e * SEATS))
                op(v.memset, CH[:, :, :], 0.0)
                pair(0, True, False)
                with dve.Fori(1, B // 2 - 1) as i:
                    step.loop(i - 1, 2 * (12 + 9))
                    pair(i, False, False)
                step.end(B // 2 - 2)
                pair(B // 2 - 1, False, True)
                tables()
                largest()
                batch_norms()

        with ExitStack() as ctx:
            def tile(name, shape, dt=F32):
                return sb(name, shape, dt, ctx)

            XB, YB = tile("XB", [P, 2, 4, P]), tile("YB", [P, 2, 4, P])
            XT = tile("bbXT", [P, 2, BLOCK])
            G = tile("G", [P, 2, HC, BLOCK])
            W1E, W2E, B1E = tile("W1E", [P, 2, HID]), tile("W2E", [P, 2, HC * P]), tile("B1E", [P, 2, HC])
            U, Y, M = ([ctx.enter_context(nc.psum_tensor(f"b{n}{i}", [P, HALF], F32)) for i in range(2)]
                       for n in ("U", "Y", "N"))
            turned, xt_ready, w1_ready, w2_ready, u_ready, g_ready, y_ready, yb_ready = (sem("bb_" + n) for n in (
                "turned", "xt_ready", "w1_ready", "w2_ready", "u_ready", "g_ready", "y_ready", "yb_ready"))
            xb_loaded, yb_stored = ([sem(f"bb_{n}{q}") for q in range(2)] for n in ("xb_loaded", "yb_stored"))
            assert HC == 2 and NB % 2 == 1
            block = ctx.enter_context(nc.Block())

            def blocks(eng, do):
                for k in range(3):
                    do(k, k // 2, k % 2, False)
                with eng.Fori(2, (NB - 3) // 2 + 1) as i:
                    do(2 * i - 1, i - 1, 1, False)
                    do(2 * i, i, 0, False)
                do(NB - 2, (NB - 2) // 2, 1, False)
                do(NB - 1, (NB - 1) // 2, 0, True)

            @block.sync
            def _(sp):
                def load(k, i, q, last):
                    if reached(k, 2):
                        hold(sp, turned, k - 1)
                    row = sp.value_load(FROM[0:1, bass.ds(k, 1)], min_val=0, max_val=SPARE)
                    sp.dma_start(XB[:, q, :, :], sorted_x[bass.ds(row, BLOCK), :].rearrange("(t p) d -> p t d", p=P)
                                 ).then_inc(xb_loaded[q], 16)

                blocks(sp, load)

            @block.gpsimd
            def _(pool):
                def store(k, i, q, last):
                    hold(pool, yb_ready, k + 1)
                    pool.dma_start(sorted_y[bass.ds(k * BLOCK, BLOCK), :].rearrange("(t p) d -> p t d", p=P), YB[:, q, :, :]
                                   ).then_inc(yb_stored[q], 16)

                blocks(pool, store)
                for q in range(2):
                    pool.wait_ge(yb_stored[q], 16 * ((NB + 1 - q) // 2))

            @block.tensor
            def _(pe):
                def turn(i, q):
                    hold(pe, xb_loaded[q], 16 * (i + 1))
                    for t in range(4):
                        j = pe.transpose(M[q][:, t * P:(t + 1) * P], XB[:, q, t, :], ident[:, :])
                    j.then_inc(turned, 1)

                def out(k, q):
                    hold(pe, g_ready, 2 * k + 2)
                    hold(pe, w2_ready, k + 1)
                    if reached(k, 2):
                        hold(pe, yb_ready, k - 1)
                    for c in range(HC):
                        for t in range(4):
                            j = pe.matmul(Y[q][:, t * P:(t + 1) * P], G[:, q, c, t * P:(t + 1) * P], W2E[:, q, c * P:(c + 1) * P],
                                          start=(c == 0 and t == 0), stop=(c == HC - 1 and t == 3))
                    j.then_inc(y_ready, 1)

                def work(k, i, q, last):
                    hold(pe, xt_ready, k + 1)
                    hold(pe, w1_ready, k + 1)
                    for c in range(HC):
                        if reached(k, 1):
                            hold(pe, g_ready, 2 * k - 1 + c)
                        pe.matmul(U[c][:, :], W1E[:, q, c * P:(c + 1) * P], XT[:, q, :], start=True, stop=True
                                  ).then_inc(u_ready, 1)
                    if not last:
                        turn(i + q, 1 - q)
                    if reached(k, 1):
                        out(k - 1, 1 - q)

                turn(0, 0)
                blocks(pe, work)
                out(NB - 1, (NB - 1) % 2)

            @block.scalar
            def _(act):
                def copy_xt(k, q):
                    act.wait_ge(turned, k + 1)
                    nc.scalar.activation(XT[:, q, :], M[q][:, :], ACT.Identity,
                                         bias=pcol[:, at["L0_ffn_beta"]:at["L0_ffn_beta"] + 1],
                                         scale=pcol[:, at["L0_ffn_gamma"]:at["L0_ffn_gamma"] + 1]).then_inc(xt_ready, 1)

                def work(k, i, q, last):
                    for c in range(HC):
                        act.wait_ge(u_ready, 2 * k + c + 1)
                        if c == 0 and reached(k, 2):
                            act.wait_ge(y_ready, k - 1)
                        nc.scalar.activation(G[:, q, c, :], U[c][:, :], ACT.Gelu, bias=B1E[:, q, c:c + 1]).then_inc(g_ready, 1)
                    if not last:
                        copy_xt(k + 1, 1 - q)

                copy_xt(0, 0)
                blocks(act, work)

            @block.vector
            def _(dve):
                def expert(k):
                    return dve.value_load(EXPERT[0:1, bass.ds(k, 1)], min_val=0, max_val=E - 1)

                def first_weights(k, q):
                    if reached(k, 2):
                        hold(dve, g_ready, 2 * k - 2)
                    e = expert(k)
                    nc.vector.tensor_copy(B1E[:, q, :], pcol[:, bass.ds(e * HC + at["L0_ffn_b1"], HC)])
                    nc.vector.tensor_copy(W1E[:, q, :], W1[:, bass.ds(e * HID, HID)]).then_inc(w1_ready, 1)

                def second_weights(k, q):
                    e = expert(k)
                    nc.vector.tensor_copy(W2E[:, q, :], W2[:, bass.ds(e * HC * P, HC * P)]).then_inc(w2_ready, 1)

                def finish(k, i, q):
                    e = expert(k)
                    hold(dve, y_ready, k + 1)
                    if reached(k, 2):
                        hold(dve, yb_stored[q], 16 * i)
                    nc.vector.tensor_tensor(YB[:, q, :, :], Y[q][:, :].rearrange("p (t d) -> p t d", d=P),
                                            b20[:, bass.ds(e * P, P)].unsqueeze(1).to_broadcast([P, 4, P]), ALU.add
                                            ).then_inc(yb_ready, 1)

                def work(k, i, q, last):
                    if not last:
                        first_weights(k + 1, 1 - q)
                    if reached(k, 1):
                        finish(k - 1, i + q - 1, 1 - q)
                    if not last:
                        second_weights(k + 1, 1 - q)

                first_weights(0, 0)
                second_weights(0, 0)
                blocks(dve, work)
                finish(NB - 1, (NB - 1) // 2, 0)

        shared_sems = {}

        def either(name):
            if name not in shared_sems:
                shared_sems[name] = sem("c_" + name)
            return shared_sems[name]

        def edge_attention(kinds, ctx, pre):
            def tile(name, shape, dt=F32):
                return sb(pre + name, shape, dt, ctx)

            ADJ = tile("ADJ", [P, 4, N], I32)
            NK = tile("NK", [P, 2, kinds, N], BF16)
            AK = tile("AK", [P, 2, kinds, P])
            ST, MV, RS = tile("ST", [P, NT, 6]), tile("MV", [P, NT, 2]), tile("RS", [P, 2, NT])
            MVN, RSN = tile("MVN", [P, NT, 2]), tile("RSN", [P, 2, NT])
            YG = W1[:, :].rearrange("p (k d) -> p k d", d=P)
            ROW_B = tile("ROW_B", [P, 2 * NT], I32)
            XN = tile("XN", [P, N])
            XNN = b20
            XB, XT = W2, tile("XT", [P, 2 * N])
            ACC = tile("ACC", [P, 2, N]) if kinds > 1 else None
            R4, Y, PR, PT = (tile(n, [P, 2, N]) for n in ("R4", "Y", "PR", "PT"))
            MX, NMX, Z, RZ = (tile(n, [P, 2]) for n in ("MX", "NMX", "Z", "RZ"))
            T = [ctx.enter_context(nc.psum_tensor(f"{pre}T{i}", [P, N], F32)) for i in range(2)]
            TP = [ctx.enter_context(nc.psum_tensor(f"{pre}TP{i}", [P, HALF], F32)) for i in range(2)]
            O = ctx.enter_context(nc.psum_tensor(pre + "O", [P, HALF], F32))
            M = ctx.enter_context(nc.psum_tensor(pre + "M", [P, HALF], F32))
            (mv_ready, rs_ready, xn_ready, dstep, pstep, xt_ps, xt_ready, made, t_ready, t_read, acc_ready, r4_ready, y_ready,
             shift_ready, pr_ready, pv_done, x_added, xb_ready, next_mv_ready, next_rs_ready, next_xn_ready, nt_ps, nt_ready,
             ft_ready, row_ready, joined) = (either(n) for n in (
                 "mv_ready", "rs_ready", "xn_ready", "dve_step", "pool_step", "xt_ps", "xt_ready", "made", "t_ready",
                 "t_read", "acc_ready", "r4_ready", "y_ready", "shift_ready", "pr_ready", "pv_done", "x_added", "xb_ready",
                 "next_mv_ready", "next_rs_ready", "next_xn_ready", "nt_ps", "nt_ready", "ft_ready", "row_ready",
                 "joined"))
            tp_ps, tp_read = ([either(f"{n}{h}") for h in range(2)] for n in ("tp_ps", "tp_read"))
            gathered = [either(f"gathered{k}") for k in range(2)]
            loaded = [either(f"adj_loaded{i}") for i in range(4)]
            K = kinds
            LAST = B - 1
            block = ctx.enter_context(nc.Block())

            @block.sync
            def _(sp):
                def load(b):
                    for t in range(NT):
                        wait(sp, made, b * NT + t - 3)
                        sp.dma_start(ADJ[:, t % 4, :], adj[bass.ds(b, 1), t * P:(t + 1) * P, :].rearrange("o p i -> (o p) i")
                                     ).then_inc(loaded[t % 4], 16)
                load(0)
                with sp.Fori(1, B) as b:
                    load(b)

            @block.gpsimd
            def _(pool):
                step = Count()

                def batch(b):
                    ln_root(pool, b, MV, RS, pstep, step, mv_ready, rs_ready)
                    pool.wait_ge(xn_ready, b + 1)
                    nc.gpsimd.tensor_copy(XB[:, bass.ds((b % 2) * N, N)], XN[:, :]).then_inc(xb_ready, 1)

                def root_next(b):
                    ln_root(pool, b, MVN, RSN, pstep, step, next_mv_ready, next_rs_ready)

                def feature(b):
                    pool.wait_ge(nt_ready, 2 * b + 2)
                    hold(pool, ft_ready, b + 1)
                    nc.gpsimd.tensor_tensor(FT[:, :], FT[:, :], XTN[:, bass.ds(b * N, N)], ALU.add).then_inc(ft_ready, 1)

                def gather(b):
                    if reached(b, 1):
                        hold(pool, joined, 2 * b)
                    nc.gpsimd.tensor_copy(ROW_B[:, :], ROW_I[:, bass.ds(b * 2 * NT, 2 * NT)]).then_inc(row_ready, 1)
                    hold(pool, row_ready, b + 1)
                    for t in range(2 * NT):
                        nc.gpsimd.indirect_dma_start(YG[:, t, :], None, sorted_y,
                                                     bass.IndirectOffsetOnAxis(ap=ROW_B[:, t:t + 1], axis=0)
                                                     ).then_inc(gathered[t // NT], 16)

                gather(0)
                nc.gpsimd.memset(FT[:, :], 0.0).then_inc(ft_ready, 1)
                batch(0)
                gather(1)
                batch(1)
                gather(2)
                with pool.Fori(2, B - 1) as b:
                    step.loop(b - 2, 2)
                    root_next(b - 2)
                    batch(b)
                    gather(b + 1)
                    feature(b - 2)
                step.end(B - 3)
                root_next(B - 3)
                batch(B - 1)
                feature(B - 3)
                for b in (B - 2, B - 1):
                    root_next(b)
                    feature(b)
                pool.wait_ge(ft_ready, B + 1)

            @block.tensor
            def _(pe):
                def turn_x(b, h, second=False):
                    pe.wait_ge(xn_ready, b + 1)
                    if h == 1 or second:
                        hold(pe, xt_ready, 2 * b + h)
                    elif reached(b, 2):
                        hold(pe, nt_ready, 2 * b - 2)
                    for t in range(4):
                        i = pe.transpose(M[:, t * P:(t + 1) * P], XN[:, bass.ts(4 * h + t, P)], ident[:, :])
                    i.then_inc(xt_ps, 1)

                def turn_next(b, h, turned):
                    pe.wait_ge(next_xn_ready, b + 1)
                    if h == 0:
                        hold(pe, xt_ready, turned)
                    else:
                        hold(pe, nt_ready, 2 * b + 1)
                    for t in range(4):
                        i = pe.transpose(M[:, t * P:(t + 1) * P], XNN[:, bass.ts(4 * h + t, P)], ident[:, :])
                    i.then_inc(nt_ps, 1)

                def scores(b, r):
                    g = b * NT + r
                    hold(pe, made, g + 1)
                    for k in range(K):
                        t = T[k % 2] if K > 1 else T[r % 2]
                        if reached(g * K + k, 2):
                            hold(pe, t_read, g * K + k - 1)
                        for h in range(2):
                            pe.matmul(t[:, h * HALF:(h + 1) * HALF], AK[:, r % 2, k, :],
                                      XT[:, bass.ds((b % 2) * N + h * HALF, HALF)], start=True, stop=False)
                            i = pe.matmul(t[:, h * HALF:(h + 1) * HALF], blockI[:, :], NK[:, r % 2, k, h * HALF:(h + 1) * HALF],
                                          start=False, stop=True)
                        i.then_inc(t_ready, 1)

                def turn_p(b, r):
                    pe.wait_ge(pr_ready, b * NT + r + 1)
                    for h in range(2):
                        wait(pe, tp_read[h], b * NT + r)
                        for c in range(4):
                            i = pe.transpose(TP[h][:, c * P:(c + 1) * P], PR[:, r % 2, (4 * h + c) * P:(4 * h + c + 1) * P],
                                             ident[:, :])
                        i.then_inc(tp_ps[h], 1)

                def attend(b, r):
                    if r == 0:
                        hold(pe, xb_ready, b + 1)
                    hold(pe, x_added, b * NT + r)
                    for h in range(2):
                        hold(pe, tp_read[h], b * NT + r + 1)
                        for c in range(4 * h, 4 * h + 4):
                            i = pe.matmul(O[:, 0:P], PT[:, r % 2, c * P:(c + 1) * P], XB[:, bass.ds((b % 2) * N + c * P, P)],
                                          start=(c == 0), stop=(c == NT - 1))
                    i.then_inc(pv_done, 1)

                def batch(b, first, last):
                    for r in range(NT):
                        scores(b, r)
                        if not last and r == 6:
                            turn_x(b + 1, 0, first)
                        if r >= 1:
                            turn_p(b, r - 1)
                        elif not first:
                            turn_p(b - 1, NT - 1)
                        if r >= 2:
                            attend(b, r - 2)
                        elif not first:
                            attend(b - 1, NT - 2 + r)
                        if not first and r in (4, 5):
                            turn_next(b - 1, r - 4, 2 * b + 2)
                        if not last and r == 6:
                            turn_x(b + 1, 1)

                for h in range(2):
                    turn_x(0, h)
                batch(0, True, False)
                with pe.Fori(1, LAST) as b:
                    batch(b, False, False)
                batch(LAST, False, True)
                turn_p(LAST, NT - 1)
                attend(LAST, NT - 2)
                attend(LAST, NT - 1)
                for h in range(2):
                    turn_next(LAST, h, 2 * B)

            @block.scalar
            def _(act):
                def copy_xt(b, h):
                    act.wait_ge(xt_ps, 2 * b + h + 1)
                    wait(act, t_ready, (b - 1) * NT * K)
                    wait(act, made, (b - 1) * NT)
                    nc.scalar.copy(XT[:, bass.ds((b % 2) * N + h * HALF, HALF)], M[:, :]).then_inc(xt_ready, 1)

                def copy_next(b, h):
                    act.wait_ge(nt_ps, 2 * b + h + 1)
                    nc.scalar.copy(XTN[:, bass.ds(b * N + h * HALF, HALF)], M[:, :]).then_inc(nt_ready, 1)

                def relu(b, r):
                    g = b * NT + r
                    wait(act, y_ready, g - 1)
                    if K > 1:
                        act.wait_ge(t_ready, g * K + 1)
                        nc.scalar.copy(ACC[:, r % 2, :], T[0][:, :]).then_inc(t_read, 1)
                        act.wait_ge(acc_ready, g * (K - 1) + K - 1)
                        nc.scalar.activation(R4[:, r % 2, :], ACC[:, r % 2, :], ACT.Relu, scale=4.0).then_inc(r4_ready, 1)
                    else:
                        act.wait_ge(t_ready, g + 1)
                        nc.scalar.activation(R4[:, r % 2, :], T[r % 2][:, :], ACT.Relu, scale=4.0).then_inc(r4_ready, 1)

                def prob(b, r):
                    g = b * NT + r
                    act.wait_ge(shift_ready, g + 1)
                    wait(act, tp_ps[1], g - 1)
                    wait(act, x_added, g - 1)
                    nc.scalar.activation(PR[:, r % 2, :], Y[:, r % 2, :], ACT.Exp, bias=NMX[:, r % 2:r % 2 + 1], scale=SLOPE,
                                         accum_out=Z[:, r % 2:r % 2 + 1]).then_inc(pr_ready, 1)

                def copy_p(b, r):
                    g = b * NT + r
                    act.wait_ge(tp_ps[0], g + 1)
                    wait(act, pv_done, g - 1)
                    nc.scalar.copy(PT[:, r % 2, 0:HALF], TP[0][:, :]).then_inc(tp_read[0], 1)

                def batch(b, first, last):
                    for r in range(NT):
                        relu(b, r)
                        if not last and r == 6:
                            copy_xt(b + 1, 0)
                        if r >= 1:
                            copy_p(b, r - 1)
                        elif not first:
                            copy_p(b - 1, NT - 1)
                        prob(b, r)
                        if not first and r in (4, 5):
                            copy_next(b - 1, r - 4)
                        if not last and r == 6:
                            copy_xt(b + 1, 1)

                for h in range(2):
                    copy_xt(0, h)
                batch(0, True, False)
                with act.Fori(1, LAST) as b:
                    batch(b, False, False)
                batch(LAST, False, True)
                copy_p(LAST, NT - 1)
                for h in range(2):
                    copy_next(LAST, h)

            @block.vector
            def _(dve):
                step = Count()

                def make(b, r):
                    g = b * NT + r
                    if r == 0:
                        dve.wait_ge(xt_ready, 2 * b + 2)
                    wait(dve, t_ready, (g - 1) * K)
                    for k in range(K):
                        nc.vector.tensor_scalar(AK[:, r % 2, k, :], XT[:, bass.ds((b % 2) * N + r * P, P)],
                                                pcol[:, at[f"L1_gnn_a{k}"]:at[f"L1_gnn_a{k}"] + 1], None, ALU.mult)
                    dve.wait_ge(loaded[r % 4], 16 * (b * (NT // 4) + r // 4 + 1))
                    for k in range(K):
                        i = nc.vector.tensor_scalar(NK[:, r % 2, k, :], ADJ[:, r % 4, :], float(k + 1), None, ALU.not_equal)
                    i.then_inc(made, 1)

                def shift(b, r):
                    g = b * NT + r
                    for k in range(1, K):
                        hold(dve, t_read, g * K + k)
                        dve.wait_ge(t_ready, g * K + k + 1)
                        nc.vector.tensor_tensor(ACC[:, r % 2, :], ACC[:, r % 2, :], T[k % 2][:, :], ALU.max).then_inc(t_read, 1)
                        hold(dve, t_read, g * K + k + 1)
                        dve.sem_inc(acc_ready, 1)
                    if reached(g, 2):
                        hold(dve, pr_ready, g - 1)
                    hold(dve, r4_ready, g + 1)
                    i = nc.vector.tensor_tensor_reduce(Y[:, r % 2, :], T[r % 2][:, :] if K == 1 else ACC[:, r % 2, :],
                                                       R4[:, r % 2, :], 1.0, -3.0e38, ALU.add, ALU.max, MX[:, r % 2:r % 2 + 1])
                    i.then_inc(y_ready, 1)
                    hold(dve, y_ready, g + 1)
                    if K == 1:
                        dve.sem_inc(t_read, 1)
                    nc.vector.tensor_scalar(NMX[:, r % 2:r % 2 + 1], MX[:, r % 2:r % 2 + 1], -SLOPE, None, ALU.mult
                                            ).then_inc(shift_ready, 1)

                def copy_p(b, r):
                    g = b * NT + r
                    dve.wait_ge(tp_ps[1], g + 1)
                    wait(dve, pv_done, g - 1)
                    nc.vector.tensor_copy(PT[:, r % 2, HALF:N], TP[1][:, :]).then_inc(tp_read[1], 1)

                def add(b, r):
                    g = b * NT + r
                    nc.vector.reciprocal(RZ[:, r % 2:r % 2 + 1], Z[:, r % 2:r % 2 + 1]).then_inc(dstep, 1)
                    dve.wait_ge(dstep, step.next())
                    dve.wait_ge(pv_done, g + 1)
                    xb = X[:, bass.ds(b * N + r * P, P)]
                    nc.vector.scalar_tensor_tensor(out=xb, in0=O[:, 0:P], scalar=RZ[:, r % 2:r % 2 + 1], in1=xb,
                                                   op0=ALU.mult, op1=ALU.add).then_inc(x_added, 1)

                def norm(b):
                    if reached(b, 1):
                        dve.wait_ge(xt_ps, 2 * b)
                        dve.wait_ge(xb_ready, b)
                    ln_apply(dve, b, MV, RS[:, 1, :], XN, 0, rs_ready, xn_ready)

                def join(b, k):
                    hold(dve, gathered[k], 16 * NT * (b + 1))
                    for t in range(NT):
                        xb = X[:, bass.ds((b * NT + t) * P, P)]
                        i = nc.vector.scalar_tensor_tensor(out=xb, in0=YG[:, k * NT + t, :],
                                                           scalar=SHARE[:, bass.ds((b * 2 + k) * NT + t, 1)], in1=xb,
                                                           op0=ALU.mult, op1=ALU.add)
                    i.then_inc(joined, 1)
                    hold(dve, joined, 2 * b + k + 1)

                def stats_next(b):
                    hold(dve, x_added, (b + 1) * NT)
                    ln_stats(dve, b, ST, MVN, dstep, step, next_mv_ready)

                def norm_next(b):
                    ln_apply(dve, b, MVN, RSN[:, 1, :], XNN, 0, next_rs_ready, next_xn_ready)

                def batch(b, first, last):
                    for r in range(NT):
                        if not (last and r == NT - 1):
                            make(b + (r + 1) // NT, (r + 1) % NT)
                        shift(b, r)
                        if r >= 1:
                            copy_p(b, r - 1)
                        elif not first:
                            copy_p(b - 1, NT - 1)
                        if r >= 2:
                            add(b, r - 2)
                        elif not first:
                            add(b - 1, NT - 2 + r)
                        if not first:
                            if r == 1:
                                stats_next(b - 1)
                            if r == 3:
                                norm_next(b - 1)
                        if not last:
                            for k in range(2):
                                if r == ((2, 3) if first else (0, 2))[k]:
                                    join(b + 1, k)
                            if r == 4:
                                ln_stats(dve, b + 1, ST, MV, dstep, step, mv_ready)
                            if r == 5:
                                norm(b + 1)

                for k in range(2):
                    join(0, k)
                ln_stats(dve, 0, ST, MV, dstep, step, mv_ready)
                norm(0)
                make(0, 0)
                batch(0, True, False)
                with dve.Fori(1, LAST) as b:
                    step.loop(b - 1, 10)
                    batch(b, False, False)
                step.end(LAST - 1)
                batch(LAST, False, True)
                copy_p(LAST, NT - 1)
                add(LAST, NT - 2)
                add(LAST, NT - 1)
                stats_next(LAST)
                dve.wait_ge(nt_ps, 2 * LAST)
                norm_next(LAST)

        XTN = sb("XTN", [P, B * N])
        FT = sb("FT", [P, N])
        several = nc.values_load(flag[:, :], min_val=0, max_val=1)
        with nc.If(several > 0):
            with ExitStack() as ctx:
                edge_attention(4, ctx, "g_")
        with nc.Else():
            with ExitStack() as ctx:
                edge_attention(1, ctx, "f_")

        with ExitStack() as last_layer:
            def tile(name, shape, dt=F32, ctx=last_layer):
                return sb(name, shape, dt, ctx)

            BIAS = tile("BIAS", [P, N])
            WBC = tile("WBC", [P, E, N])

            with ExitStack() as ctx:
                LG, EX, W8, WR = (tile("d" + n, [P, NT, E], F32, ctx) for n in ("LG", "EX", "W8", "WR"))
                mx, sm, rs = (tile("d" + n, [P, NT], F32, ctx) for n in ("mx", "sm", "rs"))
                W3 = tile("dW3", [P, NT, 3 * E], BF16, ctx)
                WT3 = tile("dWT3", [3 * E, N], BF16, ctx)
                WT8 = tile("dWT8", [E, N], F32, ctx)
                M = [ctx.enter_context(nc.psum_tensor(f"dM{i}", [P, HALF], F32)) for i in range(2)]
                BC = [ctx.enter_context(nc.psum_tensor(f"BC{i}", [P, HALF], F32)) for i in range(2)]
                W3T = M[0][:, :].bitcast(BF16)
                (dstep, lg_ps, lg_ready, ex_ready, w_ready, w3t_ps,
                 wt3_ready, bc_ps, bc_act, bc_dve) = (sem("d_" + n) for n in (
                     "dve_step", "lg_ps", "lg_ready",
                     "ex_ready", "w_ready", "w3t_ps", "wt3_ready", "bc_ps", "bc_act", "bc_dve"))
                wt8_ps = [sem(f"d_wt8_ps{h}") for h in range(2)]
                wt8_ready, bias_ps, bias_ready = sem("d_wt8_ready"), sem("d_bias_ps"), sem("d_bias_ready")
                block = ctx.enter_context(nc.Block())

                @block.tensor
                def _(pe):
                    for t in range(NT):
                        i = pe.matmul(M[0][:, t * E:(t + 1) * E], FT[:, t * P:(t + 1) * P], Wr1[:, :], start=True, stop=True)
                    i.then_inc(lg_ps, 1)
                    pe.wait_ge(w_ready, 1)
                    for t in range(NT):
                        i = pe.transpose(W3T[0:3 * E, t * P:(t + 1) * P], W3[:, t, :], identb[:, :])
                    i.then_inc(w3t_ps, 1)
                    pe.wait_ge(wt3_ready, 1)
                    for h in range(2):
                        for t in range(4):
                            i = pe.transpose(M[h][0:E, t * P:(t + 1) * P], W8[:, 4 * h + t, :], ident[:, :])
                        i.then_inc(wt8_ps[h], 1)
                    for h in range(2):
                        pe.wait_ge(wt8_ready, h + 1)
                        for t in range(4):
                            i = pe.matmul(M[h][:, t * P:(t + 1) * P], WT8[:, (4 * h + t) * P:(4 * h + t + 1) * P], bo1[:, :],
                                          start=True, stop=True)
                        i.then_inc(bias_ps, 1)
                    for k in range(2 * E):
                        wait(pe, (bc_act, bc_dve)[k % 2], k // 2)
                        pe.matmul(BC[k % 2][:, :], pick[:, k // 2 * P:(k // 2 + 1) * P],
                                  WT3[:, k % 2 * HALF:(k % 2 + 1) * HALF], start=True, stop=True).then_inc(bc_ps, 1)

                @block.scalar
                def _(act):
                    act.wait_ge(lg_ready, 1)
                    nc.scalar.activation(EX[:, :, :], LG[:, :, :], ACT.Exp).then_inc(ex_ready, 1)
                    for h in range(2):
                        act.wait_ge(wt8_ps[h], 1)
                        nc.scalar.copy(WT8[:, h * HALF:(h + 1) * HALF], M[h][0:E, :]).then_inc(wt8_ready, 1)
                    for h in range(2):
                        act.wait_ge(bias_ps, h + 1)
                        nc.scalar.copy(BIAS[:, h * HALF:(h + 1) * HALF], M[h][:, :]).then_inc(bias_ready, 1)
                    for e in range(E):
                        act.wait_ge(bc_ps, 2 * e + 1)
                        nc.scalar.copy(WBC[:, e, 0:HALF], BC[0][:, :]).then_inc(bc_act, 1)

                @block.vector
                def _(dve):
                    step = Count()
                    v = nc.vector

                    def op(f, *a, **k):
                        f(*a, **k).then_inc(dstep, 1)
                        dve.wait_ge(dstep, step.next())

                    def wide(t):
                        return t[:, :].unsqueeze(2).to_broadcast([P, NT, E])

                    dve.wait_ge(lg_ps, 1)
                    op(v.scalar_tensor_tensor, out=LG[:, :, :], in0=M[0][:, 0:NT * E].rearrange("p (t e) -> p t e", e=E),
                       scalar=1.0 / B, in1=br1[:, :].unsqueeze(1).to_broadcast([P, NT, E]), op0=ALU.mult, op1=ALU.add)
                    op(v.tensor_reduce, mx[:, :], LG[:, :, :], AX_X, ALU.max)
                    v.tensor_tensor(LG[:, :, :], LG[:, :, :], wide(mx), ALU.subtract).then_inc(lg_ready, 1)
                    dve.wait_ge(ex_ready, 1)
                    op(v.tensor_reduce, sm[:, :], EX[:, :, :], AX_X, ALU.add)
                    op(v.reciprocal, rs[:, :], sm[:, :])
                    op(v.tensor_tensor, W8[:, :, :], EX[:, :, :], wide(rs), ALU.mult)
                    op(v.tensor_copy, W3[:, :, 0:E], W8[:, :, :])
                    op(v.tensor_tensor, WR[:, :, :], W8[:, :, :], W3[:, :, 0:E], ALU.subtract)
                    op(v.tensor_copy, W3[:, :, E:2 * E], WR[:, :, :])
                    v.tensor_tensor(W3[:, :, 2 * E:3 * E], WR[:, :, :], W3[:, :, E:2 * E], ALU.subtract).then_inc(w_ready, 1)
                    dve.wait_ge(w3t_ps, 1)
                    v.tensor_copy(WT3[:, :], W3T[0:3 * E, 0:N]).then_inc(wt3_ready, 1)
                    for e in range(E):
                        dve.wait_ge(bc_ps, 2 * e + 2)
                        v.tensor_copy(WBC[:, e, HALF:N], BC[1][:, :]).then_inc(bc_dve, 1)

            with ExitStack() as ctx:
                H1, H2, GW, YS = (tile(n, [P, 2, HALF], F32, ctx) for n in ("H1", "H2", "dGW", "dYS"))
                U1, U2, Y, M = ([ctx.enter_context(nc.psum_tensor(f"e{n}{i}", [P, HALF], F32)) for i in range(2)]
                                for n in ("U1", "U2", "Y", "M"))
                u1_ready, h1_ready, u2_ready, h2_ready, gw_ready, y_mm, bias_added = (sem("e_" + n) for n in (
                    "u1_ready", "h1_ready", "u2_ready", "h2_ready", "gw_ready", "y_mm", "bias_added"))
                ys_ready, yt_ps, x_added, stored = ([sem(f"e_{n}{h}") for h in range(2)] for n in (
                    "ys_ready", "yt_ps", "x_added", "stored"))
                S = 2 * E
                AGO = 3
                block = ctx.enter_context(nc.Block())

                @block.sync
                def _(sp):
                    with sp.Fori(0, B) as b:
                        for q in range(2):
                            sp.wait_ge(x_added[q], b + 1)
                            sp.dma_start(out[bass.ds(b, 1), q * HALF:(q + 1) * HALF, :].rearrange("o (t p) d -> p (o t) d", p=P),
                                         X[:, bass.ds(b * N + q * HALF, HALF)].rearrange("p (t d) -> p t d", d=P)
                                         ).then_inc(stored[q], 16)
                    for q in range(2):
                        sp.wait_ge(stored[q], 16 * B)

                @block.gpsimd
                def _(pool):
                    with pool.Fori(0, B) as b:
                        xb = X[:, bass.ds(b * N, N)]
                        nc.gpsimd.tensor_tensor(xb, xb, BIAS[:, :], ALU.add).then_inc(bias_added, 1)

                @block.tensor
                def _(pe):
                    def first(b, s):
                        wait(pe, h1_ready, b * S + s - 1)
                        pe.matmul(U1[s % 2][:, :], V1[:, s % E * P:(s % E + 1) * P], XTN[:, bass.ds(b * N + s // E * HALF, HALF)],
                                  start=True, stop=True).then_inc(u1_ready, 1)

                    def second(b, s):
                        pe.wait_ge(h1_ready, b * S + s + 1)
                        wait(pe, h2_ready, b * S + s - 1)
                        pe.matmul(U2[s % 2][:, :], V2[:, s % E * P:(s % E + 1) * P], H1[:, s % 2, :],
                                  start=True, stop=True).then_inc(u2_ready, 1)

                    def third(b, s):
                        q, e = s // E, s % E
                        if e == 0:
                            wait(pe, ys_ready[q], b)
                        pe.wait_ge(gw_ready, b * S + s + 1)
                        pe.matmul(Y[q][:, :], Vo[:, e * P:(e + 1) * P], GW[:, s % 2, :], start=(e == 0), stop=(e == E - 1)
                                  ).then_inc(y_mm, 1)

                    def turn_y(b, q):
                        pe.wait_ge(ys_ready[q], b + 1)
                        for t in range(4):
                            i = pe.transpose(M[q][:, t * P:(t + 1) * P], YS[:, q, t * P:(t + 1) * P], ident[:, :])
                        i.then_inc(yt_ps[q], 1)

                    def batch(b, start):
                        for s in range(S):
                            first(b, s)
                            if s >= AGO:
                                third(b, s - AGO)
                            elif not start:
                                third(b - 1, S + s - AGO)
                            if s >= 1:
                                second(b, s - 1)
                            elif not start:
                                second(b - 1, S - 1)
                            if s == 5 and not start:
                                turn_y(b - 1, 1)
                            if s == 13:
                                turn_y(b, 0)

                    batch(0, True)
                    with pe.Fori(1, B) as b:
                        batch(b, False)
                    second(B - 1, S - 1)
                    for s in range(S - AGO, S):
                        third(B - 1, s)
                    turn_y(B - 1, 1)

                @block.scalar
                def _(act):
                    def relu1(b, s):
                        act.wait_ge(u1_ready, b * S + s + 1)
                        wait(act, u2_ready, b * S + s - 1)
                        e = s % E
                        nc.scalar.activation(H1[:, s % 2, :], U1[s % 2][:, :], ACT.Relu, bias=bn[:, E + e:E + e + 1],
                                             scale=bn[:, e:e + 1]).then_inc(h1_ready, 1)

                    def relu2(b, s):
                        act.wait_ge(u2_ready, b * S + s + 1)
                        wait(act, gw_ready, b * S + s - 1)
                        e = s % E
                        nc.scalar.activation(H2[:, s % 2, :], U2[s % 2][:, :], ACT.Relu, bias=bn[:, 3 * E + e:3 * E + e + 1],
                                             scale=bn[:, 2 * E + e:2 * E + e + 1]).then_inc(h2_ready, 1)

                    def copy_y(b, q):
                        act.wait_ge(y_mm, b * S + (q + 1) * E)
                        nc.scalar.copy(YS[:, q, :], Y[q][:, :]).then_inc(ys_ready[q], 1)

                    def batch(b, start):
                        for s in range(S):
                            relu1(b, s)
                            if s >= 1:
                                relu2(b, s - 1)
                            elif not start:
                                relu2(b - 1, S - 1)
                            if s == 3 and not start:
                                copy_y(b - 1, 1)
                            if s == 11:
                                copy_y(b, 0)

                    batch(0, True)
                    with act.Fori(1, B) as b:
                        batch(b, False)
                    relu2(B - 1, S - 1)
                    copy_y(B - 1, 1)

                @block.vector
                def _(dve):
                    def weight(b, s):
                        q, e = s // E, s % E
                        dve.wait_ge(h2_ready, b * S + s + 1)
                        wait(dve, y_mm, b * S + s - 1)
                        nc.vector.tensor_tensor(GW[:, s % 2, :], H2[:, s % 2, :], WBC[:, e, q * HALF:(q + 1) * HALF],
                                                ALU.mult).then_inc(gw_ready, 1)

                    def add(b, q):
                        hold(dve, bias_added, b + 1)
                        dve.wait_ge(yt_ps[q], b + 1)
                        xb = X[:, bass.ds(b * N + q * HALF, HALF)]
                        nc.vector.tensor_tensor(xb, M[q][:, :], xb, ALU.add).then_inc(x_added[q], 1)

                    def batch(b, start):
                        for s in range(S):
                            weight(b, s)
                            if s == 5 and not start:
                                add(b - 1, 1)
                            if s == 13:
                                add(b, 0)

                    batch(0, True)
                    with dve.Fori(1, B) as b:
                        batch(b, False)
                    add(B - 1, 1)



_PARAMS = (["L0_gnn_W", "L0_gnn_a"] + [f"L0_ffn_{n}" for n in ("gamma", "beta", "Wr", "br", "W1", "b1", "W2", "b2")]
           + [f"L1_gnn_a{k}" for k in range(4)]
           + [f"L1_ffn_{n}" for n in ("Wr", "br", "W1", "b1", "g1", "be1", "m1", "v1", "W2", "b2", "g2", "be2", "m2", "v2",
                                      "Wo", "bo")])


def kernel(**inputs):
    import numpy as np
    import concourse.bacc as bacc
    from concourse.bass_utils import run_bass_kernel_spmd

    nc = bacc.Bacc("TRN2", target_bir_lowering=False, num_devices=1)
    arrays, given = {}, {}
    for name in ["x", "adj"] + _PARAMS:
        a = np.ascontiguousarray(inputs[name])
        arrays[f"in_{name}"] = a
        given[name] = nc.dram_tensor(f"in_{name}", a.shape, mybir.dt.from_np(a.dtype), kind="ExternalInput").ap()
    x, adj = given.pop("x"), given.pop("adj")
    out = nc.dram_tensor("out_x", x.shape, F32, kind="ExternalOutput").ap()
    program(nc, x, adj, given, out)
    return run_bass_kernel_spmd(nc, [arrays], core_ids=[0]).results[0]["out_x"]
```
